# Optimizing a Trainium2 kernel written in Bass

```python
import numpy as np
import jax
import jax.numpy as jnp

def _softmax(x, axis=-1):
    return jax.nn.softmax(x, axis=axis)

def _gelu(x):
    return jax.nn.gelu(x, approximate=True)

def _silu(x):
    return jax.nn.silu(x)

def _sigmoid(x):
    return jax.nn.sigmoid(x)

def _layernorm(x, axis=-1, eps=1e-05):
    m = jnp.mean(x, axis=axis, keepdims=True)
    v = jnp.var(x, axis=axis, keepdims=True)
    return (x - m) / jnp.sqrt(v + eps)

def _scatter_add(tgt, idx, src, axis=0):
    return tgt.at[idx].add(src)

def _segment_sum(src, seg, n):
    return jax.ops.segment_sum(src, seg, n)
kernel_name = 'mk_decoder_postln_d2_seqx_r4_b6ddf1'

def setup_inputs(seed: int=0):
    np.random.seed(seed)
    _w = jnp.asarray

    def _rec_inputs():
        import jax
        import jax.numpy as jnp
        _rk = jax.random.key(seed)
        x = -0.0002928 + 1 * jax.random.normal(jax.random.fold_in(_rk, 1), (16, 128, 512), jnp.float32)
        _lenS = 128 - jax.random.randint(jax.random.fold_in(_rk, 7), (16,), 0, max(1, 128 // 4) + 1, jnp.int32)
        _lenS2 = 128 - jax.random.randint(jax.random.fold_in(_rk, 8), (16,), 0, max(1, 128 // 4) + 1, jnp.int32)
        _ctx_2048P = jax.random.normal(jax.random.fold_in(_rk, 11), (16, 16, 512), jnp.float32)
        _ctx_2048c = jax.random.dirichlet(jax.random.fold_in(_rk, 511), 0.3 * jnp.ones((16,), jnp.float32), (16, 128))
        _ctx_2048t = jnp.einsum('bsk,bkd->bsd', _ctx_2048c, _ctx_2048P)
        _ctx_2048t = _ctx_2048t * jax.lax.rsqrt(jnp.mean(jnp.square(_ctx_2048t)) + 1e-12) * 0.953939
        ctx_2048 = -1.39393e-06 + 0.999914 * (_ctx_2048t + 0.3 * jax.random.normal(jax.random.fold_in(_rk, 611), (16, 128, 512), jnp.float32))
        return (x, ctx_2048)
    x, ctx_2048 = _rec_inputs()

    def _L0_attn_setup():
        import jax, jax.numpy as jnp
        import numpy as np
        B, S, DM = (2, 512, 512)
        H, KVH, HD = (16, 4, 128)
        REP = H // KVH
        ROPE_BASE = 10000.0
        EPS = 1e-06

        def _rope_tables(seq_len, dim):
            inv_freq = 1.0 / ROPE_BASE ** (jnp.arange(0, dim, 2, dtype=jnp.float32) / dim)
            t = jnp.arange(seq_len, dtype=jnp.float32)
            freqs = jnp.outer(t, inv_freq)
            emb = jnp.concatenate([freqs, freqs], -1)
            return (jnp.cos(emb), jnp.sin(emb))

        def _rotate_half(x):
            d = x.shape[-1] // 2
            return jnp.concatenate([-x[..., d:], x[..., :d]], axis=-1)
        key = jax.random.key(seed)
        k0, k1, k2, k3, k4 = jax.random.split(key, 5)
        w = lambda k, o, i: jax.random.normal(k, (o, i), jnp.float32) * (1.0 / np.sqrt(i))
        return {'x': jax.random.normal(k0, (B, S, DM), jnp.float32), 'Wq': w(k1, H * HD, DM), 'Wk': w(k2, KVH * HD, DM), 'Wv': w(k3, KVH * HD, DM), 'Wo': w(k4, DM, H * HD)}
    _L0_attn_all = _L0_attn_setup()
    _L0_attn_in = {k: v for k, v in _L0_attn_all.items() if k in ('Wq', 'Wk', 'Wv', 'Wo')}
    del _L0_attn_all

    def _L0_xattn_setup():
        import jax, jax.numpy as jnp
        import numpy as np
        B, S, E, NH = (2, 256, 512, 16)
        DH = E // NH
        EPS = 1e-06

        def _mlstm_forward(q, k, v, Wi, bi, Wf, bf, ln_scale):
            b, s, e = q.shape
            nh = Wi.shape[1]
            dh = e // nh
            x = jnp.concatenate([q, k, v], axis=-1)
            ig = (x @ Wi + bi).transpose(0, 2, 1)[..., None]
            fg = (x @ Wf + bf).transpose(0, 2, 1)[..., None]
            split = lambda t: t.reshape(b, s, nh, dh).transpose(0, 2, 1, 3)
            qh, kh, vh = (split(q), split(k), split(v))
            log_f = jax.nn.log_sigmoid(fg)
            log_f_cum = jnp.concatenate([jnp.zeros((b, nh, 1, 1), q.dtype), jnp.cumsum(log_f, axis=2)], axis=2)
            fg_mat = log_f_cum - jnp.transpose(log_f_cum, (0, 1, 3, 2))
            ltr = jnp.tril(jnp.ones((s, s), dtype=bool))
            log_fg = jnp.where(ltr, fg_mat[:, :, 1:, 1:], -jnp.inf)
            log_D = log_fg + jnp.transpose(ig, (0, 1, 3, 2))
            max_log_D = jnp.max(log_D, axis=-1, keepdims=True)
            D = jnp.exp(log_D - max_log_D)
            qk = jnp.einsum('bhsd,bhtd->bhst', qh, kh) / jnp.sqrt(jnp.asarray(dh, q.dtype))
            C = qk * D
            normalizer = jnp.maximum(jnp.abs(C.sum(-1, keepdims=True)), jnp.exp(-max_log_D))
            Cn = C / (normalizer + EPS)
            h = jnp.einsum('bhst,bhtd->bhsd', Cn, vh)
            mu = h.mean(-1, keepdims=True)
            var = ((h - mu) ** 2).mean(-1, keepdims=True)
            hn = (h - mu) * jax.lax.rsqrt(var + EPS)
            hn = hn * ln_scale.reshape(1, nh, 1, dh)
            return hn.transpose(0, 2, 1, 3).reshape(b, s, e)
        key = jax.random.key(seed)
        ks = jax.random.split(key, 6)
        q = jax.random.normal(ks[0], (B, S, E), dtype=jnp.float32)
        k = jax.random.normal(ks[1], (B, S, E), dtype=jnp.float32)
        v = jax.random.normal(ks[2], (B, S, E), dtype=jnp.float32)
        Wi = jax.random.normal(ks[3], (3 * E, NH), dtype=jnp.float32) * 0.02
        bi = jax.random.normal(ks[4], (NH,), dtype=jnp.float32) * 0.1
        Wf = jax.random.normal(ks[5], (3 * E, NH), dtype=jnp.float32) * 0.02
        bf = jnp.linspace(3.0, 6.0, NH, dtype=jnp.float32)
        ln_scale = jnp.ones((E,), dtype=jnp.float32)
        return {'q': q, 'k': k, 'v': v, 'Wi': Wi, 'bi': bi, 'Wf': Wf, 'bf': bf, 'ln_scale': ln_scale}
    _L0_xattn_all = _L0_xattn_setup()
    _L0_xattn_in = {k: v for k, v in _L0_xattn_all.items() if k in ('Wi', 'bi', 'Wf', 'bf', 'ln_scale')}
    del _L0_xattn_all

    def _L0_ffn_setup():
        import jax, jax.numpy as jnp
        import numpy as np
        TOP_K = 2
        key = jax.random.key(seed)
        ks = jax.random.split(key, 5)
        B, S, D, INTER, E = (4, 512, 512, 512, 8)
        x = jax.random.normal(ks[0], (B, S, D), dtype=jnp.float32)
        w1 = jax.random.normal(ks[1], (INTER, D), dtype=jnp.float32) * (1.0 / np.sqrt(D))
        w3 = jax.random.normal(ks[2], (INTER, INTER), dtype=jnp.float32) * (1.0 / np.sqrt(INTER))
        w2 = jax.random.normal(ks[3], (D, INTER), dtype=jnp.float32) * (1.0 / np.sqrt(INTER))
        wr = jax.random.normal(ks[4], (E, D), dtype=jnp.float32) * (1.0 / np.sqrt(D))
        return {'x': x, 'w1': w1, 'w3': w3, 'w2': w2, 'wr': wr}
    _L0_ffn_all = _L0_ffn_setup()
    _L0_ffn_in = {k: v for k, v in _L0_ffn_all.items() if k in ('w1', 'w3', 'w2', 'wr')}
    del _L0_ffn_all

    def _L1_attn_setup():
        import math
        import jax, jax.numpy as jnp
        import numpy as np
        EMBED_DIM = 512
        NUM_HEADS = 16
        HEAD_DIM = EMBED_DIM // NUM_HEADS
        CHUNK = 128
        RMS_EPS = 1e-05

        def _build_slopes(n):

            def pow2(n):
                start = 2.0 ** (-2.0 ** (-(math.log2(n) - 3)))
                return [start * start ** i for i in range(n)]
            if math.log2(n).is_integer():
                s = pow2(n)
            else:
                closest = 2 ** math.floor(math.log2(n))
                s = pow2(closest) + pow2(2 * closest)[0::2][:n - closest]
            return jnp.asarray(s, dtype=jnp.float32)

        def _rotary(x_BTHD, offset=0):
            T, D = (x_BTHD.shape[1], x_BTHD.shape[-1])
            freq = (1.0 / 1024.0) ** jnp.linspace(0.0, 1.0, D // 4, dtype=jnp.float32)
            freq = jnp.concatenate([freq, jnp.zeros(D // 4, dtype=jnp.float32)])
            t = jnp.arange(offset, offset + T, dtype=jnp.float32)
            theta = t[:, None] * freq[None, :]
            cos = jnp.cos(theta)[None, :, None, :]
            sin = jnp.sin(theta)[None, :, None, :]
            x1, x2 = jnp.split(x_BTHD.astype(jnp.float32), 2, axis=-1)
            y1 = x1 * cos + x2 * sin
            y2 = -x1 * sin + x2 * cos
            return jnp.concatenate([y1, y2], axis=-1).astype(x_BTHD.dtype)

        def _lightning_attn(q, k, v, slopes):
            B, H, T, D = q.shape
            C = CHUNK
            NC = T // C
            r = jnp.exp(-slopes)
            i = jnp.arange(C, dtype=jnp.float32)
            q_decay = r[:, None] ** (i[None, :] + 1.0)
            k_decay = r[:, None] ** (C - 1.0 - i[None, :])
            diff = i[:, None] - i[None, :]
            mask = diff >= 0
            dmask = jnp.where(mask[None], r[:, None, None] ** jnp.where(mask, diff, 0.0)[None], 0.0)
            r_C = r ** float(C)

            def reshape_chunks(x):
                return x.reshape(B, H, NC, C, D).transpose(2, 0, 1, 3, 4)
            qc, kc, vc = (reshape_chunks(q), reshape_chunks(k), reshape_chunks(v))

            def step(kv, qkv):
                qi, ki, vi = qkv
                inter = jnp.einsum('bhcd,bhde->bhce', qi * q_decay[None, :, :, None], kv)
                scores = jnp.einsum('bhcd,bhsd->bhcs', qi, ki) * dmask[None]
                intra = jnp.einsum('bhcs,bhse->bhce', scores, vi)
                kv_new = r_C[None, :, None, None] * kv + jnp.einsum('bhcd,bhce->bhde', ki * k_decay[None, :, :, None], vi)
                return (kv_new, inter + intra)
            kv0 = jnp.zeros((B, H, D, D), dtype=q.dtype)
            _, out = jax.lax.scan(step, kv0, (qc, kc, vc))
            return out.transpose(1, 2, 0, 3, 4).reshape(B, H, T, D)

        def _rms_norm(x, w):
            var = jnp.mean(jnp.square(x), axis=-1, keepdims=True)
            return x * jax.lax.rsqrt(var + RMS_EPS) * w
        key = jax.random.key(seed)
        ks = jax.random.split(key, 6)
        sc = 1.0 / math.sqrt(EMBED_DIM)
        return {'x': jax.random.normal(ks[0], (4, 1024, EMBED_DIM), dtype=jnp.float32), 'Wq': jax.random.normal(ks[1], (EMBED_DIM, EMBED_DIM), dtype=jnp.float32) * sc, 'Wk': jax.random.normal(ks[2], (EMBED_DIM, EMBED_DIM), dtype=jnp.float32) * sc, 'Wv': jax.random.normal(ks[3], (EMBED_DIM, EMBED_DIM), dtype=jnp.float32) * sc, 'Wo': jax.random.normal(ks[4], (EMBED_DIM, EMBED_DIM), dtype=jnp.float32) * sc, 'rms_w': jnp.ones((EMBED_DIM,), dtype=jnp.float32)}
    _L1_attn_all = _L1_attn_setup()
    _L1_attn_in = {k: v for k, v in _L1_attn_all.items() if k in ('Wq', 'Wk', 'Wv', 'Wo', 'rms_w')}
    del _L1_attn_all

    def _L1_xattn_setup():
        import jax, jax.numpy as jnp
        import numpy as np
        N_HEAD = 8
        key = jax.random.key(seed)
        k1, k2, k3 = jax.random.split(key, 3)
        B, D, L = (4, 256, 512)
        q = jax.random.normal(k1, (B, D, L), dtype=jnp.float32)
        k = jax.random.normal(k2, (B, D, L), dtype=jnp.float32)
        v = jax.random.normal(k3, (B, D, L), dtype=jnp.float32)
        gamma = jnp.ones((), dtype=jnp.float32)
        return {'q': q, 'k': k, 'v': v, 'gamma': gamma}
    _L1_xattn_all = _L1_xattn_setup()
    _L1_xattn_in = {k: v for k, v in _L1_xattn_all.items() if k in ('gamma',)}
    del _L1_xattn_all

    def _L1_ffn_setup():
        import jax, jax.numpy as jnp
        import numpy as np
        DIM = 512
        INTER = 352
        E = 16
        TOPK = 4
        G = 4
        TOPK_G = 2
        N_SHARED = 2
        SHARED_INTER = N_SHARED * INTER
        ROUTE_SCALE = 1.0

        def _moe_forward(x, Wg, W1, W3, W2, Ws1, Ws3, Ws2):
            B, S, D = x.shape
            xt = x.reshape(-1, D)
            T = xt.shape[0]
            scores = jax.nn.softmax(xt @ Wg.T, axis=-1)
            sg = scores.reshape(T, G, E // G)
            group_scores = sg.max(axis=-1)
            gidx = jax.lax.top_k(group_scores, TOPK_G)[1]
            gmask = jax.nn.one_hot(gidx, G, dtype=jnp.float32).sum(axis=1) > 0
            masked = jnp.where(gmask[:, :, None], sg, -jnp.inf).reshape(T, E)
            topi = jax.lax.top_k(masked, TOPK)[1]
            weights = jnp.take_along_axis(scores, topi, axis=1) * ROUTE_SCALE
            combine = jnp.zeros((T, E), xt.dtype).at[jnp.arange(T)[:, None], topi].add(weights)
            h = jax.nn.silu(jnp.einsum('td,eid->eti', xt, W1)) * jnp.einsum('td,eid->eti', xt, W3)
            expert_out = jnp.einsum('eti,edi->etd', h, W2)
            y = jnp.einsum('etd,te->td', expert_out, combine)
            z = jax.nn.silu(xt @ Ws1.T) * (xt @ Ws3.T) @ Ws2.T
            return (y + z).reshape(B, S, D)
        key = jax.random.key(seed)
        ks = jax.random.split(key, 8)
        s = 0.02
        x = jax.random.normal(ks[0], (1, 512, DIM), dtype=jnp.float32)
        Wg = jax.random.normal(ks[1], (E, DIM), dtype=jnp.float32) * s
        W1 = jax.random.normal(ks[2], (E, INTER, DIM), dtype=jnp.float32) * s
        W3 = jax.random.normal(ks[3], (E, INTER, DIM), dtype=jnp.float32) * s
        W2 = jax.random.normal(ks[4], (E, DIM, INTER), dtype=jnp.float32) * s
        Ws1 = jax.random.normal(ks[5], (SHARED_INTER, DIM), dtype=jnp.float32) * s
        Ws3 = jax.random.normal(ks[6], (SHARED_INTER, DIM), dtype=jnp.float32) * s
        Ws2 = jax.random.normal(ks[7], (DIM, SHARED_INTER), dtype=jnp.float32) * s
        return {'x': x, 'Wg': Wg, 'W1': W1, 'W3': W3, 'W2': W2, 'Ws1': Ws1, 'Ws3': Ws3, 'Ws2': Ws2}
    _L1_ffn_all = _L1_ffn_setup()
    _L1_ffn_in = {k: v for k, v in _L1_ffn_all.items() if k in ('Wg', 'W1', 'W3', 'W2', 'Ws1', 'Ws3', 'Ws2')}
    del _L1_ffn_all
    return {'x': x, 'ctx_2048': ctx_2048, 'L0_attn_Wq': _L0_attn_in['Wq'], 'L0_attn_Wk': _L0_attn_in['Wk'], 'L0_attn_Wv': _L0_attn_in['Wv'], 'L0_attn_Wo': _L0_attn_in['Wo'], 'L0_xattn_Wi': _L0_xattn_in['Wi'], 'L0_xattn_bi': _L0_xattn_in['bi'], 'L0_xattn_Wf': _L0_xattn_in['Wf'], 'L0_xattn_bf': _L0_xattn_in['bf'], 'L0_xattn_ln_scale': _L0_xattn_in['ln_scale'], 'L0_ffn_w1': _L0_ffn_in['w1'], 'L0_ffn_w3': _L0_ffn_in['w3'], 'L0_ffn_w2': _L0_ffn_in['w2'], 'L0_ffn_wr': _L0_ffn_in['wr'], 'L1_attn_Wq': _L1_attn_in['Wq'], 'L1_attn_Wk': _L1_attn_in['Wk'], 'L1_attn_Wv': _L1_attn_in['Wv'], 'L1_attn_Wo': _L1_attn_in['Wo'], 'L1_attn_rms_w': _L1_attn_in['rms_w'], 'L1_xattn_gamma': _L1_xattn_in['gamma'], 'L1_ffn_Wg': _L1_ffn_in['Wg'], 'L1_ffn_W1': _L1_ffn_in['W1'], 'L1_ffn_W3': _L1_ffn_in['W3'], 'L1_ffn_W2': _L1_ffn_in['W2'], 'L1_ffn_Ws1': _L1_ffn_in['Ws1'], 'L1_ffn_Ws3': _L1_ffn_in['Ws3'], 'L1_ffn_Ws2': _L1_ffn_in['Ws2']}

def reference(x, ctx_2048, L0_attn_Wq, L0_attn_Wk, L0_attn_Wv, L0_attn_Wo, L0_xattn_Wi, L0_xattn_bi, L0_xattn_Wf, L0_xattn_bf, L0_xattn_ln_scale, L0_ffn_w1, L0_ffn_w3, L0_ffn_w2, L0_ffn_wr, L1_attn_Wq, L1_attn_Wk, L1_attn_Wv, L1_attn_Wo, L1_attn_rms_w, L1_xattn_gamma, L1_ffn_Wg, L1_ffn_W1, L1_ffn_W3, L1_ffn_W2, L1_ffn_Ws1, L1_ffn_Ws3, L1_ffn_Ws2):
    import jax
    import jax.numpy as jnp

    def _L0_attn_ref(x, Wq, Wk, Wv, Wo):
        import jax, jax.numpy as jnp
        import numpy as np
        B, S, DM = (2, 512, 512)
        H, KVH, HD = (16, 4, 128)
        REP = H // KVH
        ROPE_BASE = 10000.0
        EPS = 1e-06

        def _rope_tables(seq_len, dim):
            inv_freq = 1.0 / ROPE_BASE ** (jnp.arange(0, dim, 2, dtype=jnp.float32) / dim)
            t = jnp.arange(seq_len, dtype=jnp.float32)
            freqs = jnp.outer(t, inv_freq)
            emb = jnp.concatenate([freqs, freqs], -1)
            return (jnp.cos(emb), jnp.sin(emb))

        def _rotate_half(x):
            d = x.shape[-1] // 2
            return jnp.concatenate([-x[..., d:], x[..., :d]], axis=-1)
        bsz, seq_len, _ = x.shape
        q = (x @ Wq.T).reshape(bsz, seq_len, H, HD).transpose(0, 2, 1, 3)
        k = (x @ Wk.T).reshape(bsz, seq_len, KVH, HD).transpose(0, 2, 1, 3)
        v = (x @ Wv.T).reshape(bsz, seq_len, KVH, HD).transpose(0, 2, 1, 3)
        cos, sin = _rope_tables(seq_len, HD)
        cos, sin = (cos[None, None], sin[None, None])
        q = q * cos + _rotate_half(q) * sin
        k = k * cos + _rotate_half(k) * sin
        k = jnp.repeat(k, REP, axis=1)
        v = jnp.repeat(v, REP, axis=1)
        qf = jax.nn.elu(q) + 1.0
        kf = jax.nn.elu(k) + 1.0
        qf_t = qf.transpose(2, 0, 1, 3)
        kf_t = kf.transpose(2, 0, 1, 3)
        v_t = v.transpose(2, 0, 1, 3)

        def step(carry, inp):
            state, z = carry
            q_s, k_s, v_s = inp
            state = state + k_s[..., :, None] * v_s[..., None, :]
            z = z + k_s
            num = jnp.einsum('bhe,bhed->bhd', q_s, state)
            den = jnp.einsum('bhe,bhe->bh', q_s, z)[..., None] + EPS
            return ((state, z), num / den)
        init = (jnp.zeros((bsz, H, HD, HD), x.dtype), jnp.zeros((bsz, H, HD), x.dtype))
        _, out = jax.lax.scan(step, init, (qf_t, kf_t, v_t))
        out = out.transpose(1, 0, 2, 3).reshape(bsz, seq_len, H * HD)
        return out @ Wo.T

    def _L0_xattn_ref(q, k, v, Wi, bi, Wf, bf, ln_scale):
        import jax, jax.numpy as jnp
        import numpy as np
        B, S, E, NH = (2, 256, 512, 16)
        DH = E // NH
        EPS = 1e-06

        def _mlstm_forward(q, k, v, Wi, bi, Wf, bf, ln_scale):
            b, s, e = q.shape
            nh = Wi.shape[1]
            dh = e // nh
            x = jnp.concatenate([q, k, v], axis=-1)
            ig = (x @ Wi + bi).transpose(0, 2, 1)[..., None]
            fg = (x @ Wf + bf).transpose(0, 2, 1)[..., None]
            split = lambda t: t.reshape(b, s, nh, dh).transpose(0, 2, 1, 3)
            qh, kh, vh = (split(q), split(k), split(v))
            log_f = jax.nn.log_sigmoid(fg)
            log_f_cum = jnp.concatenate([jnp.zeros((b, nh, 1, 1), q.dtype), jnp.cumsum(log_f, axis=2)], axis=2)
            fg_mat = log_f_cum - jnp.transpose(log_f_cum, (0, 1, 3, 2))
            ltr = jnp.tril(jnp.ones((s, s), dtype=bool))
            log_fg = jnp.where(ltr, fg_mat[:, :, 1:, 1:], -jnp.inf)
            log_D = log_fg + jnp.transpose(ig, (0, 1, 3, 2))
            max_log_D = jnp.max(log_D, axis=-1, keepdims=True)
            D = jnp.exp(log_D - max_log_D)
            qk = jnp.einsum('bhsd,bhtd->bhst', qh, kh) / jnp.sqrt(jnp.asarray(dh, q.dtype))
            C = qk * D
            normalizer = jnp.maximum(jnp.abs(C.sum(-1, keepdims=True)), jnp.exp(-max_log_D))
            Cn = C / (normalizer + EPS)
            h = jnp.einsum('bhst,bhtd->bhsd', Cn, vh)
            mu = h.mean(-1, keepdims=True)
            var = ((h - mu) ** 2).mean(-1, keepdims=True)
            hn = (h - mu) * jax.lax.rsqrt(var + EPS)
            hn = hn * ln_scale.reshape(1, nh, 1, dh)
            return hn.transpose(0, 2, 1, 3).reshape(b, s, e)
        return _mlstm_forward(q, k, v, Wi, bi, Wf, bf, ln_scale)

    def _L0_ffn_ref(x, w1, w3, w2, wr):
        import jax, jax.numpy as jnp
        import numpy as np
        TOP_K = 2
        B, S, D = x.shape
        xr = x.reshape(-1, D)
        route_probs = jax.nn.softmax(xr @ wr.T, axis=-1)
        routes_k, indices_k = jax.lax.top_k(route_probs, TOP_K)
        gates = routes_k / jnp.sum(routes_k, axis=-1, keepdims=True)
        h = jax.nn.silu(xr @ w1.T)
        h = jax.nn.silu(h @ w3.T)
        h = h @ w2.T
        out = jnp.zeros_like(xr)
        for k in range(TOP_K):
            out = out.at[indices_k[:, k]].add(gates[:, k:k + 1] * h)
        return out.reshape(B, S, D)

    def _L1_attn_ref(x, Wq, Wk, Wv, Wo, rms_w):
        import math
        import jax, jax.numpy as jnp
        import numpy as np
        EMBED_DIM = 512
        NUM_HEADS = 16
        HEAD_DIM = EMBED_DIM // NUM_HEADS
        CHUNK = 128
        RMS_EPS = 1e-05

        def _build_slopes(n):

            def pow2(n):
                start = 2.0 ** (-2.0 ** (-(math.log2(n) - 3)))
                return [start * start ** i for i in range(n)]
            if math.log2(n).is_integer():
                s = pow2(n)
            else:
                closest = 2 ** math.floor(math.log2(n))
                s = pow2(closest) + pow2(2 * closest)[0::2][:n - closest]
            return jnp.asarray(s, dtype=jnp.float32)

        def _rotary(x_BTHD, offset=0):
            T, D = (x_BTHD.shape[1], x_BTHD.shape[-1])
            freq = (1.0 / 1024.0) ** jnp.linspace(0.0, 1.0, D // 4, dtype=jnp.float32)
            freq = jnp.concatenate([freq, jnp.zeros(D // 4, dtype=jnp.float32)])
            t = jnp.arange(offset, offset + T, dtype=jnp.float32)
            theta = t[:, None] * freq[None, :]
            cos = jnp.cos(theta)[None, :, None, :]
            sin = jnp.sin(theta)[None, :, None, :]
            x1, x2 = jnp.split(x_BTHD.astype(jnp.float32), 2, axis=-1)
            y1 = x1 * cos + x2 * sin
            y2 = -x1 * sin + x2 * cos
            return jnp.concatenate([y1, y2], axis=-1).astype(x_BTHD.dtype)

        def _lightning_attn(q, k, v, slopes):
            B, H, T, D = q.shape
            C = CHUNK
            NC = T // C
            r = jnp.exp(-slopes)
            i = jnp.arange(C, dtype=jnp.float32)
            q_decay = r[:, None] ** (i[None, :] + 1.0)
            k_decay = r[:, None] ** (C - 1.0 - i[None, :])
            diff = i[:, None] - i[None, :]
            mask = diff >= 0
            dmask = jnp.where(mask[None], r[:, None, None] ** jnp.where(mask, diff, 0.0)[None], 0.0)
            r_C = r ** float(C)

            def reshape_chunks(x):
                return x.reshape(B, H, NC, C, D).transpose(2, 0, 1, 3, 4)
            qc, kc, vc = (reshape_chunks(q), reshape_chunks(k), reshape_chunks(v))

            def step(kv, qkv):
                qi, ki, vi = qkv
                inter = jnp.einsum('bhcd,bhde->bhce', qi * q_decay[None, :, :, None], kv)
                scores = jnp.einsum('bhcd,bhsd->bhcs', qi, ki) * dmask[None]
                intra = jnp.einsum('bhcs,bhse->bhce', scores, vi)
                kv_new = r_C[None, :, None, None] * kv + jnp.einsum('bhcd,bhce->bhde', ki * k_decay[None, :, :, None], vi)
                return (kv_new, inter + intra)
            kv0 = jnp.zeros((B, H, D, D), dtype=q.dtype)
            _, out = jax.lax.scan(step, kv0, (qc, kc, vc))
            return out.transpose(1, 2, 0, 3, 4).reshape(B, H, T, D)

        def _rms_norm(x, w):
            var = jnp.mean(jnp.square(x), axis=-1, keepdims=True)
            return x * jax.lax.rsqrt(var + RMS_EPS) * w
        B, T, E = x.shape
        H, D = (NUM_HEADS, HEAD_DIM)
        q = (x @ Wq).reshape(B, T, H, D)
        k = (x @ Wk).reshape(B, T, H, D)
        v = (x @ Wv).reshape(B, T, H, D)
        q = _rotary(q)
        k = _rotary(k)
        q, k, v = (t.transpose(0, 2, 1, 3) for t in (q, k, v))
        slopes = _build_slopes(H)
        attn = _lightning_attn(q, k, v, slopes)
        attn = attn.transpose(0, 2, 1, 3).reshape(B, T, E)
        attn = _rms_norm(attn, rms_w)
        return attn @ Wo

    def _L1_xattn_ref(q, k, v, gamma):
        import jax, jax.numpy as jnp
        import numpy as np
        N_HEAD = 8
        B, Dq, Lq = q.shape
        Dv, Lk = (v.shape[-2], v.shape[-1])
        h = N_HEAD
        dq = Dq // h
        dv = Dv // h
        qh = q.reshape(B, h, dq, Lq)
        kh = k.reshape(B, h, dq, Lk)
        vh = v.reshape(B, h, dv, Lk)
        scale = 1.0 / jnp.sqrt(jnp.asarray(dq, dtype=q.dtype))
        qk = jnp.einsum('bhdq,bhdl->bhql', qh, kh) * scale
        sm = jax.nn.softmax(qk, axis=-1)
        ret = jnp.einsum('bhql,bhdl->bhdq', sm, vh)
        ret = ret.reshape(B, Dv, Lq)
        return gamma * ret

    def _L1_ffn_ref(x, Wg, W1, W3, W2, Ws1, Ws3, Ws2):
        import jax, jax.numpy as jnp
        import numpy as np
        DIM = 512
        INTER = 352
        E = 16
        TOPK = 4
        G = 4
        TOPK_G = 2
        N_SHARED = 2
        SHARED_INTER = N_SHARED * INTER
        ROUTE_SCALE = 1.0

        def _moe_forward(x, Wg, W1, W3, W2, Ws1, Ws3, Ws2):
            B, S, D = x.shape
            xt = x.reshape(-1, D)
            T = xt.shape[0]
            scores = jax.nn.softmax(xt @ Wg.T, axis=-1)
            sg = scores.reshape(T, G, E // G)
            group_scores = sg.max(axis=-1)
            gidx = jax.lax.top_k(group_scores, TOPK_G)[1]
            gmask = jax.nn.one_hot(gidx, G, dtype=jnp.float32).sum(axis=1) > 0
            masked = jnp.where(gmask[:, :, None], sg, -jnp.inf).reshape(T, E)
            topi = jax.lax.top_k(masked, TOPK)[1]
            weights = jnp.take_along_axis(scores, topi, axis=1) * ROUTE_SCALE
            combine = jnp.zeros((T, E), xt.dtype).at[jnp.arange(T)[:, None], topi].add(weights)
            h = jax.nn.silu(jnp.einsum('td,eid->eti', xt, W1)) * jnp.einsum('td,eid->eti', xt, W3)
            expert_out = jnp.einsum('eti,edi->etd', h, W2)
            y = jnp.einsum('etd,te->td', expert_out, combine)
            z = jax.nn.silu(xt @ Ws1.T) * (xt @ Ws3.T) @ Ws2.T
            return (y + z).reshape(B, S, D)
        return _moe_forward(x, Wg, W1, W3, W2, Ws1, Ws3, Ws2)
    x = _layernorm(x + _L0_attn_ref(x, L0_attn_Wq, L0_attn_Wk, L0_attn_Wv, L0_attn_Wo), axis=-1)
    x = _layernorm(x + _L0_xattn_ref(x, ctx_2048, ctx_2048, L0_xattn_Wi, L0_xattn_bi, L0_xattn_Wf, L0_xattn_bf, L0_xattn_ln_scale), axis=-1)
    x = _layernorm(x + _L0_ffn_ref(x, L0_ffn_w1, L0_ffn_w3, L0_ffn_w2, L0_ffn_wr), axis=-1)
    x = _layernorm(x + _L1_attn_ref(x, L1_attn_Wq, L1_attn_Wk, L1_attn_Wv, L1_attn_Wo, L1_attn_rms_w), axis=-1)
    x = _layernorm(x + _L1_xattn_ref(x, ctx_2048, ctx_2048, L1_xattn_gamma), axis=-1)
    x = _layernorm(x + _L1_ffn_ref(x, L1_ffn_Wg, L1_ffn_W1, L1_ffn_W3, L1_ffn_W2, L1_ffn_Ws1, L1_ffn_Ws3, L1_ffn_Ws2), axis=-1)
    return x

_drawn_inputs = setup_inputs


def setup_inputs(seed=0):
    import zlib

    import numpy as np

    out = dict(_drawn_inputs(seed))
    spreads = {'L0_xattn_ln_scale': (1.0, 0.2), 'L1_attn_rms_w': (1.0, 0.2)}
    factors = {'L0_attn_Wq': 4.287,
     'L0_xattn_bi': 95.846,
     'L0_ffn_wr': 14.086,
     'L1_ffn_Wg': 7.813,
     'L1_ffn_W1': 6.887,
     'L1_ffn_W3': 6.764,
     'L1_ffn_W2': 6.754,
     'L1_ffn_Ws1': 8.0,
     'L1_ffn_Ws3': 8.0,
     'L1_ffn_Ws2': 8.0}
    for name, (base, spread) in spreads.items():
        noise = np.random.default_rng([zlib.crc32(name.encode()), seed]).standard_normal(out[name].shape)
        drawn = base * np.exp(spread * noise) if base else spread * noise
        out[name] = jnp.asarray(drawn.astype(out[name].dtype))
    for name, factor in factors.items():
        out[name] = (out[name] * factor).astype(out[name].dtype)
    return out
```

```python
from contextlib import ExitStack

import numpy as np

import concourse.bass as bass
from concourse import mybir

F32 = mybir.dt.float32
BF16 = mybir.dt.bfloat16
U32 = mybir.dt.uint32
ALU = mybir.AluOpType
ACT = mybir.ActivationFunctionType
AX = mybir.AxisListType

P = 128
SEQS = 16
D = 512
KC = D // P
GROUPS = 4
GB = SEQS // GROUPS
GT = GB * P
BANKS = 8

H0 = 16
KV0 = 4
REP = H0 // KV0
HX = 16
HD = 32
HR = P // HD
VS = HD + 1
EPS_DEN = 1e-6
EPS_LN = 1e-5
EPS_MLSTM = 1e-6
BIG = 1e30

E0 = 8
NE = 16
FI = 352
FS = 704
CH = 8
CD = P // CH


class Signal:

    def __init__(self, sem, per=0, unit=1):
        self.sem, self.per, self.unit = sem, per * unit, unit

    def wait(self, eng, turn, count):
        value = turn * self.per + count * self.unit
        if not (isinstance(value, int) and value == 0):
            eng.wait_ge(self.sem, value)


class Steps:

    def __init__(self, sem, per):
        self.sem, self.per, self.n = sem, per, 0

    def did(self, ins):
        self.n += 1
        ins.then_inc(self.sem, 1)

    def wait(self, eng, turn):
        eng.wait_ge(self.sem, turn * self.per + self.n)

    def close(self, name):
        if self.n != self.per:
            raise ValueError(f"{name}: {self.n} steps")


class Tiles:

    def __init__(self, banks, filled, order, drained):
        self.banks, self.order, self.drained = banks, order, drained
        self.at = {key: n for n, key in enumerate(order)}
        self.filled = Signal(filled, len(order))
        self.slots = -(-len(order) // len(banks)) * len(banks)

    def bank(self, key):
        return self.banks[self.at[key] % len(self.banks)]

    def start(self, pe, turn, key, needs=()):
        n = self.at[key] - len(self.banks)
        if n >= 0:
            sig, count = self.drained(self.order[n])
        elif isinstance(turn, int):
            sig, count = None, 0
        else:
            n += self.slots
            n = n if n < len(self.order) else n - len(self.banks)
            sig, count = self.drained(self.order[n])[0], 0
        needs = list(needs)
        if sig and not any(s is sig and c >= count for s, c in needs):
            needs = [(s, c) for s, c in needs if s is not sig] + [(sig, count)]
        for s, c in needs:
            s.wait(pe, turn, c)
        return self.bank(key)

    def done(self, ins):
        ins.then_inc(self.filled.sem, 1)

    def wait(self, eng, turn, key):
        self.filled.wait(eng, turn, self.at[key] + 1)
        return self.bank(key)


def build_layer0(nc, t):
    with ExitStack() as ctx:
        def sb(name, shape, dt=F32):
            return ctx.enter_context(nc.sbuf_tensor("a_" + name, shape, dt))

        def signal(name, per, unit=1):
            return Signal(ctx.enter_context(nc.semaphore("a_" + name)), per, unit)

        banks = [ctx.enter_context(nc.psum_tensor(f"a_bank{i}", [P, 512], F32)) for i in range(BANKS)]

        wq = sb("wq", [P, 2, KC, D])
        wk = sb("wk", [P, KC, KV0 * P])
        wv = sb("wv", [P, KC, KV0 * P])
        wo = sb("wo", [P, 2, REP, D])
        w1, w3 = wq[:, 0], wq[:, 1]
        wr = sb("wr", [P, KC, E0])
        wi = sb("wi", [P, 3 * KC, HX])
        wf = sb("wf", [P, 3 * KC, HX])
        bias = sb("bias", [P, 2])
        lnw = sb("lnw", [P, D])
        cos = sb("cos", [P, P])
        sin = sb("sin", [P, P])
        causal = sb("causal", [P, P])
        barred = sb("barred", [P, P])
        ident = sb("ident", [P, P])
        sel = sb("sel", [P, HX, P])
        iota = sb("iota", [P, E0])
        ones = sb("ones", [P, P])

        xg = sb("xg", [P, GB, D])
        xT = sb("xT", [P, KC, GT])
        cT = sb("cT", [P, KC, GT])
        scratch = sb("scratch", [P, 10240])
        kf = scratch[:, 0:2048].rearrange("p (j t) -> p j t", j=KV0)
        v = scratch[:, 2048:4096].rearrange("p (b t) -> p b t", b=GB)
        qf = scratch[:, 4096:8192].rearrange("p (u r t) -> p u r t", u=2, r=REP)
        st = scratch[:, 8192:10240].rearrange("p (b t) -> p b t", b=GB)
        scratch2 = sb("scratch2", [P, 8192])
        ot = scratch2[:, 0:2048].rearrange("p (b r t) -> p b r t", b=GB, r=REP)
        rt1 = scratch2[:, 2048:3072].rearrange("p (u t) -> p u t", u=2)
        rt2 = scratch2[:, 3072:4096].rearrange("p (u t) -> p u t", u=2)
        ry = scratch2[:, 4096:5120].rearrange("p (u t) -> p u t", u=2)
        ee = scratch2[:, 5120:6144].rearrange("p (u t) -> p u t", u=2)
        dn = scratch2[:, 7168:8192].rearrange("p (u t) -> p u t", u=2)
        xz = sb("xz", [P, 2, GB, HR, P])
        dec = scratch[:, 0:4096].rearrange("p (u r b s) -> p u r b s", u=2, r=HR, b=GB)
        cc = scratch[:, 4096:8192].rearrange("p (u b r s) -> p u b r s", u=2, b=GB, r=HR)
        hv = scratch[:, 8192:10240].rearrange("p (n e) -> p n e", e=HD)
        hc = scratch2[:, 0:2048].rearrange("p (n e) -> p n e", e=HD)
        hs = scratch2[:, 2048:4096].rearrange("p (n e) -> p n e", e=HD)
        ho = scratch2[:, 4096:4096 + GB * HX * VS].rearrange("p (b h e) -> p b h e", b=GB, h=HX)
        va = sb("va", [P, GB * HX * VS + P - VS])
        ga = sb("ga", [P, GT])
        gi, gf, g1, g2 = (scratch[0:HX, 8192 + GT * n:8192 + GT * (n + 1)] for n in range(4))
        g3 = scratch2[0:HX, 0:GT]
        am = sb("am", [P, GB, 48])
        em = sb("em", [P, GB, HX])
        hn = sb("hn", [P, GB * HX])
        hm = sb("hm", [P, GB * HX])
        h1 = scratch[:, 0:2048].rearrange("p (c t) -> p c t", c=KC)
        h2 = scratch[:, 2048:4096].rearrange("p (b t) -> p b t", b=GB)
        se = scratch2[:, 0:1024].rearrange("p (u t) -> p u t", u=2)
        sr = scratch2[:, 1024:1536]
        pr = sb("pr", [P, GB, E0])
        rmx = sb("rmx", [P, GB])
        top = sb("top", [P, GB, 8])
        topi = sb("topi", [P, GB, 8], U32)
        topf = sb("topf", [P, GB, 8])
        eq = sb("eq", [P, 2, E0])
        gate = sb("gate", [P, GB, E0])
        fsum = sb("fsum", [E0, D])
        pre = sb("pre", [E0, D])
        stats = sb("stats", [P, GB, 6])
        mom = sb("mom", [P, GB, 2])
        lnv = sb("lnv", [P, GB])
        rstd = sb("rstd", [P, GB])
        eps = sb("eps", [P, 2])
        held = sb("held", [P, 2])

        NF = KV0 + H0
        weights = signal("weights", 0, 16)
        NW = 13
        wq_in = [signal(f"wq_in{u}", KV0 // 2 + 1, 16) for u in range(2)]
        wo_in = [signal(f"wo_in{u}", KV0 // 2, 16) for u in range(2)]
        x_in, xT_in, c_in, cT_in = (signal(n, 1, 16) for n in ("x_in", "xT_in", "c_in", "cT_in"))
        consts = signal("consts", 0)
        wsum = signal("wsum", 0)
        rope_parts, rope_sum = signal("rope_parts", NF), signal("rope_sum", NF)
        elu_parts, feature = signal("elu_parts", NF), signal("feature", NF)
        v_ready = signal("v_ready", GB)
        masked, den_copied = signal("masked", KV0 * GB), signal("den_copied", KV0 * GB)
        o_scaled, y_added = signal("o_scaled", KV0 * GB), signal("y_added", KV0 * GB)
        moments, rstd_ready, normed = signal("moments", 3), signal("rstd_ready", 3), signal("normed", 3 * GB)
        xT_ready = signal("xT_ready", 2 * KC)
        xz_spread, xz_ready = signal("xz_spread", KC * (HR - 1)), signal("xz_ready", KC)
        gates_copied, gate_abs, gate_log = signal("gates_copied", 1), signal("gate_abs", 1), signal("gate_log", 1)
        gates_ready, gt_copied = signal("gates_ready", 1), signal("gt_copied", 1)
        em_ready = signal("em_ready", 1)
        decay_arg, decay = signal("decay_arg", HX), signal("decay", HX)
        c_ready, ho_ready = signal("c_ready", KC * GB), signal("ho_ready", KC * GB)
        h_centred, h_squared, h_rstd = signal("h_centred", 1), signal("h_squared", 1), signal("h_rstd", 1)
        h_var = signal("h_var", 1)
        rt_shift, rt_exp, routed = signal("rt_shift", 1), signal("rt_exp", 1), signal("routed", 1)
        h_exp, h_ready = signal("h_exp", KC + GB), signal("h_ready", KC + GB)
        f_added, pre_ready = signal("f_added", 1), signal("pre_ready", 1)
        stored = signal("stored", 2, 16)
        fstored = signal("fstored", 0, 16)

        order = [("k", j) for j in range(KV0)] + [("v", b) for b in range(GB)]
        order += [("q", r) for r in range(REP)]
        for j in range(KV0):
            if j + 1 < KV0:
                order += [("q", REP * (j + 1) + r) for r in range(REP)]
            order += [("s", j, b) for b in range(GB)]
            if j:
                order += [("y", j - 1, b) for b in range(GB)]
            order += [(kind, j, b) for b in range(GB) for kind in ("d", "o")]
        order += [("y", KV0 - 1, b) for b in range(GB)]
        order += [("xt", 0, c) for c in range(KC)] + [("gate",), ("gt",)]
        order += [("cb", h) for h in range(HR)]
        for c in range(KC):
            if c + 1 < KC:
                order += [("cb", HR * (c + 1) + r) for r in range(HR)]
            order += [("qk", c, b) for b in range(GB)]
            if c:
                order += [("ho", c - 1, b) for b in range(GB)]
        order += [("ho", KC - 1, b) for b in range(GB)]
        order += [("xt", 1, c) for c in range(KC)] + [("rt",)]
        order += [("f1", c) for c in range(KC)] + [("f2", b) for b in range(GB)] + [("fa",)]

        def drained(key):
            kind, *n = key
            return {
                "k": lambda: (rope_parts, n[0] + 1),
                "v": lambda: (v_ready, n[0] + 1),
                "q": lambda: (rope_parts, KV0 + n[0] + 1),
                "s": lambda: (masked, GB * n[0] + n[1] + 1),
                "d": lambda: (den_copied, GB * n[0] + n[1] + 1),
                "o": lambda: (o_scaled, GB * n[0] + n[1] + 1),
                "y": lambda: (y_added, GB * n[0] + n[1] + 1),
                "xt": lambda: (xT_ready, KC * n[0] + n[1] + 1),
                "gate": lambda: (gates_copied, 1),
                "gt": lambda: (gt_copied, 1),
                "cb": lambda: (decay_arg, n[0] + 1),
                "qk": lambda: (c_ready, GB * n[0] + n[1] + 1),
                "ho": lambda: (ho_ready, GB * n[0] + n[1] + 1),
                "rt": lambda: (rt_shift, 1),
                "f1": lambda: (h_ready, n[0] + 1),
                "f2": lambda: (h_ready, KC + n[0] + 1),
                "fa": lambda: (f_added, 1),
            }[kind]()

        tiles = Tiles(banks, ctx.enter_context(nc.semaphore("a_filled")), order, drained)
        vstep = Steps(ctx.enter_context(nc.semaphore("a_vector_step")), 68)
        astep = Steps(ctx.enter_context(nc.semaphore("a_scalar_step")), 25)
        block = ctx.enter_context(nc.Block())

        def by_batch(ap):
            return ap.unsqueeze(1).broadcast_to([ap.shape[0], GB, P])

        @block.sync
        def _(sp):
            for dst, src in ((wk, "wk0"), (cos, "cos0"), (sin, "sin0"), (wv, "wv0"), (causal, "causal"),
                             (wi, "wi0"), (wf, "wf0"), (barred, "barred"), (sel, "sel"), (lnw, "lnw0"),
                             (wr, "wr0"), (iota, "iota"), (bias, "bias0")):
                sp.dma_start(dst[:], t[src]).then_inc(weights.sem, 16)
            sp.wait_ge(consts.sem, 10)
            with sp.Fori(0, GROUPS) as g:
                h_ready.wait(sp, g, 0)
                sp.dma_start(xT[:, :, :], t["xT"][g]).then_inc(xT_in.sem, 16)
                for j in range(2):
                    sp.dma_start(wq[:, j], t["wq0"][j]).then_inc(wq_in[j].sem, 16)
                    sp.dma_start(wo[:, j], t["wo0"][j]).then_inc(wo_in[j].sem, 16)
                sp.dma_start(cT[:, :, :], t["cT"][g]).then_inc(cT_in.sem, 16)
                sp.dma_start(va[:, 0:GB * HX * VS].rearrange("p (n e) -> p n e", e=VS)[:, :, 0:HD],
                             t["c"][g].rearrange("p b (h e) -> p (b h) e", e=HD)).then_inc(c_in.sem, 16)
                stored.wait(sp, g, 0)
                sp.dma_start(xg[:, :, :], t["x"][g]).then_inc(x_in.sem, 16)
                for j in range(2, KV0 + 2):
                    feature.wait(sp, g, KV0 + REP * (j - 1))
                    src = t["wq0"][j] if j < KV0 else t[("w10", "w30")[j - KV0]]
                    sp.dma_start(wq[:, j % 2], src).then_inc(wq_in[j % 2].sem, 16)
                    if j < KV0:
                        y_added.wait(sp, g, GB * (j - 1))
                        sp.dma_start(wo[:, j % 2], t["wo0"][j]).then_inc(wo_in[j % 2].sem, 16)
            f_added.wait(sp, GROUPS, 0)
            sp.dma_start(t["fsum"], fsum[:, :]).then_inc(fstored.sem, 16)
            sp.wait_ge(fstored.sem, 16)
            sp.wait_ge(stored.sem, 2 * 16 * GROUPS)

        @block.gpsimd
        def _(pool):
            pool.memset(ident[:, :], 0.0).then_inc(consts.sem, 1)
            pool.memset(ones[:, :], 1.0).then_inc(consts.sem, 1)
            pool.memset(xz[:], 0.0).then_inc(consts.sem, 1)
            pool.memset(va[:], 1.0).then_inc(consts.sem, 1)
            pool.memset(ga[:], 0.0).then_inc(consts.sem, 1)
            pool.memset(fsum[:], 0.0).then_inc(consts.sem, 1)
            pool.memset(eps[:, 0:1], EPS_LN).then_inc(consts.sem, 1)
            pool.memset(eps[:, 1:2], EPS_MLSTM).then_inc(consts.sem, 1)
            pool.memset(held[:], 0.0).then_inc(consts.sem, 1)
            pool.wait_ge(consts.sem, 9)
            pool.affine_select(out=ident[:, :], in_=ident[:, :], compare_op=ALU.not_equal, fill=1.0,
                               base=0, pattern=[[-1, P]], channel_multiplier=1).then_inc(consts.sem, 1)
            pool.wait_ge(consts.sem, 10)
            pool.wait_ge(weights.sem, 16 * NW)
            for w in (wi, wf):
                pool.tensor_tensor(w[:, KC:2 * KC, :], w[:, KC:2 * KC, :], w[:, 2 * KC:3 * KC, :],
                                   ALU.add).then_inc(wsum.sem, 1)
            pool.wait_ge(wsum.sem, 2)
            with pool.Fori(0, GROUPS) as g:
                xz_ready.wait(pool, g, 0)

                def rope(n):
                    rope_parts.wait(pool, g, n + 1)
                    feature.wait(pool, g, max(n - 1, 0))
                    pool.tensor_tensor(ry[:, n % 2, :], rt1[:, n % 2, :], rt2[:, n % 2, :],
                                       ALU.add).then_inc(rope_sum.sem, 1)

                for n in range(NF):
                    rope(n)
                for c in range(KC):
                    xT_ready.wait(pool, g, c + 1)
                    c_ready.wait(pool, g, GB * max(c - 1, 0))
                    for r in range(HR):
                        rows = slice(HD * r, HD * r + HD)
                        src = xT[rows, c, :].rearrange("p (b s) -> p b s", b=GB)
                        if r == 0:
                            xz_ready.wait(pool, g, c)
                        else:
                            xz_spread.wait(pool, g, (HR - 1) * c + r)
                        ins = pool.tensor_tensor(xz[rows, c % 2, :, r, :], src, by_batch(ones[rows, :]), ALU.mult)
                        ins.then_inc(xz_ready.sem if r == HR - 1 else xz_spread.sem, 1)

        @block.scalar
        def _(act):
            act.wait_ge(weights.sem, 16 * NW)
            act.wait_ge(consts.sem, 10)
            with act.Fori(0, GROUPS) as g:
                astep.n = 0

                def elu(n):
                    rope_sum.wait(act, g, n + 1)
                    feature.wait(act, g, max(n - 1, 0))
                    astep.did(act.activation(ee[:, n % 2, :], ry[:, n % 2, :], ACT.Relu, scale=-1.0))
                    astep.wait(act, g)
                    act.activation(ee[:, n % 2, :], ee[:, n % 2, :], ACT.Exp, scale=-1.0).then_inc(elu_parts.sem, 1)

                def norm(i):
                    moments.wait(act, g, i + 1)
                    astep.did(act.activation(lnv[:, :], mom[:, :, 1], ACT.Ln, bias=eps[:, 0:1]))
                    astep.wait(act, g)
                    act.activation(rstd[:, :], lnv[:, :], ACT.Exp, scale=-0.5).then_inc(rstd_ready.sem, 1)

                def turned(i):
                    for c in range(KC):
                        bank = tiles.wait(act, g, ("xt", i, c))
                        if i == 1:
                            xz_ready.wait(act, g, KC)
                        act.activation(xT[:, c, :], bank[:, :], ACT.Copy).then_inc(xT_ready.sem, 1)

                for j in range(KV0):
                    elu(j)
                for b in range(GB):
                    bank = tiles.wait(act, g, ("v", b))
                    act.activation(v[:, b, :], bank[:, :], ACT.Copy).then_inc(v_ready.sem, 1)
                for r in range(REP):
                    elu(KV0 + r)
                for j in range(KV0):
                    if j + 1 < KV0:
                        for r in range(REP):
                            elu(KV0 + REP * (j + 1) + r)
                    for b in range(GB):
                        n = GB * j + b
                        bank = tiles.wait(act, g, ("d", j, b))
                        o_scaled.wait(act, g, max(n - 1, 0))
                        act.activation(dn[:, n % 2, :], bank[:, :], ACT.Copy,
                                       bias=EPS_DEN).then_inc(den_copied.sem, 1)
                norm(0)
                turned(0)
                bank = tiles.wait(act, g, ("gate",))
                act.activation(gi[:, :], bank[0:HX, :], ACT.Identity, bias=bias[0:HX, 0:1])
                act.activation(gf[:, :], bank[32:32 + HX, :], ACT.Identity,
                               bias=bias[32:32 + HX, 0:1]).then_inc(gates_copied.sem, 1)
                gate_abs.wait(act, g, 1)
                astep.did(act.activation(g2[:, :], g2[:, :], ACT.Exp, scale=-1.0))
                astep.wait(act, g)
                act.activation(g2[:, :], g2[:, :], ACT.Ln, bias=1.0).then_inc(gate_log.sem, 1)
                gt_copied.wait(act, g, 1)
                act.activation(em[:, :, :], am[:, :, 32:48], ACT.Exp).then_inc(em_ready.sem, 1)

                def decays(c):
                    for r in range(HR):
                        decay_arg.wait(act, g, HR * c + r + 1)
                        act.activation(dec[:, c % 2, r, :, :], dec[:, c % 2, r, :, :], ACT.Exp,
                                       scale=-1.0).then_inc(decay.sem, 1)

                def heads(c):
                    for b in range(GB):
                        bank = tiles.wait(act, g, ("ho", c, b))
                        act.activation(ho[:, b, HR * c:HR * c + HR, :],
                                       bank[:, :].rearrange("p (r e) -> p r e", r=HR)[:, :, 0:VS],
                                       ACT.Copy).then_inc(ho_ready.sem, 1)

                decays(0)
                for c in range(KC):
                    if c + 1 < KC:
                        decays(c + 1)
                    if c:
                        heads(c - 1)
                heads(KC - 1)
                h_centred.wait(act, g, 1)
                act.activation(hs[:], hc[:], ACT.Square).then_inc(h_squared.sem, 1)
                h_var.wait(act, g, 1)
                astep.did(act.activation(hm[:, :], hm[:, :], ACT.Ln, scale=1.0 / HD, bias=eps[:, 1:2]))
                astep.wait(act, g)
                act.activation(hm[:, :], hm[:, :], ACT.Exp, scale=-0.5).then_inc(h_rstd.sem, 1)
                norm(1)
                turned(1)
                rt_shift.wait(act, g, 1)
                act.activation(pr[:], pr[:], ACT.Exp).then_inc(rt_exp.sem, 1)
                for n in range(KC + GB):
                    bank = tiles.wait(act, g, ("f1", n) if n < KC else ("f2", n - KC))
                    h_ready.wait(act, g, max(n - 1, 0))
                    act.activation(se[:, n % 2, :], bank[:, :], ACT.Exp, scale=-1.0).then_inc(h_exp.sem, 1)
                norm(2)
                pre_ready.wait(act, g, 1)
                act.dma_start(t["pre"][g], pre[:, :]).then_inc(stored.sem, 16)
                normed.wait(act, g, 3 * GB)
                act.dma_start(t["x3"][g], xg[:, :, :]).then_inc(stored.sem, 16)
            astep.close("layer 0, scalar")

        @block.tensor
        def _(pe):
            pe.wait_ge(weights.sem, 16 * NW)
            pe.wait_ge(wsum.sem, 2)

            with pe.Fori(0, GROUPS) as g:
                def chunks(key, lhs, rhs, n=KC, needs=()):
                    bank = tiles.start(pe, g, key, needs)
                    for c in range(n):
                        ins = pe.matmul(bank[:, :], lhs(c), rhs(c), start=(c == 0), stop=(c == n - 1))
                    tiles.done(ins)

                def queries(j):
                    wq_in[j % 2].wait(pe, g, j // 2 + 1)
                    for r in range(REP):
                        h = REP * j + r
                        chunks(("q", h), lambda c: wq[:, j % 2, c, r * P:(r + 1) * P], lambda c: xT[:, c, :])

                def outputs(j):
                    wo_in[j % 2].wait(pe, g, j // 2 + 1)
                    for b in range(GB):
                        chunks(("y", j, b), lambda r: ot[:, b, r, :], lambda r: wo[:, j % 2, r, :], REP,
                               [(o_scaled, GB * j + b + 1)])

                def turn_x(i):
                    for c in range(KC):
                        bank = tiles.start(pe, g, ("xt", i, c))
                        for b in range(GB):
                            if c == 0:
                                normed.wait(pe, g, GB * i + b + 1)
                            ins = pe.transpose(bank[:, b * P:(b + 1) * P], xg[:, b, c * P:(c + 1) * P], ident[:, :])
                        tiles.done(ins)

                xT_in.wait(pe, g, 1)
                for j in range(KV0):
                    chunks(("k", j), lambda c: wk[:, c, j * P:(j + 1) * P], lambda c: xT[:, c, :])
                for b in range(GB):
                    chunks(("v", b), lambda c: xT[:, c, b * P:(b + 1) * P], lambda c: wv[:, c, :])
                queries(0)
                for j in range(KV0):
                    if j + 1 < KV0:
                        queries(j + 1)
                    for b in range(GB):
                        cols = slice(b * P, (b + 1) * P)
                        bank = tiles.start(pe, g, ("s", j, b), [(feature, KV0 + REP * (j + 1))])
                        tiles.done(pe.matmul(bank[:, :], kf[:, j, cols], qf[:, j % 2, :, cols],
                                             start=True, stop=True))
                    if j:
                        outputs(j - 1)
                    v_ready.wait(pe, g, GB)
                    for b in range(GB):
                        bank = tiles.start(pe, g, ("d", j, b), [(masked, GB * j + b + 1)])
                        tiles.done(pe.matmul(bank[:, :], ones[:, :], st[:, b, :], start=True, stop=True))
                        bank = tiles.start(pe, g, ("o", j, b))
                        tiles.done(pe.matmul(bank[:, :], v[:, b, j * P:(j + 1) * P], st[:, b, :],
                                             start=True, stop=True))
                outputs(KV0 - 1)

                turn_x(0)
                bank = tiles.start(pe, g, ("gate",), [(xT_ready, KC)])
                cT_in.wait(pe, g, 1)
                for at, w in ((0, wi), (32, wf)):
                    for c in range(2 * KC):
                        src = xT[:, c, :] if c < KC else cT[:, c - KC, :]
                        ins = pe.matmul(bank[at:at + HX, :], w[:, c, :], src, start=(c == 0), stop=(c == 2 * KC - 1))
                tiles.done(ins)
                gates_ready.wait(pe, g, 1)
                bank = tiles.start(pe, g, ("gt",))
                for b in range(GB):
                    ins = pe.transpose(bank[:, b * P:(b + 1) * P], ga[:, b * P:(b + 1) * P], ident[:, :])
                tiles.done(ins)

                def spread(c):
                    for r in range(HR):
                        h = HR * c + r
                        bank = tiles.start(pe, g, ("cb", h))
                        tiles.done(pe.matmul(bank[:, :], sel[:, h, :], ga[:, :], start=True, stop=True))

                def values(c):
                    c_in.wait(pe, g, 1)
                    for b in range(GB):
                        bank = tiles.start(pe, g, ("ho", c, b), [(c_ready, GB * c + b + 1)])
                        for r in range(HR):
                            at = VS * (HX * b + HR * c + r)
                            ins = pe.matmul(bank[:, r * P:(r + 1) * P], cc[:, c % 2, b, r, :],
                                            va[:, at:at + P], start=True, stop=True)
                        tiles.done(ins)

                spread(0)
                for c in range(KC):
                    if c + 1 < KC:
                        spread(c + 1)
                    xz_ready.wait(pe, g, c + 1)
                    for b in range(GB):
                        bank = tiles.start(pe, g, ("qk", c, b))
                        tiles.done(pe.matmul(bank[:, :], cT[:, c, b * P:(b + 1) * P], xz[:, c % 2, b, :, :],
                                             start=True, stop=True))
                    if c:
                        values(c - 1)
                values(KC - 1)

                turn_x(1)
                bank = tiles.start(pe, g, ("rt",), [(xT_ready, 2 * KC)])
                for b in range(GB):
                    for c in range(KC):
                        ins = pe.matmul(bank[:, b * E0:(b + 1) * E0], xT[:, c, b * P:(b + 1) * P], wr[:, c, :],
                                        start=(c == 0), stop=(c == KC - 1))
                tiles.done(ins)
                wq_in[0].wait(pe, g, KV0 // 2 + 1)
                for i in range(KC):
                    chunks(("f1", i), lambda c: w1[:, c, i * P:(i + 1) * P], lambda c: xT[:, c, :])
                wq_in[1].wait(pe, g, KV0 // 2 + 1)
                for b in range(GB):
                    chunks(("f2", b), lambda c: h1[:, c, b * P:(b + 1) * P], lambda c: w3[:, c, :],
                           needs=[(h_ready, KC)])
                routed.wait(pe, g, 1)
                bank = tiles.start(pe, g, ("fa",), [(h_ready, KC + GB)])
                for b in range(GB):
                    ins = pe.matmul(bank[0:E0, :], gate[:, b, :], h2[:, b, :], start=(b == 0), stop=(b == GB - 1))
                tiles.done(ins)

        @block.vector
        def _(dve):
            dve.wait_ge(weights.sem, 16 * NW)
            dve.wait_ge(consts.sem, 10)
            with dve.Fori(0, GROUPS) as g:
                vstep.n = 0

                def parts(n):
                    bank = tiles.wait(dve, g, ("k", n) if n < KV0 else ("q", n - KV0))
                    rope_sum.wait(dve, g, max(n - 1, 0))
                    view = bank[:, :].rearrange("p (b s) -> p b s", b=GB)
                    u = n % 2
                    dve.tensor_tensor(rt1[:, u, :].rearrange("p (b s) -> p b s", b=GB), view,
                                      by_batch(cos[:, :]), ALU.mult)
                    for to, of in ((0, 64), (64, 0)):
                        ins = dve.tensor_tensor(
                            rt2[to:to + 64, u, :].rearrange("p (b s) -> p b s", b=GB), view[of:of + 64],
                            by_batch(sin[of:of + 64, :]), ALU.mult)
                    ins.then_inc(rope_parts.sem, 1)

                def features(n):
                    elu_parts.wait(dve, g, n + 1)
                    j, r = divmod(n - KV0, REP)
                    out = kf[:, n, :] if n < KV0 else qf[:, j % 2, r, :]
                    dve.scalar_tensor_tensor(out, ry[:, n % 2, :], 0.0, ee[:, n % 2, :], ALU.max,
                                             ALU.add).then_inc(feature.sem, 1)

                def run_of(first, count):
                    for n in range(first, first + count):
                        parts(n)
                        if n > first:
                            features(n - 1)
                    features(first + count - 1)

                def added(j):
                    for b in range(GB):
                        bank = tiles.wait(dve, g, ("y", j, b))
                        if j:
                            y_added.wait(dve, g, GB * (j - 1) + b + 1)
                        dve.tensor_tensor(xg[:, b, :], bank[:, :], xg[:, b, :], ALU.add).then_inc(y_added.sem, 1)

                def norm(i, last):
                    last()
                    for b in range(GB):
                        ins = dve.bn_stats(stats[:, b, :], xg[:, b, :])
                    vstep.did(ins)
                    vstep.wait(dve, g)
                    dve.tensor_copy(held[:, 1:2], held[:, 0:1])
                    for b in range(GB):
                        ins = dve.bn_aggr(mom[:, b, :], stats[:, b, :])
                    ins.then_inc(moments.sem, 1)
                    rstd_ready.wait(dve, g, i + 1)
                    for b in range(GB):
                        dve.tensor_scalar(xg[:, b, :], xg[:, b, :], mom[:, b, 0:1], rstd[:, b:b + 1],
                                          ALU.subtract, ALU.mult).then_inc(normed.sem, 1)

                run_of(0, KV0)
                run_of(KV0, REP)
                x_in.wait(dve, g, 1)
                for j in range(KV0):
                    if j + 1 < KV0:
                        run_of(KV0 + REP * (j + 1), REP)
                    for b in range(GB):
                        bank = tiles.wait(dve, g, ("s", j, b))
                        dve.tensor_tensor(st[:, b, :].rearrange("p (r q) -> p r q", r=REP),
                                          bank[:, :].rearrange("p (r q) -> p r q", r=REP),
                                          by_batch(causal[:, :]), ALU.mult).then_inc(masked.sem, 1)
                    if j:
                        added(j - 1)
                    for b in range(GB):
                        n = GB * j + b
                        den_copied.wait(dve, g, n + 1)
                        vstep.did(dve.reciprocal(dn[:, n % 2, :], dn[:, n % 2, :]))
                        vstep.wait(dve, g)
                        bank = tiles.wait(dve, g, ("o", j, b))
                        dve.tensor_tensor(ot[:, b, :, :], bank[:, :].rearrange("p (r q) -> p r q", r=REP),
                                          dn[:, n % 2, :].rearrange("p (r q) -> p r q", r=REP),
                                          ALU.mult).then_inc(o_scaled.sem, 1)
                added(KV0 - 1)
                norm(0, lambda: y_added.wait(dve, g, KV0 * GB))

                gates_copied.wait(dve, g, 1)
                vstep.did(dve.tensor_scalar(g1[:, :], gf[:, :], 0.0, None, ALU.min))
                dve.scalar_tensor_tensor(g2[:, :], gf[:, :], -1.0, gf[:, :], ALU.mult,
                                         ALU.max).then_inc(gate_abs.sem, 1)
                gate_log.wait(dve, g, 1)
                vstep.wait(dve, g)
                vstep.did(dve.tensor_tensor(g1[:, :], g1[:, :], g2[:, :], ALU.subtract))
                vstep.wait(dve, g)
                for b in range(GB):
                    cols = slice(b * P, (b + 1) * P)
                    ins = dve.tensor_tensor_scan(g3[:, cols], ones[0:HX, :], g1[:, cols], 0.0, ALU.mult, ALU.add)
                vstep.did(ins)
                vstep.wait(dve, g)
                vstep.did(dve.tensor_tensor(ga[0:HX, :], gi[:, :], g3[:, :], ALU.subtract))
                vstep.wait(dve, g)
                for b in range(GB):
                    cols = slice(b * P, (b + 1) * P)
                    ins = dve.tensor_tensor_scan(g1[:, cols], ones[0:HX, :], ga[0:HX, cols], -3e38,
                                                 ALU.mult, ALU.max)
                vstep.did(ins)
                vstep.wait(dve, g)
                dve.scalar_tensor_tensor(ga[32:32 + HX, :], g3[:, :], -1.0, g1[:, :], ALU.mult, ALU.subtract)
                dve.tensor_copy(ga[64:64 + HX, :], g1[:, :]).then_inc(gates_ready.sem, 1)
                bank = tiles.wait(dve, g, ("gt",))
                dve.tensor_copy(am[:, :, :], bank[:, :].rearrange("p (b n) -> p b n", b=GB)[:, :, 0:48])\
                   .then_inc(gt_copied.sem, 1)
                gt_copied.wait(dve, g, 1)

                def decay_args(c):
                    c_ready.wait(dve, g, GB * max(c - 1, 0))
                    for r in range(HR):
                        h = HR * c + r
                        bank = tiles.wait(dve, g, ("cb", h))
                        for b in range(GB):
                            ins = dve.scalar_tensor_tensor(
                                dec[:, c % 2, r, b, :], bank[:, b * P:(b + 1) * P], am[:, b, h:h + 1],
                                barred[:, :], ALU.subtract, ALU.max)
                        ins.then_inc(decay_arg.sem, 1)

                decay_args(0)
                for c in range(KC):
                    if c + 1 < KC:
                        decay_args(c + 1)
                    decay.wait(dve, g, HR * (c + 1))
                    for b in range(GB):
                        bank = tiles.wait(dve, g, ("qk", c, b))
                        dve.scalar_tensor_tensor(
                            cc[:, c % 2, b, :, :], bank[:, :].rearrange("p (r s) -> p r s", r=HR),
                            float(HD) ** -0.5, dec[:, c % 2, :, b, :], ALU.mult, ALU.mult).then_inc(c_ready.sem, 1)

                hall = ho.rearrange("p b h e -> p (b h) e")
                ho_ready.wait(dve, g, KC * GB)
                em_ready.wait(dve, g, 1)

                def chained(ins):
                    vstep.did(ins)
                    vstep.wait(dve, g)

                def wide(ap):
                    return ap.unsqueeze(2).broadcast_to([P, GB * HX, HD])

                chained(dve.tensor_copy(hm[:, :], hall[:, :, HD]))
                chained(dve.scalar_tensor_tensor(hn[:, :], hm[:, :], -1.0, hm[:, :], ALU.mult, ALU.max))
                chained(dve.tensor_tensor(hn[:, :], hn[:, :], em[:, :, :].rearrange("p b h -> p (b h)"), ALU.max))
                chained(dve.tensor_scalar(hn[:, :], hn[:, :], EPS_MLSTM, None, ALU.add))
                chained(dve.reciprocal(hn[:, :], hn[:, :]))
                chained(dve.tensor_tensor(hv[:], hall[:, :, 0:HD], wide(hn[:, :]), ALU.mult))
                chained(dve.tensor_reduce(hm[:, :], hv[:], AX.X, ALU.add))
                chained(dve.tensor_scalar(hm[:, :], hm[:, :], 1.0 / HD, None, ALU.mult))
                dve.tensor_tensor(hc[:], hv[:], wide(hm[:, :]), ALU.subtract).then_inc(h_centred.sem, 1)
                h_squared.wait(dve, g, 1)
                dve.tensor_reduce(hm[:, :], hs[:], AX.X, ALU.add).then_inc(h_var.sem, 1)
                h_rstd.wait(dve, g, 1)
                chained(dve.tensor_tensor(hc[:], hc[:], wide(hm[:, :]), ALU.mult))
                hrow = hc.rearrange("p (b h) e -> p b (h e)", b=GB)
                chained(dve.tensor_tensor(hrow, hrow, lnw[:, :].unsqueeze(1).broadcast_to([P, GB, D]), ALU.mult))
                chained(dve.tensor_tensor(xg[:, :, :], xg[:, :, :], hrow, ALU.add))
                norm(1, lambda: None)

                normed.wait(dve, g, 2 * GB)
                stored.wait(dve, g, 0)
                dve.tensor_copy(pre[:, :], xg[0:E0, 0, :]).then_inc(pre_ready.sem, 1)

                def each(ap):
                    return ap.unsqueeze(2).broadcast_to([P, GB, E0])

                bank = tiles.wait(dve, g, ("rt",))
                logits = bank[:, 0:GB * E0].rearrange("p (b e) -> p b e", b=GB)
                chained(dve.tensor_reduce(rmx[:, :], logits, AX.X, ALU.max))
                dve.tensor_tensor(pr[:, :, :], logits, each(rmx[:, :]), ALU.subtract).then_inc(rt_shift.sem, 1)
                rt_exp.wait(dve, g, 1)
                chained(dve.tensor_reduce(rmx[:, :], pr[:, :, :], AX.X, ALU.add))
                chained(dve.reciprocal(rmx[:, :], rmx[:, :]))
                chained(dve.tensor_tensor(pr[:, :, :], pr[:, :, :], each(rmx[:, :]), ALU.mult))
                dve.tensor_copy(held[:, 1:2], held[:, 0:1])
                for b in range(GB):
                    ins = dve.max(top[:, b, :], pr[:, b, :])
                chained(ins)
                dve.tensor_copy(held[:, 1:2], held[:, 0:1])
                for b in range(GB):
                    ins = dve.max_index(topi[:, b, :], top[:, b, :], pr[:, b, :])
                chained(ins)
                chained(dve.tensor_copy(topf[:, :, :], topi[:, :, :]))
                chained(dve.tensor_tensor(rmx[:, :], top[:, :, 0], top[:, :, 1], ALU.add))
                chained(dve.reciprocal(rmx[:, :], rmx[:, :]))
                chained(dve.tensor_tensor(top[:, :, 0:2], top[:, :, 0:2],
                                          rmx[:, :].unsqueeze(2).broadcast_to([P, GB, 2]), ALU.mult))
                for b in range(GB):
                    for k in range(2):
                        ins = dve.tensor_scalar(eq[:, k, :], iota[:, :], topf[:, b, k:k + 1], top[:, b, k:k + 1],
                                                ALU.is_equal, ALU.mult)
                    chained(ins)
                    ins = dve.tensor_tensor(gate[:, b, :], eq[:, 0, :], eq[:, 1, :], ALU.add)
                    if b < GB - 1:
                        chained(ins)
                ins.then_inc(routed.sem, 1)

                for n in range(KC + GB):
                    h_exp.wait(dve, g, n + 1)
                    chained(dve.tensor_scalar(se[:, n % 2, :], se[:, n % 2, :], 1.0, None, ALU.add))
                    chained(dve.reciprocal(sr, se[:, n % 2, :]))
                    bank = tiles.bank(("f1", n) if n < KC else ("f2", n - KC))
                    out = h1[:, n, :] if n < KC else h2[:, n - KC, :]
                    dve.tensor_tensor(out, bank[:, :], sr, ALU.mult).then_inc(h_ready.sem, 1)
                bank = tiles.wait(dve, g, ("fa",))
                dve.tensor_tensor(fsum[:, :], bank[0:E0, :], fsum[:, :], ALU.add).then_inc(f_added.sem, 1)
                norm(2, lambda: None)
            vstep.close("layer 0, vector")


def build_row_fix(nc, t):
    with ExitStack() as ctx:
        def sb(name, shape, dt=F32):
            return ctx.enter_context(nc.sbuf_tensor("b_" + name, shape, dt))

        w2, fs, ft = sb("w2", [P, KC, D]), sb("fs", [P, D]), sb("ft", [P, KC, P])
        ident, rows = sb("ident", [P, P]), sb("rows", [E0, D])
        stats, mom, rstd, eps = sb("stats", [E0, 6]), sb("mom", [E0, 2]), sb("rstd", [E0, 1]), sb("eps", [E0, 1])
        bank = ctx.enter_context(nc.psum_tensor("b_bank", [P, 512], F32))
        out = ctx.enter_context(nc.psum_tensor("b_out", [P, 512], F32))
        cleared, loaded, turned, copied, product, fixed, scaled, stored = (
            ctx.enter_context(nc.semaphore("b_" + n))
            for n in ("cleared", "loaded", "turned", "copied", "product", "fixed", "scaled", "stored"))
        step = ctx.enter_context(nc.semaphore("b_step"))
        block = ctx.enter_context(nc.Block())

        @block.sync
        def _(sp):
            sp.dma_start(w2[:], t["w20"]).then_inc(loaded, 16)
            sp.dma_start(ident[:], t["ident"]).then_inc(loaded, 16)
            sp.dma_start(rows[:], t["pre"][0]).then_inc(loaded, 16)
            sp.wait_ge(cleared, 2)
            sp.dma_start(fs[0:E0, :], t["fsum"]).then_inc(loaded, 16)
            sp.wait_ge(step, 5)
            sp.dma_start(t["x3"][0][0:E0, 0, :], rows[:]).then_inc(stored, 16)
            sp.wait_ge(stored, 16)

        @block.gpsimd
        def _(pool):
            pool.memset(fs[:], 0.0).then_inc(cleared, 1)
            pool.memset(eps[:], EPS_LN).then_inc(cleared, 1)

        @block.tensor
        def _(pe):
            pe.wait_ge(loaded, 64)
            for c in range(KC):
                ins = pe.transpose(bank[:, c * P:(c + 1) * P], fs[:, c * P:(c + 1) * P], ident[:, :])
            ins.then_inc(turned, 1)
            pe.wait_ge(copied, 1)
            for c in range(KC):
                ins = pe.matmul(out[:, :], ft[:, c, :], w2[:, c, :], start=(c == 0), stop=(c == KC - 1))
            ins.then_inc(product, 1)

        @block.vector
        def _(dve):
            dve.wait_ge(turned, 1)
            dve.tensor_copy(ft[:].rearrange("p c t -> p (c t)"), bank[:, :]).then_inc(copied, 1)
            dve.wait_ge(product, 1)
            dve.tensor_tensor(rows[:, :], out[0:E0, :], rows[:, :], ALU.add).then_inc(step, 1)
            dve.wait_ge(step, 1)
            dve.bn_stats(stats[:, :], rows[:, :]).then_inc(step, 1)
            dve.wait_ge(step, 2)
            dve.bn_aggr(mom[:, :], stats[:, :]).then_inc(step, 1)
            dve.wait_ge(scaled, 2)
            dve.tensor_scalar(rows[:, :], rows[:, :], mom[:, 0:1], rstd[:, 0:1],
                              ALU.subtract, ALU.mult).then_inc(step, 2)

        @block.scalar
        def _(act):
            act.wait_ge(cleared, 2)
            act.wait_ge(step, 3)
            act.activation(rstd[:, :], mom[:, 1:2], ACT.Ln, bias=eps[:, 0:1]).then_inc(scaled, 1)
            act.wait_ge(scaled, 1)
            act.activation(rstd[:, :], rstd[:, :], ACT.Exp, scale=-0.5).then_inc(scaled, 1)


def build_layer1(nc, t):
    with ExitStack() as ctx:
        def sb(name, shape, dt=F32):
            return ctx.enter_context(nc.sbuf_tensor("c_" + name, shape, dt))

        def signal(name, per, unit=1):
            return Signal(ctx.enter_context(nc.semaphore("c_" + name)), per, unit)

        PARTS = 3
        TERMS = ((0, 0), (0, 1), (1, 0), (1, 1), (0, 2), (2, 0))
        TR = len(TERMS) * CD
        SR = TR + PARTS
        LC = D // P

        banks = [ctx.enter_context(nc.psum_tensor(f"c_bank{i}", [P, 1024], F32)) for i in range(3)]
        pv = ctx.enter_context(nc.psum_tensor("c_pv", [P, 2, 512], F32))

        wq, wk, wv, wo = (sb(n, [P, KC, D]) for n in ("wq", "wk", "wv", "wo"))
        cos, sin = sb("cos", [P, CD]), sb("sin", [P, CD])
        decay = sb("decay", [P, HX, P])
        rmsw = sb("rmsw", [P, KC])
        gamma = sb("gamma", [P, 1])
        ident, ones = sb("ident", [P, P]), sb("ones", [P, P])
        perm = sb("perm", [P, 4, P])
        eps = sb("eps", [P, 1])
        held = sb("held", [P, 2])

        xg = sb("xg", [P, GB, D])
        area = sb("area", [P, 20480])
        yq = area[:, 0:2048].rearrange("p (b n) -> p b n", b=GB)
        yk = area[:, 2048:4096].rearrange("p (b n) -> p b n", b=GB)
        v = area[:, 4096:6144].rearrange("p (b n) -> p b n", b=GB)
        kT = area[:, 6144:8192].rearrange("p (b c n) -> p b c n", b=GB, c=KC)
        qT = area[:, 8192:10240].rearrange("p (b c n) -> p b c n", b=GB, c=KC)
        sm = area[:, 10240:14336].rearrange("p (u c r q) -> p u c r q", u=2, c=KC, r=HR)
        sq = yq.rearrange("p b (c q) -> p b c q", c=KC)
        at = yk.rearrange("p b (c q) -> p b c q", c=KC)
        r1 = area[:, 16384:17408].rearrange("p (u n) -> p u n", u=2)
        r2 = area[:, 17408:18432].rearrange("p (u n) -> p u n", u=2)
        xT = area[:, 18432:20480].rearrange("p (c t) -> p c t", c=KC)
        xz = sb("xz", [P, 2, KC, HR, P])
        probs = area[:, 0:4096].rearrange("p (u l n) -> p u l n", u=2, l=LC)
        ov = area[:, 4096:5120].rearrange("p (o n) -> p o n", o=2)
        rec = area[:, 5120:5632]
        cres = area[:, 5632:6144]
        qres = area[:, 6144:6656]
        cgr = area[:, 6656:8704].rearrange("p (b n) -> p b n", b=GB)
        cT = area[:, 8704:10752].rearrange("p (l t) -> p l t", l=LC)
        mx = sb("mx", [P, 2, P])
        mrow = sb("mrow", [P, P])
        qs = sb("qs", [P, 2, CH, D], BF16)
        ks = sb("ks", [P, 2, CH, D], BF16)
        qp = area[:, 10752:12288].bitcast(BF16).rearrange("p (u k n) -> p u k n", u=2, k=PARTS)
        kp = area[:, 12288:13824].bitcast(BF16).rearrange("p (u k n) -> p u k n", u=2, k=PARTS)
        mp = sb("mp", [P, 2, PARTS, P], BF16)
        vt = sb("vt", [P, LC, GB, CH, 32])
        stats, mom = sb("stats", [P, GB, 6]), sb("mom", [P, GB, 2])
        rstd, lnv, rms = sb("rstd", [P, GB]), sb("lnv", [P, GB]), sb("rms", [P, GB])

        NW, NC = 11, 7
        weights, consts = signal("weights", 0, 16), signal("consts", 0)
        x_in, c_in, cT_in = signal("x_in", 1, 16), signal("c_in", 1, 16), signal("cT_in", 1, 16)
        xT_ready, v_ready = signal("xT_ready", KC), signal("v_ready", GB)
        rot_parts, rotated = signal("rot_parts", 2 * GB), signal("rotated", 2 * GB)
        turned, spread_part, spread = signal("turned", 2 * GB), signal("spread_part", 3 * GB), signal("spread", GB)
        masked = signal("masked", KC * GB)
        squared, scaled, rms_ready, y_added = (signal(n, k) for n, k in (
            ("squared", GB), ("scaled", GB), ("rms_ready", 1), ("y_added", GB)))
        moments, rstd_ready, normed = signal("moments", 2), signal("rstd_ready", 2), signal("normed", 2 * GB)
        q_part, q_left, q_ready = signal("q_part", 2 * GB), signal("q_left", GB), signal("q_ready", GB)
        k_ready, vt_ready = signal("k_ready", GB), signal("vt_ready", 1)
        k_step = signal("k_step", 3 * GB)
        q_out, k_out, m_out = (signal(n, GB, 16) for n in ("q_out", "k_out", "m_out"))
        qs_in = [signal(f"qs_in{u}", len(TERMS) * GB // 2, 16) for u in range(2)]
        ks_in = [signal(f"ks_in{u}", len(TERMS) * GB // 2, 16) for u in range(2)]
        ms_in = [signal(f"ms_in{u}", GB // 2, 16) for u in range(2)]
        maxed, m_ready = signal("maxed", 2 * CH * GB), signal("m_ready", GB)
        exped = signal("exped", 2 * CH * GB)
        pv_done, pv_copied, rec_ready, added = (signal(n, GB) for n in ("pv_done", "pv_copied", "rec_ready", "added"))
        stored = signal("stored", 1, 16)

        order = [("xt", c) for c in range(KC)]
        for b in range(GB):
            order += [("q", b), ("k", b), ("v", b)]
        for b in range(GB):
            order += [("qt", b), ("kt", b)]
        for b in range(GB):
            order += [("s", b, c) for c in range(KC)]
            if b:
                order += [("a", b - 1)]
        order += [("a", GB - 1), ("ss",)] + [("y", b) for b in range(GB)]
        order += [("p", 0, h, u) for h in range(CH) for u in range(2)] + [("mt", 0)]
        for b in range(GB):
            for h in range(CH):
                order += [("e", b, h, u) for u in range(2)]
                if b + 1 < GB:
                    order += [("p", b + 1, h, u) for u in range(2)]
            if b + 1 < GB:
                order += [("mt", b + 1)]
            order += [("den", b), ("ret", b)]

        def drained(key):
            kind, *n = key
            return {
                "xt": lambda: (xT_ready, n[0] + 1),
                "q": lambda: (rot_parts, 2 * n[0] + 1),
                "k": lambda: (rot_parts, 2 * n[0] + 2),
                "v": lambda: (v_ready, n[0] + 1),
                "qt": lambda: (turned, 2 * n[0] + 1),
                "kt": lambda: (turned, 2 * n[0] + 2),
                "s": lambda: (masked, KC * n[0] + n[1] + 1),
                "a": lambda: (scaled, n[0] + 1),
                "ss": lambda: (rms_ready, 1),
                "y": lambda: (y_added, n[0] + 1),
                "p": lambda: (maxed, 2 * CH * n[0] + 2 * n[1] + n[2] + 1),
                "mt": lambda: (m_ready, n[0] + 1),
                "e": lambda: (exped, 2 * CH * n[0] + 2 * n[1] + n[2] + 1),
                "den": lambda: (rec_ready, n[0] + 1),
                "ret": lambda: (added, n[0] + 1),
            }[kind]()

        tiles = Tiles(banks, ctx.enter_context(nc.semaphore("c_filled")), order, drained)
        vstep = Steps(ctx.enter_context(nc.semaphore("c_vector_step")), 26)
        astep = Steps(ctx.enter_context(nc.semaphore("c_scalar_step")), 3)
        block = ctx.enter_context(nc.Block())

        @block.sync
        def _(sp):
            for dst, src in ((ident, "ident"), (wq, "wq1"), (cos, "cos1"), (sin, "sin1"), (wk, "wk1"), (wv, "wv1"),
                             (decay, "decay1"), (rmsw, "rms1"), (wo, "wo1"), (perm, "perm"), (gamma, "gamma1")):
                sp.dma_start(dst[:], t[src]).then_inc(weights.sem, 16)
            with sp.Fori(0, GROUPS) as g:
                stored.wait(sp, g, 0)
                sp.dma_start(xg[:, :, :], t["x3"][g]).then_inc(x_in.sem, 16)
                y_added.wait(sp, g, GB)
                sp.dma_start(cgr, t["c"][g]).then_inc(c_in.sem, 16)
                sp.dma_start(cT, t["cT"][g]).then_inc(cT_in.sem, 16)

                def out(b, ready, part, parked, done):
                    ready.wait(sp, g, b + 1)
                    sp.dma_start(parked[b % 2], part[:, b % 2]).then_inc(done.sem, 16)

                def stack(b, parked, done, side, dst, ins):
                    done.wait(sp, g, b + 1)
                    if side:
                        exped.wait(sp, g, 2 * CH * max(b - 1, 0))
                    for n, pair in enumerate(TERMS):
                        sp.dma_start(dst[CD * n:CD * n + CD, b % 2],
                                     parked[b % 2].rearrange("(h d) k l -> k d h l", d=CD)[pair[side]])\
                          .then_inc(ins[b % 2].sem, 16)

                def operands(b):
                    out(b, k_ready, kp, t["kpark"], k_out)
                    out(b, q_ready, qp, t["qpark"], q_out)
                    stack(b, t["kpark"], k_out, 1, ks, ks_in)
                    stack(b, t["qpark"], q_out, 0, qs, qs_in)

                def maxima(b):
                    m_ready.wait(sp, g, b + 1)
                    sp.dma_start(t["mpark"][b % 2].rearrange("k (x q) -> x k q", x=CH * LC), mp[0:CH * LC, b % 2])\
                      .then_inc(m_out.sem, 16)
                    m_out.wait(sp, g, b + 1)
                    sp.dma_start(qs[TR:SR, b % 2].rearrange("k h l -> k (h l)"), t["mpark"][b % 2])\
                      .then_inc(ms_in[b % 2].sem, 16)

                operands(0)
                operands(1)
                maxima(0)
                for b in range(1, GB):
                    maxima(b)
                    if b + 1 < GB:
                        operands(b + 1)
                normed.wait(sp, g, 2 * GB)
                sp.dma_start(t["x5"][g], xg[:, :, :]).then_inc(stored.sem, 16)
            sp.wait_ge(stored.sem, 16 * GROUPS)

        @block.gpsimd
        def _(pool):
            pool.memset(xz[:], 0.0).then_inc(consts.sem, 1)
            pool.memset(vt[:], 0.0).then_inc(consts.sem, 1)
            pool.memset(ones[:], 1.0).then_inc(consts.sem, 1)
            pool.memset(ks[:], 1.0).then_inc(consts.sem, 1)
            pool.memset(eps[:], EPS_LN).then_inc(consts.sem, 1)
            pool.memset(mx[:], 0.0).then_inc(consts.sem, 1)
            pool.wait_ge(consts.sem, 6)
            pool.memset(vt[:, :, :, :, CD], 1.0).then_inc(consts.sem, 1)
            pool.wait_ge(consts.sem, NC)
            with pool.Fori(0, GROUPS) as g:
                vt_ready.wait(pool, g, 0)
                k_ready.wait(pool, g, 0)
                for b in range(GB):
                    for i in range(2):
                        n = 2 * b + i
                        rot_parts.wait(pool, g, n + 1)
                        pool.tensor_tensor((yq, yk)[i][:, b, :], r1[:, i, :], r2[:, i, :],
                                           ALU.add).then_inc(rotated.sem, 1)
                rotated.wait(pool, g, 2 * GB)
                for b in range(GB):
                    turned.wait(pool, g, 2 * b + 1)
                    masked.wait(pool, g, KC * max(b - 1, 0))
                    for r in range(HR):
                        rows = slice(HD * r, HD * r + HD)
                        if r == 0:
                            spread.wait(pool, g, b)
                        else:
                            spread_part.wait(pool, g, (HR - 1) * b + r)
                        pool.tensor_tensor(xz[rows, b % 2, :, r, :], qT[rows, b],
                                           ones[rows, :].unsqueeze(1).broadcast_to([HD, KC, P]), ALU.mult)\
                            .then_inc((spread if r == HR - 1 else spread_part).sem, 1)
                spread.wait(pool, g, GB)
                cT_in.wait(pool, g, 1)
                for l in range(LC):
                    src = cT[:, l, :].rearrange("p (b h d) -> p b h d", b=GB, h=CH)
                    ins = pool.tensor_tensor(vt[:, l, :, :, 0:CD], src,
                                             ones[:, 0:1].unsqueeze(2).unsqueeze(3).broadcast_to([P, GB, CH, CD]),
                                             ALU.mult)
                ins.then_inc(vt_ready.sem, 1)
                c_in.wait(pool, g, 1)
                for b in range(GB):
                    u = b % 2
                    q_out.wait(pool, g, 0)
                    k_out.wait(pool, g, max(b - 1, 0))
                    one = ones[:, 0:1].broadcast_to([P, D])
                    if b:
                        k_ready.wait(pool, g, b)
                    pool.tensor_tensor(kp[:, u, 0, :], cgr[:, b, :], one, ALU.mult).then_inc(k_step.sem, 1)
                    k_step.wait(pool, g, 3 * b + 1)
                    pool.tensor_tensor(cres, cgr[:, b, :], kp[:, u, 0, :], ALU.subtract).then_inc(k_step.sem, 1)
                    k_step.wait(pool, g, 3 * b + 2)
                    pool.tensor_tensor(kp[:, u, 1, :], cres, one, ALU.mult).then_inc(k_step.sem, 1)
                    k_step.wait(pool, g, 3 * b + 3)
                    pool.tensor_tensor(kp[:, u, 2, :], cres, kp[:, u, 1, :], ALU.subtract).then_inc(k_ready.sem, 1)

        @block.scalar
        def _(act):
            act.wait_ge(weights.sem, 16 * NW)
            act.wait_ge(consts.sem, NC)
            with act.Fori(0, GROUPS) as g:
                astep.n = 0

                def root(src, signal, count, ready, scale=1.0):
                    signal.wait(act, g, count)
                    astep.did(act.activation(lnv[:, :], src, ACT.Ln, bias=eps[:, 0:1], scale=scale))
                    astep.wait(act, g)

                for c in range(KC):
                    bank = tiles.wait(act, g, ("xt", c))
                    act.activation(xT[:, c, :], bank[:, 0:512], ACT.Copy).then_inc(xT_ready.sem, 1)
                for b in range(GB):
                    bank = tiles.wait(act, g, ("v", b))
                    act.activation(v[:, b, :], bank[:, 0:512], ACT.Copy).then_inc(v_ready.sem, 1)
                for b in range(GB):
                    for i in range(2):
                        bank = tiles.wait(act, g, (("qt", "kt")[i], b))
                        act.activation((qT, kT)[i][:, b], bank[:, 0:512].rearrange("p (c n) -> p c n", c=KC),
                                       ACT.Copy).then_inc(turned.sem, 1)
                for b in range(GB):
                    bank = tiles.wait(act, g, ("a", b))
                    act.activation(sq[:, b], bank[:, 0:512].rearrange("p (c n) -> p c n", c=KC),
                                   ACT.Square).then_inc(squared.sem, 1)
                bank = tiles.wait(act, g, ("ss",))
                astep.did(act.activation(lnv[:, :], bank[:, 0:GB * P].rearrange("p (b n) -> p b n", b=GB)[:, :, 0],
                                         ACT.Ln, bias=eps[:, 0:1], scale=1.0 / D))
                astep.wait(act, g)
                act.activation(rms[:, :], lnv[:, :], ACT.Exp, scale=-0.5).then_inc(rms_ready.sem, 1)

                def norm(i):
                    moments.wait(act, g, i + 1)
                    rms_ready.wait(act, g, 1)
                    rstd_ready.wait(act, g, i)
                    astep.did(act.activation(lnv[:, :], mom[:, :, 1], ACT.Ln, bias=eps[:, 0:1]))
                    astep.wait(act, g)
                    act.activation(rstd[:, :], lnv[:, :], ACT.Exp, scale=-0.5).then_inc(rstd_ready.sem, 1)

                norm(0)

                def parts(b):
                    u = b % 2
                    normed.wait(act, g, b + 1)
                    q_out.wait(act, g, max(b - 1, 0))
                    act.activation(qp[:, u, 0, :], xg[:, b, :], ACT.Copy).then_inc(q_part.sem, 1)
                    q_left.wait(act, g, b + 1)
                    act.activation(qp[:, u, 1, :], qres, ACT.Copy).then_inc(q_part.sem, 1)

                parts(0)
                parts(1)
                for b in range(GB):
                    for h in range(CH):
                        if h == 2 and b + 2 < GB:
                            parts(b + 2)
                        for u in range(2):
                            bank = tiles.wait(act, g, ("e", b, h, u))
                            act.activation(probs[:, h % 2, 2 * u:2 * u + 2, :],
                                           bank[:, :].rearrange("p (l n) -> p l n", l=2), ACT.Exp,
                                           scale=float(CD) ** -0.5).then_inc(exped.sem, 1)
                    pv_done.wait(act, g, b + 1)
                    act.activation(ov, pv[:, :, :], ACT.Copy).then_inc(pv_copied.sem, 1)
                norm(1)
            astep.close("layer 1, scalar")

        @block.tensor
        def _(pe):
            pe.wait_ge(weights.sem, 16 * NW)
            pe.wait_ge(consts.sem, NC)
            with pe.Fori(0, GROUPS) as g:
                x_in.wait(pe, g, 1)
                for c in range(KC):
                    bank = tiles.start(pe, g, ("xt", c))
                    for b in range(GB):
                        ins = pe.transpose(bank[:, b * P:(b + 1) * P], xg[:, b, c * P:(c + 1) * P], ident[:, :])
                    tiles.done(ins)
                for b in range(GB):
                    for kind, w in (("q", wq), ("k", wk), ("v", wv)):
                        bank = tiles.start(pe, g, (kind, b), [(xT_ready, KC)])
                        for c in range(KC):
                            ins = pe.matmul(bank[:, 0:512], xT[:, c, b * P:(b + 1) * P], w[:, c, :],
                                            start=(c == 0), stop=(c == KC - 1))
                        tiles.done(ins)
                for b in range(GB):
                    for i in range(2):
                        bank = tiles.start(pe, g, (("qt", "kt")[i], b), [(rotated, 2 * b + i + 1)])
                        for c in range(KC):
                            ins = pe.transpose(bank[:, c * P:(c + 1) * P], (yq, yk)[i][:, b, c * P:(c + 1) * P],
                                               ident[:, :])
                        tiles.done(ins)

                def attend(b):
                    bank = tiles.start(pe, g, ("a", b), [(masked, KC * (b + 1))])
                    v_ready.wait(pe, g, GB)
                    for c in range(KC):
                        for r in range(HR):
                            at0 = HD * (HR * c + r)
                            ins = pe.matmul(bank[HD * r:HD * r + HD, c * P:(c + 1) * P], v[:, b, at0:at0 + HD],
                                            sm[:, b % 2, c, r, :], start=True, stop=True)
                    tiles.done(ins)

                for b in range(GB):
                    for c in range(KC):
                        bank = tiles.start(pe, g, ("s", b, c), [(spread, b + 1), (turned, 2 * b + 2)])
                        tiles.done(pe.matmul(bank[:, 0:512], kT[:, b, c, :], xz[:, b % 2, c], start=True, stop=True))
                    if b:
                        attend(b - 1)
                attend(GB - 1)
                bank = tiles.start(pe, g, ("ss",))
                for b in range(GB):
                    squared.wait(pe, g, b + 1)
                    for c in range(KC):
                        ins = pe.matmul(bank[:, b * P:(b + 1) * P], sq[:, b, c, :], ones[:, :],
                                        start=(c == 0), stop=(c == KC - 1))
                tiles.done(ins)
                for b in range(GB):
                    bank = tiles.start(pe, g, ("y", b), [(scaled, b + 1)])
                    for c in range(KC):
                        ins = pe.matmul(bank[:, 0:512], at[:, b, c, :], wo[:, c, :],
                                        start=(c == 0), stop=(c == KC - 1))
                    tiles.done(ins)

                def first(b, h):
                    if h == 0:
                        n = len(TERMS) * (b // 2 + 1)
                        qs_in[b % 2].wait(pe, g, n)
                        ks_in[b % 2].wait(pe, g, n)
                    for u in range(2):
                        bank = tiles.start(pe, g, ("p", b, h, u))
                        for i in range(2):
                            at0 = (2 * u + i) * P
                            ins = pe.matmul(bank[:, 512 * i:512 * i + 512], qs[0:TR, b % 2, h, at0:at0 + P],
                                            ks[0:TR, b % 2, h, :], start=True, stop=True)
                        tiles.done(ins)

                def turn_max(b):
                    bank = tiles.start(pe, g, ("mt", b), [(maxed, 2 * CH * (b + 1))])
                    tiles.done(pe.transpose(bank[:, 0:P], mx[:, b % 2, :], ident[:, :]))

                def second(b, h):
                    if h == 0:
                        ms_in[b % 2].wait(pe, g, b // 2 + 1)
                    for u in range(2):
                        bank = tiles.start(pe, g, ("e", b, h, u))
                        for i in range(2):
                            at0 = (2 * u + i) * P
                            ins = pe.matmul(bank[:, 512 * i:512 * i + 512], ks[0:SR, b % 2, h, at0:at0 + P],
                                            qs[0:SR, b % 2, h, :], start=True, stop=True)
                        tiles.done(ins)

                def values(b, h):
                    exped.wait(pe, g, 2 * CH * b + 2 * h + 2)
                    if h == 0:
                        vt_ready.wait(pe, g, 1)
                        pv_copied.wait(pe, g, b)
                    rows = slice(32 * (h // 2), 32 * (h // 2) + 32)
                    for l in range(LC):
                        ins = pe.matmul(pv[rows, h % 2, :], vt[:, l, b, h, :], probs[:, h % 2, l, :],
                                        start=(l == 0), stop=(l == LC - 1))
                    if h == CH - 1:
                        ins.then_inc(pv_done.sem, 1)

                for h in range(CH):
                    first(0, h)
                turn_max(0)
                for b in range(GB):
                    for h in range(CH):
                        second(b, h)
                        if b + 1 < GB:
                            first(b + 1, h)
                        if h:
                            values(b, h - 1)
                    values(b, CH - 1)
                    if b + 1 < GB:
                        turn_max(b + 1)
                    for kind, at0 in (("den", 2), ("ret", 0)):
                        bank = tiles.start(pe, g, (kind, b), [(pv_copied, b + 1)])
                        for o in range(2):
                            ins = pe.matmul(bank[:, 0:512], perm[:, at0 + o, :], ov[:, o, :],
                                            start=(o == 0), stop=(o == 1))
                        tiles.done(ins)

        @block.vector
        def _(dve):
            dve.wait_ge(weights.sem, 16 * NW)
            dve.wait_ge(consts.sem, NC)
            with dve.Fori(0, GROUPS) as g:
                vstep.n = 0

                def chained(ins):
                    vstep.did(ins)
                    vstep.wait(dve, g)

                for b in range(GB):
                    for i in range(2):
                        bank = tiles.wait(dve, g, (("q", "k")[i], b))
                        rotated.wait(dve, g, max(2 * b + i - 1, 0))
                        view = bank[:, 0:512].rearrange("p (h e d) -> p h e d", h=HX, e=2)
                        one = r1[:, i, :].rearrange("p (h d) -> p h d", d=CD)
                        two = r2[:, i, :].rearrange("p (h e d) -> p h e d", h=HX, e=2)
                        dve.tensor_tensor(one, bank[:, 0:512].rearrange("p (h d) -> p h d", d=CD),
                                          cos[:, :].unsqueeze(1).broadcast_to([P, 2 * HX, CD]), ALU.mult)
                        table = sin[:, :].unsqueeze(1).broadcast_to([P, HX, CD])
                        dve.tensor_tensor(two[:, :, 0, :], view[:, :, 1, :], table, ALU.mult)
                        dve.scalar_tensor_tensor(two[:, :, 1, :], view[:, :, 0, :], -1.0, table, ALU.mult,
                                                 ALU.mult).then_inc(rot_parts.sem, 1)

                def scale_out(b):
                    bank = tiles.wait(dve, g, ("a", b))
                    squared.wait(dve, g, b + 1)
                    dve.tensor_tensor(at[:, b], bank[:, 0:512].rearrange("p (c n) -> p c n", c=KC),
                                      rmsw[:, :].unsqueeze(2).broadcast_to([P, KC, P]),
                                      ALU.mult).then_inc(scaled.sem, 1)

                for b in range(GB):
                    for c in range(KC):
                        bank = tiles.wait(dve, g, ("s", b, c))
                        dve.tensor_tensor(sm[:, b % 2, c], bank[:, 0:512].rearrange("p (r n) -> p r n", r=HR),
                                          decay[:, HR * c:HR * c + HR, :], ALU.mult).then_inc(masked.sem, 1)
                    if b:
                        scale_out(b - 1)
                scale_out(GB - 1)
                rms_ready.wait(dve, g, 1)
                for b in range(GB):
                    bank = tiles.wait(dve, g, ("y", b))
                    dve.scalar_tensor_tensor(xg[:, b, :], bank[:, 0:512], rms[:, b:b + 1], xg[:, b, :],
                                             ALU.mult, ALU.add).then_inc(y_added.sem, 1)

                def norm(i, last):
                    last()
                    for b in range(GB):
                        ins = dve.bn_stats(stats[:, b, :], xg[:, b, :])
                    chained(ins)
                    dve.tensor_copy(held[:, 1:2], ones[:, 0:1])
                    for b in range(GB):
                        ins = dve.bn_aggr(mom[:, b, :], stats[:, b, :])
                    ins.then_inc(moments.sem, 1)
                    rstd_ready.wait(dve, g, i + 1)
                    for b in range(GB):
                        dve.tensor_scalar(xg[:, b, :], xg[:, b, :], mom[:, b, 0:1], rstd[:, b:b + 1],
                                          ALU.subtract, ALU.mult).then_inc(normed.sem, 1)

                norm(0, lambda: y_added.wait(dve, g, GB))

                def parts(b):
                    u = b % 2
                    q_ready.wait(dve, g, b)
                    q_part.wait(dve, g, 2 * b + 1)
                    dve.tensor_tensor(qres, xg[:, b, :], qp[:, u, 0, :], ALU.subtract).then_inc(q_left.sem, 1)
                    q_part.wait(dve, g, 2 * b + 2)
                    dve.tensor_tensor(qp[:, u, 2, :], qres, qp[:, u, 1, :], ALU.subtract).then_inc(q_ready.sem, 1)

                def maxima(b, h):
                    for u in range(2):
                        bank = tiles.wait(dve, g, ("p", b, h, u))
                        at0 = LC * h + 2 * u
                        dve.tensor_reduce(mx[:, b % 2, at0:at0 + 2], bank[:, :].rearrange("p (i n) -> p i n", i=2),
                                          AX.X, ALU.max).then_inc(maxed.sem, 1)

                def max_parts(b):
                    u, rows = b % 2, slice(0, CH * LC)
                    bank = tiles.wait(dve, g, ("mt", b))
                    m_out.wait(dve, g, max(b - 1, 0))
                    chained(dve.tensor_scalar(mrow[rows, :], bank[rows, 0:P], -1.0, None, ALU.mult))
                    chained(dve.tensor_copy(mp[rows, u, 0, :], mrow[rows, :]))
                    chained(dve.tensor_tensor(mrow[rows, :], mrow[rows, :], mp[rows, u, 0, :], ALU.subtract))
                    chained(dve.tensor_copy(mp[rows, u, 1, :], mrow[rows, :]))
                    dve.tensor_tensor(mp[rows, u, 2, :], mrow[rows, :], mp[rows, u, 1, :],
                                      ALU.subtract).then_inc(m_ready.sem, 1)

                def finish(b):
                    bank = tiles.wait(dve, g, ("den", b))
                    added.wait(dve, g, b)
                    chained(dve.reciprocal(rec, bank[:, 0:512]))
                    dve.tensor_scalar(rec, rec, gamma[:, 0:1], None, ALU.mult).then_inc(rec_ready.sem, 1)
                    rec_ready.wait(dve, g, b + 1)
                    bank = tiles.wait(dve, g, ("ret", b))
                    chained(dve.tensor_tensor(rec, bank[:, 0:512], rec, ALU.mult))
                    dve.tensor_tensor(xg[:, b, :], xg[:, b, :], rec, ALU.add).then_inc(added.sem, 1)

                parts(0)
                parts(1)
                for h in range(CH):
                    maxima(0, h)
                max_parts(0)
                for b in range(GB):
                    for h in range(CH):
                        if h == 2 and b + 2 < GB:
                            parts(b + 2)
                        if b + 1 < GB:
                            maxima(b + 1, h)
                    if b + 1 < GB:
                        max_parts(b + 1)
                    finish(b)
                norm(1, lambda: added.wait(dve, g, GB))
            vstep.close("layer 1, vector")


def build_experts(nc, t):
    with ExitStack() as ctx:
        def sb(name, shape, dt=F32):
            return ctx.enter_context(nc.sbuf_tensor("d_" + name, shape, dt))

        def signal(name, per, unit=1):
            return Signal(ctx.enter_context(nc.semaphore("d_" + name)), per, unit)

        PAIRS = NE // 2
        NGR, TOPG, TOPK = 4, 2, 4
        EG = NE // NGR
        inner = chunks_of(FI)
        shared = chunks_of(FS)
        NI, NS = len(inner), len(shared)

        banks = [ctx.enter_context(nc.psum_tensor(f"d_bank{i}", [P, 512], F32)) for i in range(BANKS)]
        y = sb("y", [P, SEQS, D])
        xT = sb("xT", [P, KC, SEQS * P])
        w1, w3 = sb("w1", [P, 2, KC, FI]), sb("w3", [P, 2, KC, FI])
        w2 = sb("w2", [P, 2, NI, D])
        ws1, ws3 = sb("ws1", [P, KC, FS]), sb("ws3", [P, KC, FS])
        ws2 = sb("ws2", [P, NS, D])
        ht = sb("ht", [P, 2, NI, GT])
        hs = sb("hs", [P, NS, GT])
        gated = sb("gated", [P, 2, GT])
        wg = sb("wg", [P, KC, NE])
        iota, ident = sb("iota", [P, NE]), sb("ident", [P, P])
        eps, held = sb("eps", [P, 1]), sb("held", [P, 2])
        pr = sb("pr", [P, SEQS, NE])
        sel = sb("sel", [P, SEQS, NE])
        comb = sb("comb", [P, SEQS, NE])
        part = sb("part", [P, 2, SEQS])
        rmx = sb("rmx", [P, SEQS])
        grp = sb("grp", [P, SEQS, 8])
        top, topf = sb("top", [P, SEQS, 8]), sb("topf", [P, SEQS, 8])
        topi = sb("topi", [P, SEQS, 8], U32)
        eq = sb("eq", [P, SEQS, NE])
        stats, mom, rstd = sb("stats", [P, SEQS, 6]), sb("mom", [P, SEQS, 2]), sb("rstd", [P, SEQS])

        loaded = [signal(f"loaded{g}", 0, 16) for g in range(GROUPS)]
        weights, consts = signal("weights", 0, 16), signal("consts", 0)
        shared_in = signal("shared_in", 0, 16)
        expert_in = [signal(f"expert_in{u}", 3, 16) for u in range(2)]
        xT_ready, rt_shift, rt_exp, routed = (signal(n, 0) for n in ("xT_ready", "rt_shift", "rt_exp", "routed"))
        s_gated, s_h, s_added = (signal("s_" + n, 0) for n in ("gated", "h", "added"))
        moments, rstd_ready, normed = (signal(n, 0) for n in ("moments", "rstd_ready", "normed"))
        stored = signal("stored", 0, 16)
        UNITS = 2 * GROUPS
        silued, h_ready, y_added = signal("silued", UNITS * NI), signal("h_ready", UNITS * NI), signal("y_added", UNITS * GB)
        part_ready = signal("part_ready", 1)

        order = [("xt", b) for b in range(SEQS)] + [("rt",)]
        for g in range(GROUPS):
            order += [(kind, g, c) for c in range(NS) for kind in ("sg", "su")]
            order += [("sy", g, b) for b in range(GB)]

        def drained(key):
            kind, *n = key
            return {
                "xt": lambda: (xT_ready, n[0] + 1),
                "rt": lambda: (rt_shift, 1),
                "sg": lambda: (s_gated, NS * n[0] + n[1] + 1),
                "su": lambda: (s_h, NS * n[0] + n[1] + 1),
                "sy": lambda: (s_added, GB * n[0] + n[1] + 1),
            }[kind]()

        first = Tiles(banks, ctx.enter_context(nc.semaphore("d_filled")), order, drained)

        units = [(u, g) for u in range(2) for g in range(GROUPS)]
        order = []
        for n in range(UNITS + 1):
            if n < UNITS:
                order += [(kind, n, c) for c in range(NI) for kind in ("g", "u")]
            if n:
                order += [("y", n - 1, b) for b in range(GB)]

        def drained2(key):
            kind, *n = key
            return {
                "g": lambda: (silued, NI * n[0] + n[1] + 1),
                "u": lambda: (h_ready, NI * n[0] + n[1] + 1),
                "y": lambda: (y_added, GB * n[0] + n[1] + 1),
            }[kind]()

        second = Tiles(banks, ctx.enter_context(nc.semaphore("d_filled2")), order, drained2)
        vstep = Steps(ctx.enter_context(nc.semaphore("d_vector_step")), 0)
        astep = Steps(ctx.enter_context(nc.semaphore("d_scalar_step")), 0)
        block = ctx.enter_context(nc.Block())

        @block.sync
        def _(sp):
            sp.dma_start(ident[:], t["ident"]).then_inc(weights.sem, 16)
            for g in range(GROUPS):
                sp.dma_start(y[:, GB * g:GB * (g + 1), :], t["x5"][g]).then_inc(loaded[g].sem, 16)
            sp.dma_start(wg[:], t["wg1"]).then_inc(weights.sem, 16)
            sp.dma_start(iota[:], t["iota1"]).then_inc(weights.sem, 16)
            for dst, src in ((ws1, "ws1"), (ws3, "ws3")):
                sp.dma_start(dst[:], t[src]).then_inc(shared_in.sem, 16)
            sp.dma_start(ws2[:], t["ws2"]).then_inc(shared_in.sem, 16)
            with sp.Fori(0, PAIRS) as i:
                for u in range(2):
                    y_added.wait(sp, i, 0)
                    sp.dma_start(w1[:, u], t["w11"][2 * i + u]).then_inc(expert_in[u].sem, 16)
                    sp.dma_start(w3[:, u], t["w31"][2 * i + u]).then_inc(expert_in[u].sem, 16)
                    sp.dma_start(w2[:, u], t["w21"][2 * i + u]).then_inc(expert_in[u].sem, 16)
            for b in range(SEQS):
                sp.wait_ge(normed.sem, b + 1)
                sp.dma_start(t["out"][b], y[:, b, :]).then_inc(stored.sem, 16)
            sp.wait_ge(stored.sem, 16 * SEQS)

        @block.gpsimd
        def _(pool):
            pool.memset(eps[:], EPS_LN).then_inc(consts.sem, 1)
            pool.memset(held[:], 0.0).then_inc(consts.sem, 1)
            pool.memset(hs[:], 0.0).then_inc(consts.sem, 1)
            pool.memset(grp[:], -1.0).then_inc(consts.sem, 1)

        @block.scalar
        def _(act):
            act.wait_ge(consts.sem, 4)
            for b in range(SEQS):
                bank = first.wait(act, 0, ("xt", b))
                act.activation(xT[:, :, b * P:(b + 1) * P], bank[:, :].rearrange("p (c n) -> p c n", c=KC),
                               ACT.Copy).then_inc(xT_ready.sem, 1)
            act.wait_ge(rt_shift.sem, 1)
            act.activation(pr[:], pr[:], ACT.Exp).then_inc(rt_exp.sem, 1)
            for g in range(GROUPS):
                for c, (_, m) in enumerate(shared):
                    n = NS * g + c
                    bank = first.wait(act, 0, ("sg", g, c))
                    if n >= 2:
                        act.wait_ge(s_h.sem, n - 1)
                    act.activation(gated[0:m, n % 2, :], bank[0:m, :], ACT.Silu).then_inc(s_gated.sem, 1)
            act.wait_ge(s_h.sem, NS * GROUPS)
            with act.Fori(0, PAIRS) as i:
                for n in range(UNITS):
                    for c, (_, m) in enumerate(inner):
                        k = NI * n + c
                        bank = second.wait(act, i, ("g", n, c))
                        h_ready.wait(act, i, max(k - 1, 0))
                        act.activation(gated[0:m, k % 2, :], bank[0:m, :], ACT.Silu).then_inc(silued.sem, 1)
            act.wait_ge(moments.sem, 1)
            act.activation(rstd[:, :], mom[:, :, 1], ACT.Ln, bias=eps[:, 0:1]).then_inc(rstd_ready.sem, 1)
            act.wait_ge(rstd_ready.sem, 1)
            act.activation(rstd[:, :], rstd[:, :], ACT.Exp, scale=-0.5).then_inc(rstd_ready.sem, 1)

        @block.tensor
        def _(pe):
            def up(tiles, turn, kind, key, w, width, group, needs=()):
                bank = tiles.start(pe, turn, (kind, *key), needs)
                c0, m = width
                for c in range(KC):
                    ins = pe.matmul(bank[0:m, :], w[:, c, c0:c0 + m], xT[:, c, GT * group:GT * (group + 1)],
                                    start=(c == 0), stop=(c == KC - 1))
                tiles.done(ins)

            pe.wait_ge(weights.sem, 48)
            for b in range(SEQS):
                if b % GB == 0:
                    pe.wait_ge(loaded[b // GB].sem, 16)
                bank = first.start(pe, 0, ("xt", b))
                for c in range(KC):
                    ins = pe.transpose(bank[:, c * P:(c + 1) * P], y[:, b, c * P:(c + 1) * P], ident[:, :])
                first.done(ins)
            bank = first.start(pe, 0, ("rt",), [(xT_ready, SEQS)])
            for b in range(SEQS):
                for c in range(KC):
                    ins = pe.matmul(bank[:, b * NE:(b + 1) * NE], xT[:, c, b * P:(b + 1) * P], wg[:, c, :],
                                    start=(c == 0), stop=(c == KC - 1))
            first.done(ins)
            pe.wait_ge(shared_in.sem, 48)
            pe.wait_ge(consts.sem, 4)
            for g in range(GROUPS):
                for c in range(NS):
                    up(first, 0, "sg", (g, c), ws1, shared[c], g)
                    up(first, 0, "su", (g, c), ws3, shared[c], g)
                for b in range(GB):
                    bank = first.start(pe, 0, ("sy", g, b), [(s_h, NS * (g + 1))])
                    for c in range(NS):
                        ins = pe.matmul(bank[:, :], hs[:, c, b * P:(b + 1) * P], ws2[:, c, :],
                                        start=(c == 0), stop=(c == NS - 1))
                    first.done(ins)
            pe.wait_ge(s_added.sem, GB * GROUPS)
            with pe.Fori(0, PAIRS) as i:
                def down(n):
                    u, g = units[n]
                    for b in range(GB):
                        bank = second.start(pe, i, ("y", n, b), [(h_ready, NI * (n + 1))])
                        for c, (_, m) in enumerate(inner):
                            ins = pe.matmul(bank[:, :], ht[0:m, n % 2, c, b * P:(b + 1) * P], w2[0:m, u, c, :],
                                            start=(c == 0), stop=(c == NI - 1))
                        second.done(ins)

                for n, (u, g) in enumerate(units):
                    if g == 0:
                        expert_in[u].wait(pe, i, 3)
                    for c in range(NI):
                        up(second, i, "g", (n, c), w1[:, u], inner[c], g)
                        up(second, i, "u", (n, c), w3[:, u], inner[c], g)
                    if n:
                        down(n - 1)
                down(UNITS - 1)

        @block.vector
        def _(dve):
            dve.wait_ge(consts.sem, 4)
            dve.wait_ge(weights.sem, 48)

            def chained(ins):
                vstep.did(ins)
                vstep.wait(dve, 0)

            def wide(ap, n=NE):
                return ap.unsqueeze(2).broadcast_to([P, SEQS, n])

            bank = first.wait(dve, 0, ("rt",))
            logits = bank[:, 0:SEQS * NE].rearrange("p (b e) -> p b e", b=SEQS)
            chained(dve.tensor_reduce(rmx[:, :], logits, AX.X, ALU.max))
            dve.tensor_tensor(pr[:], logits, wide(rmx[:, :]), ALU.subtract).then_inc(rt_shift.sem, 1)
            dve.wait_ge(rt_exp.sem, 1)
            chained(dve.tensor_reduce(rmx[:, :], pr[:], AX.X, ALU.add))
            chained(dve.reciprocal(rmx[:, :], rmx[:, :]))
            chained(dve.tensor_tensor(pr[:], pr[:], wide(rmx[:, :]), ALU.mult))

            def chosen(out, src, width, count):
                for b in range(SEQS):
                    ins = dve.max(top[:, b, :], src[:, b, :])
                chained(ins)
                for b in range(SEQS):
                    ins = dve.max_index(topi[:, b, :], top[:, b, :], src[:, b, :])
                chained(ins)
                chained(dve.tensor_copy(topf[:], topi[:]))
                for k in range(count):
                    into = out if k == 0 else eq[:, :, 0:width]
                    chained(dve.tensor_tensor(into, iota[:, 0:width].unsqueeze(1).broadcast_to([P, SEQS, width]),
                                              wide(topf[:, :, k], width), ALU.is_equal))
                    if k:
                        chained(dve.tensor_tensor(out, out, eq[:, :, 0:width], ALU.add))

            chained(dve.tensor_reduce(grp[:, :, 0:NGR], pr[:].rearrange("p b (g e) -> p b g e", e=EG), AX.X, ALU.max))
            chosen(sel[:, :, 0:NGR], grp[:], NGR, TOPG)
            mask = sel[:, :, 0:NGR]
            chained(dve.tensor_tensor(comb[:].rearrange("p b (g e) -> p b g e", e=EG),
                                      pr[:].rearrange("p b (g e) -> p b g e", e=EG),
                                      mask.unsqueeze(3).broadcast_to([P, SEQS, NGR, EG]), ALU.mult))
            chained(dve.tensor_scalar(grp[:, :, 0:NGR], mask, 1.0, None, ALU.subtract))
            chained(dve.tensor_tensor(comb[:].rearrange("p b (g e) -> p b g e", e=EG),
                                      comb[:].rearrange("p b (g e) -> p b g e", e=EG),
                                      grp[:, :, 0:NGR].unsqueeze(3).broadcast_to([P, SEQS, NGR, EG]), ALU.add))
            chosen(sel[:], comb[:], NE, TOPK)
            chained(dve.tensor_tensor(comb[:], pr[:], sel[:], ALU.mult))

            for g in range(GROUPS):
                for c, (_, m) in enumerate(shared):
                    n = NS * g + c
                    bank = first.wait(dve, 0, ("su", g, c))
                    dve.wait_ge(s_gated.sem, n + 1)
                    dve.tensor_tensor(hs[0:m, c, :], bank[0:m, :], gated[0:m, n % 2, :], ALU.mult).then_inc(s_h.sem, 1)
                for b in range(GB):
                    bank = first.wait(dve, 0, ("sy", g, b))
                    dve.tensor_tensor(y[:, GB * g + b, :], bank[:, :], y[:, GB * g + b, :],
                                      ALU.add).then_inc(s_added.sem, 1)
            dve.wait_ge(s_added.sem, SEQS)
            with dve.Fori(0, PAIRS) as i:
                def take(n):
                    u, g = units[n]
                    for b in range(GB):
                        s = GB * g + b
                        bank = second.wait(dve, i, ("y", n, b))
                        y_added.wait(dve, i, max(GB * (n - GROUPS) + b + 1, 0))
                        dve.scalar_tensor_tensor(y[:, s, :], bank[:, :], part[:, u, s:s + 1], y[:, s, :],
                                                 ALU.mult, ALU.add).then_inc(y_added.sem, 1)

                y_added.wait(dve, i, 0)
                dve.tensor_copy(part[:, :, :], comb[:, :, bass.ds(2 * i, 2)].rearrange("p b u -> p u b"))\
                    .then_inc(part_ready.sem, 1)
                part_ready.wait(dve, i, 1)
                for n in range(UNITS):
                    for c, (_, m) in enumerate(inner):
                        k = NI * n + c
                        bank = second.wait(dve, i, ("u", n, c))
                        silued.wait(dve, i, k + 1)
                        dve.tensor_tensor(ht[0:m, n % 2, c, :], bank[0:m, :], gated[0:m, k % 2, :],
                                          ALU.mult).then_inc(h_ready.sem, 1)
                    if n:
                        take(n - 1)
                take(UNITS - 1)
            dve.wait_ge(y_added.sem, PAIRS * UNITS * GB)
            for b in range(SEQS):
                ins = dve.bn_stats(stats[:, b, :], y[:, b, :])
            chained(ins)
            for b in range(SEQS):
                ins = dve.bn_aggr(mom[:, b, :], stats[:, b, :])
            ins.then_inc(moments.sem, 1)
            dve.wait_ge(rstd_ready.sem, 2)
            for b in range(SEQS):
                dve.tensor_scalar(y[:, b, :], y[:, b, :], mom[:, b, 0:1], rstd[:, b:b + 1],
                                  ALU.subtract, ALU.mult).then_inc(normed.sem, 1)


def build_program(nc, t):
    t = dict(t)
    scratch = (("x3", [GROUPS, P, GB, D], F32), ("pre", [GROUPS, E0, D], F32), ("fsum", [E0, D], F32),
               ("x5", [GROUPS, P, GB, D], F32), ("kpark", [2, P, 3, D], BF16), ("qpark", [2, P, 3, D], BF16),
               ("mpark", [2, 3, CH * D], BF16))
    for name, shape, dt in scratch:
        t[name] = nc.dram_tensor("scratch_" + name, shape, dt, kind="Internal").ap()
    build_layer0(nc, t)
    build_row_fix(nc, t)
    build_layer1(nc, t)
    build_experts(nc, t)


def chunks_of(n):
    return [(a, min(P, n - a)) for a in range(0, n, P)]


def by_group(a):
    return np.ascontiguousarray(a.reshape(GROUPS, GB, P, D).transpose(0, 2, 1, 3))


def by_feature(a):
    return np.ascontiguousarray(a.reshape(GROUPS, GT, KC, P).transpose(0, 3, 2, 1))


def rows_of(a):
    return np.ascontiguousarray(a.reshape(-1, P, a.shape[-1]).transpose(1, 0, 2))


def constants():
    t = {}
    f = np.float32
    inv = (1.0 / f(10000.0) ** (np.arange(0, P, 2, dtype=f) / f(P))).astype(f)
    angle = np.outer(inv, np.arange(P, dtype=f)).astype(f)
    t["cos0"] = np.concatenate([np.cos(angle), np.cos(angle)]).astype(f)
    t["sin0"] = np.concatenate([np.sin(angle), -np.sin(angle)]).astype(f)
    k, q = np.arange(P)[:, None], np.arange(P)[None, :]
    t["causal"] = (q >= k).astype(f)
    t["barred"] = np.where(q >= k, 0.0, BIG).astype(f)
    t["ident"] = np.eye(P, dtype=f)
    sel = np.zeros((P, HX, P), f)
    sel[64 + np.arange(HX), np.arange(HX)] = 1
    t["sel"] = sel
    t["iota"] = np.broadcast_to(np.arange(E0, dtype=f), (P, E0)).copy()
    t["iota1"] = np.broadcast_to(np.arange(NE, dtype=f), (P, NE)).copy()
    freq = np.concatenate([f(1 / 1024.0) ** np.linspace(0, 1, HD // 4, dtype=f), np.zeros(HD // 4, f)]).astype(f)
    theta = (np.arange(P, dtype=f)[:, None] * freq[None, :]).astype(f)
    t["cos1"], t["sin1"] = np.cos(theta).astype(f), np.sin(theta).astype(f)
    first = 2.0 ** (-2.0 ** (-(np.log2(HX) - 3)))
    slopes = np.array([first * first ** i for i in range(HX)])
    dist = (q - k)[:, None, :]
    t["decay1"] = np.where(dist >= 0, np.exp(-slopes[None, :, None] * np.maximum(dist, 0)), 0.0).astype(f)
    perm = np.zeros((P, 4, P), f)
    for j in range(4):
        for d in range(CD):
            for odd in range(2):
                perm[32 * j + d, odd, 32 * j + CD * odd + d] = 1
                perm[32 * j + CD, 2 + odd, 32 * j + CD * odd + d] = 1
    t["perm"] = perm
    return t


def tables(i):
    t = constants()
    a = {k: np.asarray(v) for k, v in i.items()}
    t["x"], t["xT"] = by_group(a["x"]), by_feature(a["x"])
    t["c"], t["cT"] = by_group(a["ctx_2048"]), by_feature(a["ctx_2048"])
    t["wk0"], t["wv0"] = (rows_of(a["L0_attn_" + n].T) for n in ("Wk", "Wv"))
    t["wq0"] = np.stack([rows_of(w) for w in np.split(a["L0_attn_Wq"].T, KV0, axis=1)])
    t["wo0"] = np.stack([rows_of(w) for w in np.split(a["L0_attn_Wo"].T, KV0, axis=0)])
    t["wi0"], t["wf0"] = rows_of(a["L0_xattn_Wi"]), rows_of(a["L0_xattn_Wf"])
    bias = np.zeros((P, 2), np.float32)
    bias[0:HX, 0], bias[32:32 + HX, 0] = a["L0_xattn_bi"], a["L0_xattn_bf"]
    t["bias0"] = bias
    t["lnw0"] = np.broadcast_to(a["L0_xattn_ln_scale"], (P, D)).copy()
    t["w10"], t["w30"], t["w20"] = (rows_of(a["L0_ffn_" + n].T) for n in ("w1", "w3", "w2"))
    t["wr0"] = rows_of(a["L0_ffn_wr"].T)
    for n in ("q", "k", "v", "o"):
        t[f"w{n}1"] = rows_of(a[f"L1_attn_W{n}"])
    t["rms1"] = np.ascontiguousarray(a["L1_attn_rms_w"].reshape(KC, P).T)
    t["gamma1"] = np.broadcast_to(a["L1_xattn_gamma"], (P, 1)).copy()
    t["wg1"] = rows_of(a["L1_ffn_Wg"].T)
    t["w11"], t["w31"] = (np.stack([rows_of(w.T) for w in a["L1_ffn_" + n]]) for n in ("W1", "W3"))
    t["ws1"], t["ws3"] = (rows_of(a["L1_ffn_" + n].T) for n in ("Ws1", "Ws3"))

    def padded(w):
        return rows_of(np.concatenate([w.T, np.zeros((-w.shape[1] % P, D), w.dtype)]))

    t["w21"] = np.stack([padded(w) for w in a["L1_ffn_W2"]])
    t["ws2"] = padded(a["L1_ffn_Ws2"])
    return t


def kernel(**inputs):
    import concourse.bacc as bacc
    from concourse.bass_utils import run_bass_kernel_spmd

    nc = bacc.Bacc("TRN2", target_bir_lowering=False, num_devices=1)
    arrays, t = {}, {}
    for name, a in tables(inputs).items():
        arrays[f"in_{name}"] = a
        t[name] = nc.dram_tensor(f"in_{name}", a.shape, mybir.dt.from_np(a.dtype), kind="ExternalInput").ap()
    t["out"] = nc.dram_tensor("out_x", [SEQS, P, D], F32, kind="ExternalOutput").ap()
    build_program(nc, t)
    result = run_bass_kernel_spmd(nc, [arrays], core_ids=[0])
    return result.results[0]["out_x"]
```

```python
from contextlib import ExitStack

import numpy as np

import concourse.bass as bass
from concourse import mybir

F32 = mybir.dt.float32
BF16 = mybir.dt.bfloat16
U32 = mybir.dt.uint32
I32 = mybir.dt.int32
ALU = mybir.AluOpType
ACT = mybir.ActivationFunctionType
AX = mybir.AxisListType

P = 128
SEQS = 16
D = 512
KC = D // P
GROUPS = 4
GB = SEQS // GROUPS
GT = GB * P
BANKS = 8

H0 = 16
KV0 = 4
REP = H0 // KV0
HX = 16
HD = 32
HR = P // HD
VS = HD + 1
EPS_DEN = 1e-6
EPS_LN = 1e-5
EPS_MLSTM = 1e-6
BIG = 1e30

E0 = 8
NE = 16
FI = 352
FS = 704
CH = 8
CD = P // CH


class Signal:

    def __init__(self, sem, per=0, unit=1):
        self.sem, self.per, self.unit = sem, per * unit, unit

    def wait(self, eng, turn, count):
        value = turn * self.per + count * self.unit
        if not (isinstance(value, int) and value == 0):
            eng.wait_ge(self.sem, value)


class Steps:

    def __init__(self, sem, per):
        self.sem, self.per, self.n = sem, per, 0

    def did(self, ins):
        self.n += 1
        ins.then_inc(self.sem, 1)

    def wait(self, eng, turn):
        eng.wait_ge(self.sem, turn * self.per + self.n)

    def close(self, name):
        if self.n != self.per:
            raise ValueError(f"{name}: {self.n} steps")


class Tiles:

    def __init__(self, banks, filled, order, drained):
        self.banks, self.order, self.drained = banks, order, drained
        self.at = {key: n for n, key in enumerate(order)}
        self.filled = Signal(filled, len(order))
        self.slots = -(-len(order) // len(banks)) * len(banks)

    def bank(self, key):
        return self.banks[self.at[key] % len(self.banks)]

    def start(self, pe, turn, key, needs=()):
        n = self.at[key] - len(self.banks)
        if n >= 0:
            sig, count = self.drained(self.order[n])
        elif isinstance(turn, int):
            sig, count = None, 0
        else:
            n += self.slots
            n = n if n < len(self.order) else n - len(self.banks)
            sig, count = self.drained(self.order[n])[0], 0
        needs = list(needs)
        if sig and not any(s is sig and c >= count for s, c in needs):
            needs = [(s, c) for s, c in needs if s is not sig] + [(sig, count)]
        for s, c in needs:
            s.wait(pe, turn, c)
        return self.bank(key)

    def done(self, ins):
        ins.then_inc(self.filled.sem, 1)

    def wait(self, eng, turn, key):
        self.filled.wait(eng, turn, self.at[key] + 1)
        return self.bank(key)


def build_layer0(nc, t):
    with ExitStack() as ctx:
        def sb(name, shape, dt=F32):
            return ctx.enter_context(nc.sbuf_tensor("a_" + name, shape, dt))

        def signal(name, per, unit=1):
            return Signal(ctx.enter_context(nc.semaphore("a_" + name)), per, unit)

        banks = [ctx.enter_context(nc.psum_tensor(f"a_bank{i}", [P, 512], F32)) for i in range(BANKS)]

        wq = sb("wq", [P, 2, KC, D])
        wk = sb("wk", [P, KC, KV0 * P])
        wv = sb("wv", [P, KC, KV0 * P])
        wo = sb("wo", [P, 2, REP, D])
        w1, w3 = wq[:, 0], wq[:, 1]
        wr = sb("wr", [P, KC, E0])
        wi = sb("wi", [P, 3 * KC, HX])
        wf = sb("wf", [P, 3 * KC, HX])
        bias = sb("bias", [P, 2])
        lnw = sb("lnw", [P, D])
        cos = sb("cos", [P, P])
        sin = sb("sin", [P, P])
        causal = sb("causal", [P, P])
        barred = sb("barred", [P, P])
        ident = sb("ident", [P, P])
        sel = sb("sel", [P, HX, P])
        iota = sb("iota", [P, E0])
        ones = sb("ones", [P, P])

        xg = sb("xg", [P, GB, D])
        xT = sb("xT", [P, KC, GT])
        cT = sb("cT", [P, KC, GT])
        scratch = sb("scratch", [P, 10240])
        kf = scratch[:, 0:2048].rearrange("p (j t) -> p j t", j=KV0)
        v = scratch[:, 2048:4096].rearrange("p (b t) -> p b t", b=GB)
        qf = scratch[:, 4096:8192].rearrange("p (u r t) -> p u r t", u=2, r=REP)
        st = scratch[:, 8192:10240].rearrange("p (b t) -> p b t", b=GB)
        scratch2 = sb("scratch2", [P, 8192])
        ot = scratch2[:, 0:2048].rearrange("p (b r t) -> p b r t", b=GB, r=REP)
        rt1 = scratch2[:, 2048:3072].rearrange("p (u t) -> p u t", u=2)
        rt2 = scratch2[:, 3072:4096].rearrange("p (u t) -> p u t", u=2)
        ry = scratch2[:, 4096:5120].rearrange("p (u t) -> p u t", u=2)
        ee = scratch2[:, 5120:6144].rearrange("p (u t) -> p u t", u=2)
        dn = scratch2[:, 7168:8192].rearrange("p (u t) -> p u t", u=2)
        xz = sb("xz", [P, 2, GB, HR, P])
        dec = scratch[:, 0:4096].rearrange("p (u r b s) -> p u r b s", u=2, r=HR, b=GB)
        cc = scratch[:, 4096:8192].rearrange("p (u b r s) -> p u b r s", u=2, b=GB, r=HR)
        hv = scratch[:, 8192:10240].rearrange("p (n e) -> p n e", e=HD)
        hc = scratch2[:, 0:2048].rearrange("p (n e) -> p n e", e=HD)
        hs = scratch2[:, 2048:4096].rearrange("p (n e) -> p n e", e=HD)
        ho = scratch2[:, 4096:4096 + GB * HX * VS].rearrange("p (b h e) -> p b h e", b=GB, h=HX)
        va = sb("va", [P, GB * HX * VS + P - VS])
        ga = sb("ga", [P, GT])
        gi, gf, g1, g2 = (scratch[0:HX, 8192 + GT * n:8192 + GT * (n + 1)] for n in range(4))
        g3 = scratch2[0:HX, 0:GT]
        am = sb("am", [P, GB, 48])
        em = sb("em", [P, GB, HX])
        hn = sb("hn", [P, GB * HX])
        hm = sb("hm", [P, GB * HX])
        h1 = scratch[:, 0:2048].rearrange("p (c t) -> p c t", c=KC)
        h2 = scratch[:, 2048:4096].rearrange("p (b t) -> p b t", b=GB)
        se = scratch2[:, 0:1024].rearrange("p (u t) -> p u t", u=2)
        sr = scratch2[:, 1024:1536]
        pr = sb("pr", [P, GB, E0])
        rmx = sb("rmx", [P, GB])
        top = sb("top", [P, GB, 8])
        topi = sb("topi", [P, GB, 8], U32)
        topf = sb("topf", [P, GB, 8])
        eq = sb("eq", [P, 2, E0])
        gate = sb("gate", [P, GB, E0])
        fsum = sb("fsum", [E0, D])
        pre = sb("pre", [E0, D])
        stats = sb("stats", [P, GB, 6])
        mom = sb("mom", [P, GB, 2])
        lnv = sb("lnv", [P, GB])
        rstd = sb("rstd", [P, GB])
        eps = sb("eps", [P, 2])
        held = sb("held", [P, 2])

        NF = KV0 + H0
        weights = signal("weights", 0, 16)
        NW = 13
        wq_in = [signal(f"wq_in{u}", KV0 // 2 + 1, 16) for u in range(2)]
        wo_in = [signal(f"wo_in{u}", KV0 // 2, 16) for u in range(2)]
        x_in, xT_in, c_in, cT_in = (signal(n, 1, 16) for n in ("x_in", "xT_in", "c_in", "cT_in"))
        consts = signal("consts", 0)
        wsum = signal("wsum", 0)
        rope_parts, rope_sum = signal("rope_parts", NF), signal("rope_sum", NF)
        elu_parts, feature = signal("elu_parts", NF), signal("feature", NF)
        v_ready = signal("v_ready", GB)
        masked, den_copied = signal("masked", KV0 * GB), signal("den_copied", KV0 * GB)
        o_scaled, y_added = signal("o_scaled", KV0 * GB), signal("y_added", KV0 * GB)
        moments, rstd_ready, normed = signal("moments", 3), signal("rstd_ready", 3), signal("normed", 3 * GB)
        xT_ready = signal("xT_ready", 2 * KC)
        xz_spread, xz_ready = signal("xz_spread", KC * (HR - 1)), signal("xz_ready", KC)
        gates_copied, gate_abs, gate_log = signal("gates_copied", 1), signal("gate_abs", 1), signal("gate_log", 1)
        gates_ready, gt_copied = signal("gates_ready", 1), signal("gt_copied", 1)
        em_ready = signal("em_ready", 1)
        decay_arg, decay = signal("decay_arg", HX), signal("decay", HX)
        c_ready, ho_ready = signal("c_ready", KC * GB), signal("ho_ready", KC * GB)
        h_centred, h_squared, h_rstd = signal("h_centred", 1), signal("h_squared", 1), signal("h_rstd", 1)
        h_var = signal("h_var", 1)
        rt_shift, rt_exp, routed = signal("rt_shift", 1), signal("rt_exp", 1), signal("routed", 1)
        h_exp, h_ready = signal("h_exp", KC + GB), signal("h_ready", KC + GB)
        f_added, pre_ready = signal("f_added", 1), signal("pre_ready", 1)
        stored = signal("stored", 2, 16)
        fstored = signal("fstored", 0, 16)

        order = [("k", j) for j in range(KV0)] + [("v", b) for b in range(GB)]
        order += [("q", r) for r in range(REP)]
        for j in range(KV0):
            if j + 1 < KV0:
                order += [("q", REP * (j + 1) + r) for r in range(REP)]
            order += [("s", j, b) for b in range(GB)]
            if j:
                order += [("y", j - 1, b) for b in range(GB)]
            order += [(kind, j, b) for b in range(GB) for kind in ("d", "o")]
        order += [("y", KV0 - 1, b) for b in range(GB)]
        order += [("xt", 0, c) for c in range(KC)] + [("gate",), ("gt",)]
        order += [("cb", h) for h in range(HR)]
        for c in range(KC):
            if c + 1 < KC:
                order += [("cb", HR * (c + 1) + r) for r in range(HR)]
            order += [("qk", c, b) for b in range(GB)]
            if c:
                order += [("ho", c - 1, b) for b in range(GB)]
        order += [("ho", KC - 1, b) for b in range(GB)]
        order += [("xt", 1, c) for c in range(KC)] + [("rt",)]
        order += [("f1", c) for c in range(KC)] + [("f2", b) for b in range(GB)] + [("fa",)]

        def drained(key):
            kind, *n = key
            return {
                "k": lambda: (rope_parts, n[0] + 1),
                "v": lambda: (v_ready, n[0] + 1),
                "q": lambda: (rope_parts, KV0 + n[0] + 1),
                "s": lambda: (masked, GB * n[0] + n[1] + 1),
                "d": lambda: (den_copied, GB * n[0] + n[1] + 1),
                "o": lambda: (o_scaled, GB * n[0] + n[1] + 1),
                "y": lambda: (y_added, GB * n[0] + n[1] + 1),
                "xt": lambda: (xT_ready, KC * n[0] + n[1] + 1),
                "gate": lambda: (gates_copied, 1),
                "gt": lambda: (gt_copied, 1),
                "cb": lambda: (decay_arg, n[0] + 1),
                "qk": lambda: (c_ready, GB * n[0] + n[1] + 1),
                "ho": lambda: (ho_ready, GB * n[0] + n[1] + 1),
                "rt": lambda: (rt_shift, 1),
                "f1": lambda: (h_ready, n[0] + 1),
                "f2": lambda: (h_ready, KC + n[0] + 1),
                "fa": lambda: (f_added, 1),
            }[kind]()

        tiles = Tiles(banks, ctx.enter_context(nc.semaphore("a_filled")), order, drained)
        vstep = Steps(ctx.enter_context(nc.semaphore("a_vector_step")), 68)
        astep = Steps(ctx.enter_context(nc.semaphore("a_scalar_step")), 25)
        block = ctx.enter_context(nc.Block())

        def by_batch(ap):
            return ap.unsqueeze(1).broadcast_to([ap.shape[0], GB, P])

        @block.sync
        def _(sp):
            for dst, src in ((wk, "wk0"), (cos, "cos0"), (sin, "sin0"), (wv, "wv0"), (causal, "causal"),
                             (wi, "wi0"), (wf, "wf0"), (barred, "barred"), (sel, "sel"), (lnw, "lnw0"),
                             (wr, "wr0"), (iota, "iota"), (bias, "bias0")):
                sp.dma_start(dst[:], t[src]).then_inc(weights.sem, 16)
            sp.wait_ge(consts.sem, 10)
            with sp.Fori(0, GROUPS) as g:
                h_ready.wait(sp, g, 0)
                sp.dma_start(xT[:, :, :], t["xT"][g]).then_inc(xT_in.sem, 16)
                for j in range(2):
                    sp.dma_start(wq[:, j], t["wq0"][j]).then_inc(wq_in[j].sem, 16)
                    sp.dma_start(wo[:, j], t["wo0"][j]).then_inc(wo_in[j].sem, 16)
                sp.dma_start(cT[:, :, :], t["cT"][g]).then_inc(cT_in.sem, 16)
                sp.dma_start(va[:, 0:GB * HX * VS].rearrange("p (n e) -> p n e", e=VS)[:, :, 0:HD],
                             t["c"][g].rearrange("p b (h e) -> p (b h) e", e=HD)).then_inc(c_in.sem, 16)
                stored.wait(sp, g, 0)
                sp.dma_start(xg[:, :, :], t["x"][g]).then_inc(x_in.sem, 16)
                for j in range(2, KV0 + 2):
                    feature.wait(sp, g, KV0 + REP * (j - 1))
                    src = t["wq0"][j] if j < KV0 else t[("w10", "w30")[j - KV0]]
                    sp.dma_start(wq[:, j % 2], src).then_inc(wq_in[j % 2].sem, 16)
                    if j < KV0:
                        y_added.wait(sp, g, GB * (j - 1))
                        sp.dma_start(wo[:, j % 2], t["wo0"][j]).then_inc(wo_in[j % 2].sem, 16)
            f_added.wait(sp, GROUPS, 0)
            sp.dma_start(t["fsum"], fsum[:, :]).then_inc(fstored.sem, 16)
            sp.wait_ge(fstored.sem, 16)
            sp.wait_ge(stored.sem, 2 * 16 * GROUPS)

        @block.gpsimd
        def _(pool):
            pool.memset(ident[:, :], 0.0).then_inc(consts.sem, 1)
            pool.memset(ones[:, :], 1.0).then_inc(consts.sem, 1)
            pool.memset(xz[:], 0.0).then_inc(consts.sem, 1)
            pool.memset(va[:], 1.0).then_inc(consts.sem, 1)
            pool.memset(ga[:], 0.0).then_inc(consts.sem, 1)
            pool.memset(fsum[:], 0.0).then_inc(consts.sem, 1)
            pool.memset(eps[:, 0:1], EPS_LN).then_inc(consts.sem, 1)
            pool.memset(eps[:, 1:2], EPS_MLSTM).then_inc(consts.sem, 1)
            pool.memset(held[:], 0.0).then_inc(consts.sem, 1)
            pool.wait_ge(consts.sem, 9)
            pool.affine_select(out=ident[:, :], in_=ident[:, :], compare_op=ALU.not_equal, fill=1.0,
                               base=0, pattern=[[-1, P]], channel_multiplier=1).then_inc(consts.sem, 1)
            pool.wait_ge(consts.sem, 10)
            pool.wait_ge(weights.sem, 16 * NW)
            for w in (wi, wf):
                pool.tensor_tensor(w[:, KC:2 * KC, :], w[:, KC:2 * KC, :], w[:, 2 * KC:3 * KC, :],
                                   ALU.add).then_inc(wsum.sem, 1)
            pool.wait_ge(wsum.sem, 2)
            with pool.Fori(0, GROUPS) as g:
                xz_ready.wait(pool, g, 0)

                def rope(n):
                    rope_parts.wait(pool, g, n + 1)
                    feature.wait(pool, g, max(n - 1, 0))
                    pool.tensor_tensor(ry[:, n % 2, :], rt1[:, n % 2, :], rt2[:, n % 2, :],
                                       ALU.add).then_inc(rope_sum.sem, 1)

                for n in range(NF):
                    rope(n)
                for c in range(KC):
                    xT_ready.wait(pool, g, c + 1)
                    c_ready.wait(pool, g, GB * max(c - 1, 0))
                    for r in range(HR):
                        rows = slice(HD * r, HD * r + HD)
                        src = xT[rows, c, :].rearrange("p (b s) -> p b s", b=GB)
                        if r == 0:
                            xz_ready.wait(pool, g, c)
                        else:
                            xz_spread.wait(pool, g, (HR - 1) * c + r)
                        ins = pool.tensor_tensor(xz[rows, c % 2, :, r, :], src, by_batch(ones[rows, :]), ALU.mult)
                        ins.then_inc(xz_ready.sem if r == HR - 1 else xz_spread.sem, 1)

        @block.scalar
        def _(act):
            act.wait_ge(weights.sem, 16 * NW)
            act.wait_ge(consts.sem, 10)
            with act.Fori(0, GROUPS) as g:
                astep.n = 0

                def elu(n):
                    rope_sum.wait(act, g, n + 1)
                    feature.wait(act, g, max(n - 1, 0))
                    astep.did(act.activation(ee[:, n % 2, :], ry[:, n % 2, :], ACT.Relu, scale=-1.0))
                    astep.wait(act, g)
                    act.activation(ee[:, n % 2, :], ee[:, n % 2, :], ACT.Exp, scale=-1.0).then_inc(elu_parts.sem, 1)

                def norm(i):
                    moments.wait(act, g, i + 1)
                    astep.did(act.activation(lnv[:, :], mom[:, :, 1], ACT.Ln, bias=eps[:, 0:1]))
                    astep.wait(act, g)
                    act.activation(rstd[:, :], lnv[:, :], ACT.Exp, scale=-0.5).then_inc(rstd_ready.sem, 1)

                def turned(i):
                    for c in range(KC):
                        bank = tiles.wait(act, g, ("xt", i, c))
                        if i == 1:
                            xz_ready.wait(act, g, KC)
                        act.activation(xT[:, c, :], bank[:, :], ACT.Copy).then_inc(xT_ready.sem, 1)

                for j in range(KV0):
                    elu(j)
                for b in range(GB):
                    bank = tiles.wait(act, g, ("v", b))
                    act.activation(v[:, b, :], bank[:, :], ACT.Copy).then_inc(v_ready.sem, 1)
                for r in range(REP):
                    elu(KV0 + r)
                for j in range(KV0):
                    if j + 1 < KV0:
                        for r in range(REP):
                            elu(KV0 + REP * (j + 1) + r)
                    for b in range(GB):
                        n = GB * j + b
                        bank = tiles.wait(act, g, ("d", j, b))
                        o_scaled.wait(act, g, max(n - 1, 0))
                        act.activation(dn[:, n % 2, :], bank[:, :], ACT.Copy,
                                       bias=EPS_DEN).then_inc(den_copied.sem, 1)
                norm(0)
                turned(0)
                bank = tiles.wait(act, g, ("gate",))
                act.activation(gi[:, :], bank[0:HX, :], ACT.Identity, bias=bias[0:HX, 0:1])
                act.activation(gf[:, :], bank[32:32 + HX, :], ACT.Identity,
                               bias=bias[32:32 + HX, 0:1]).then_inc(gates_copied.sem, 1)
                gate_abs.wait(act, g, 1)
                astep.did(act.activation(g2[:, :], g2[:, :], ACT.Exp, scale=-1.0))
                astep.wait(act, g)
                act.activation(g2[:, :], g2[:, :], ACT.Ln, bias=1.0).then_inc(gate_log.sem, 1)
                gt_copied.wait(act, g, 1)
                act.activation(em[:, :, :], am[:, :, 32:48], ACT.Exp).then_inc(em_ready.sem, 1)

                def decays(c):
                    for r in range(HR):
                        decay_arg.wait(act, g, HR * c + r + 1)
                        act.activation(dec[:, c % 2, r, :, :], dec[:, c % 2, r, :, :], ACT.Exp,
                                       scale=-1.0).then_inc(decay.sem, 1)

                def heads(c):
                    for b in range(GB):
                        bank = tiles.wait(act, g, ("ho", c, b))
                        act.activation(ho[:, b, HR * c:HR * c + HR, :],
                                       bank[:, :].rearrange("p (r e) -> p r e", r=HR)[:, :, 0:VS],
                                       ACT.Copy).then_inc(ho_ready.sem, 1)

                decays(0)
                for c in range(KC):
                    if c + 1 < KC:
                        decays(c + 1)
                    if c:
                        heads(c - 1)
                heads(KC - 1)
                h_centred.wait(act, g, 1)
                act.activation(hs[:], hc[:], ACT.Square).then_inc(h_squared.sem, 1)
                h_var.wait(act, g, 1)
                astep.did(act.activation(hm[:, :], hm[:, :], ACT.Ln, scale=1.0 / HD, bias=eps[:, 1:2]))
                astep.wait(act, g)
                act.activation(hm[:, :], hm[:, :], ACT.Exp, scale=-0.5).then_inc(h_rstd.sem, 1)
                norm(1)
                turned(1)
                rt_shift.wait(act, g, 1)
                act.activation(pr[:], pr[:], ACT.Exp).then_inc(rt_exp.sem, 1)
                for n in range(KC + GB):
                    bank = tiles.wait(act, g, ("f1", n) if n < KC else ("f2", n - KC))
                    h_ready.wait(act, g, max(n - 1, 0))
                    act.activation(se[:, n % 2, :], bank[:, :], ACT.Exp, scale=-1.0).then_inc(h_exp.sem, 1)
                norm(2)
                pre_ready.wait(act, g, 1)
                act.dma_start(t["pre"][g], pre[:, :]).then_inc(stored.sem, 16)
                normed.wait(act, g, 3 * GB)
                act.dma_start(t["x3"][g], xg[:, :, :]).then_inc(stored.sem, 16)
            astep.close("layer 0, scalar")

        @block.tensor
        def _(pe):
            pe.wait_ge(weights.sem, 16 * NW)
            pe.wait_ge(wsum.sem, 2)

            with pe.Fori(0, GROUPS) as g:
                def chunks(key, lhs, rhs, n=KC, needs=()):
                    bank = tiles.start(pe, g, key, needs)
                    for c in range(n):
                        ins = pe.matmul(bank[:, :], lhs(c), rhs(c), start=(c == 0), stop=(c == n - 1))
                    tiles.done(ins)

                def queries(j):
                    wq_in[j % 2].wait(pe, g, j // 2 + 1)
                    for r in range(REP):
                        h = REP * j + r
                        chunks(("q", h), lambda c: wq[:, j % 2, c, r * P:(r + 1) * P], lambda c: xT[:, c, :])

                def outputs(j):
                    wo_in[j % 2].wait(pe, g, j // 2 + 1)
                    for b in range(GB):
                        chunks(("y", j, b), lambda r: ot[:, b, r, :], lambda r: wo[:, j % 2, r, :], REP,
                               [(o_scaled, GB * j + b + 1)])

                def turn_x(i):
                    for c in range(KC):
                        bank = tiles.start(pe, g, ("xt", i, c))
                        for b in range(GB):
                            if c == 0:
                                normed.wait(pe, g, GB * i + b + 1)
                            ins = pe.transpose(bank[:, b * P:(b + 1) * P], xg[:, b, c * P:(c + 1) * P], ident[:, :])
                        tiles.done(ins)

                xT_in.wait(pe, g, 1)
                for j in range(KV0):
                    chunks(("k", j), lambda c: wk[:, c, j * P:(j + 1) * P], lambda c: xT[:, c, :])
                for b in range(GB):
                    chunks(("v", b), lambda c: xT[:, c, b * P:(b + 1) * P], lambda c: wv[:, c, :])
                queries(0)
                for j in range(KV0):
                    if j + 1 < KV0:
                        queries(j + 1)
                    for b in range(GB):
                        cols = slice(b * P, (b + 1) * P)
                        bank = tiles.start(pe, g, ("s", j, b), [(feature, KV0 + REP * (j + 1))])
                        tiles.done(pe.matmul(bank[:, :], kf[:, j, cols], qf[:, j % 2, :, cols],
                                             start=True, stop=True))
                    if j:
                        outputs(j - 1)
                    v_ready.wait(pe, g, GB)
                    for b in range(GB):
                        bank = tiles.start(pe, g, ("d", j, b), [(masked, GB * j + b + 1)])
                        tiles.done(pe.matmul(bank[:, :], ones[:, :], st[:, b, :], start=True, stop=True))
                        bank = tiles.start(pe, g, ("o", j, b))
                        tiles.done(pe.matmul(bank[:, :], v[:, b, j * P:(j + 1) * P], st[:, b, :],
                                             start=True, stop=True))
                outputs(KV0 - 1)

                turn_x(0)
                bank = tiles.start(pe, g, ("gate",), [(xT_ready, KC)])
                cT_in.wait(pe, g, 1)
                for at, w in ((0, wi), (32, wf)):
                    for c in range(2 * KC):
                        src = xT[:, c, :] if c < KC else cT[:, c - KC, :]
                        ins = pe.matmul(bank[at:at + HX, :], w[:, c, :], src, start=(c == 0), stop=(c == 2 * KC - 1))
                tiles.done(ins)
                gates_ready.wait(pe, g, 1)
                bank = tiles.start(pe, g, ("gt",))
                for b in range(GB):
                    ins = pe.transpose(bank[:, b * P:(b + 1) * P], ga[:, b * P:(b + 1) * P], ident[:, :])
                tiles.done(ins)

                def spread(c):
                    for r in range(HR):
                        h = HR * c + r
                        bank = tiles.start(pe, g, ("cb", h))
                        tiles.done(pe.matmul(bank[:, :], sel[:, h, :], ga[:, :], start=True, stop=True))

                def values(c):
                    c_in.wait(pe, g, 1)
                    for b in range(GB):
                        bank = tiles.start(pe, g, ("ho", c, b), [(c_ready, GB * c + b + 1)])
                        for r in range(HR):
                            at = VS * (HX * b + HR * c + r)
                            ins = pe.matmul(bank[:, r * P:(r + 1) * P], cc[:, c % 2, b, r, :],
                                            va[:, at:at + P], start=True, stop=True)
                        tiles.done(ins)

                spread(0)
                for c in range(KC):
                    if c + 1 < KC:
                        spread(c + 1)
                    xz_ready.wait(pe, g, c + 1)
                    for b in range(GB):
                        bank = tiles.start(pe, g, ("qk", c, b))
                        tiles.done(pe.matmul(bank[:, :], cT[:, c, b * P:(b + 1) * P], xz[:, c % 2, b, :, :],
                                             start=True, stop=True))
                    if c:
                        values(c - 1)
                values(KC - 1)

                turn_x(1)
                bank = tiles.start(pe, g, ("rt",), [(xT_ready, 2 * KC)])
                for b in range(GB):
                    for c in range(KC):
                        ins = pe.matmul(bank[:, b * E0:(b + 1) * E0], xT[:, c, b * P:(b + 1) * P], wr[:, c, :],
                                        start=(c == 0), stop=(c == KC - 1))
                tiles.done(ins)
                wq_in[0].wait(pe, g, KV0 // 2 + 1)
                for i in range(KC):
                    chunks(("f1", i), lambda c: w1[:, c, i * P:(i + 1) * P], lambda c: xT[:, c, :])
                wq_in[1].wait(pe, g, KV0 // 2 + 1)
                for b in range(GB):
                    chunks(("f2", b), lambda c: h1[:, c, b * P:(b + 1) * P], lambda c: w3[:, c, :],
                           needs=[(h_ready, KC)])
                routed.wait(pe, g, 1)
                bank = tiles.start(pe, g, ("fa",), [(h_ready, KC + GB)])
                for b in range(GB):
                    ins = pe.matmul(bank[0:E0, :], gate[:, b, :], h2[:, b, :], start=(b == 0), stop=(b == GB - 1))
                tiles.done(ins)

        @block.vector
        def _(dve):
            dve.wait_ge(weights.sem, 16 * NW)
            dve.wait_ge(consts.sem, 10)
            with dve.Fori(0, GROUPS) as g:
                vstep.n = 0

                def parts(n):
                    bank = tiles.wait(dve, g, ("k", n) if n < KV0 else ("q", n - KV0))
                    rope_sum.wait(dve, g, max(n - 1, 0))
                    view = bank[:, :].rearrange("p (b s) -> p b s", b=GB)
                    u = n % 2
                    dve.tensor_tensor(rt1[:, u, :].rearrange("p (b s) -> p b s", b=GB), view,
                                      by_batch(cos[:, :]), ALU.mult)
                    for to, of in ((0, 64), (64, 0)):
                        ins = dve.tensor_tensor(
                            rt2[to:to + 64, u, :].rearrange("p (b s) -> p b s", b=GB), view[of:of + 64],
                            by_batch(sin[of:of + 64, :]), ALU.mult)
                    ins.then_inc(rope_parts.sem, 1)

                def features(n):
                    elu_parts.wait(dve, g, n + 1)
                    j, r = divmod(n - KV0, REP)
                    out = kf[:, n, :] if n < KV0 else qf[:, j % 2, r, :]
                    dve.scalar_tensor_tensor(out, ry[:, n % 2, :], 0.0, ee[:, n % 2, :], ALU.max,
                                             ALU.add).then_inc(feature.sem, 1)

                def run_of(first, count):
                    for n in range(first, first + count):
                        parts(n)
                        if n > first:
                            features(n - 1)
                    features(first + count - 1)

                def added(j):
                    for b in range(GB):
                        bank = tiles.wait(dve, g, ("y", j, b))
                        if j:
                            y_added.wait(dve, g, GB * (j - 1) + b + 1)
                        dve.tensor_tensor(xg[:, b, :], bank[:, :], xg[:, b, :], ALU.add).then_inc(y_added.sem, 1)

                def norm(i, last):
                    last()
                    for b in range(GB):
                        ins = dve.bn_stats(stats[:, b, :], xg[:, b, :])
                    vstep.did(ins)
                    vstep.wait(dve, g)
                    dve.tensor_copy(held[:, 1:2], held[:, 0:1])
                    for b in range(GB):
                        ins = dve.bn_aggr(mom[:, b, :], stats[:, b, :])
                    ins.then_inc(moments.sem, 1)
                    rstd_ready.wait(dve, g, i + 1)
                    for b in range(GB):
                        dve.tensor_scalar(xg[:, b, :], xg[:, b, :], mom[:, b, 0:1], rstd[:, b:b + 1],
                                          ALU.subtract, ALU.mult).then_inc(normed.sem, 1)

                run_of(0, KV0)
                run_of(KV0, REP)
                x_in.wait(dve, g, 1)
                for j in range(KV0):
                    if j + 1 < KV0:
                        run_of(KV0 + REP * (j + 1), REP)
                    for b in range(GB):
                        bank = tiles.wait(dve, g, ("s", j, b))
                        dve.tensor_tensor(st[:, b, :].rearrange("p (r q) -> p r q", r=REP),
                                          bank[:, :].rearrange("p (r q) -> p r q", r=REP),
                                          by_batch(causal[:, :]), ALU.mult).then_inc(masked.sem, 1)
                    if j:
                        added(j - 1)
                    for b in range(GB):
                        n = GB * j + b
                        den_copied.wait(dve, g, n + 1)
                        vstep.did(dve.reciprocal(dn[:, n % 2, :], dn[:, n % 2, :]))
                        vstep.wait(dve, g)
                        bank = tiles.wait(dve, g, ("o", j, b))
                        dve.tensor_tensor(ot[:, b, :, :], bank[:, :].rearrange("p (r q) -> p r q", r=REP),
                                          dn[:, n % 2, :].rearrange("p (r q) -> p r q", r=REP),
                                          ALU.mult).then_inc(o_scaled.sem, 1)
                added(KV0 - 1)
                norm(0, lambda: y_added.wait(dve, g, KV0 * GB))

                gates_copied.wait(dve, g, 1)
                vstep.did(dve.tensor_scalar(g1[:, :], gf[:, :], 0.0, None, ALU.min))
                dve.scalar_tensor_tensor(g2[:, :], gf[:, :], -1.0, gf[:, :], ALU.mult,
                                         ALU.max).then_inc(gate_abs.sem, 1)
                gate_log.wait(dve, g, 1)
                vstep.wait(dve, g)
                vstep.did(dve.tensor_tensor(g1[:, :], g1[:, :], g2[:, :], ALU.subtract))
                vstep.wait(dve, g)
                for b in range(GB):
                    cols = slice(b * P, (b + 1) * P)
                    ins = dve.tensor_tensor_scan(g3[:, cols], ones[0:HX, :], g1[:, cols], 0.0, ALU.mult, ALU.add)
                vstep.did(ins)
                vstep.wait(dve, g)
                vstep.did(dve.tensor_tensor(ga[0:HX, :], gi[:, :], g3[:, :], ALU.subtract))
                vstep.wait(dve, g)
                for b in range(GB):
                    cols = slice(b * P, (b + 1) * P)
                    ins = dve.tensor_tensor_scan(g1[:, cols], ones[0:HX, :], ga[0:HX, cols], -3e38,
                                                 ALU.mult, ALU.max)
                vstep.did(ins)
                vstep.wait(dve, g)
                dve.scalar_tensor_tensor(ga[32:32 + HX, :], g3[:, :], -1.0, g1[:, :], ALU.mult, ALU.subtract)
                dve.tensor_copy(ga[64:64 + HX, :], g1[:, :]).then_inc(gates_ready.sem, 1)
                bank = tiles.wait(dve, g, ("gt",))
                dve.tensor_copy(am[:, :, :], bank[:, :].rearrange("p (b n) -> p b n", b=GB)[:, :, 0:48])\
                   .then_inc(gt_copied.sem, 1)
                gt_copied.wait(dve, g, 1)

                def decay_args(c):
                    c_ready.wait(dve, g, GB * max(c - 1, 0))
                    for r in range(HR):
                        h = HR * c + r
                        bank = tiles.wait(dve, g, ("cb", h))
                        for b in range(GB):
                            ins = dve.scalar_tensor_tensor(
                                dec[:, c % 2, r, b, :], bank[:, b * P:(b + 1) * P], am[:, b, h:h + 1],
                                barred[:, :], ALU.subtract, ALU.max)
                        ins.then_inc(decay_arg.sem, 1)

                decay_args(0)
                for c in range(KC):
                    if c + 1 < KC:
                        decay_args(c + 1)
                    decay.wait(dve, g, HR * (c + 1))
                    for b in range(GB):
                        bank = tiles.wait(dve, g, ("qk", c, b))
                        dve.scalar_tensor_tensor(
                            cc[:, c % 2, b, :, :], bank[:, :].rearrange("p (r s) -> p r s", r=HR),
                            float(HD) ** -0.5, dec[:, c % 2, :, b, :], ALU.mult, ALU.mult).then_inc(c_ready.sem, 1)

                hall = ho.rearrange("p b h e -> p (b h) e")
                ho_ready.wait(dve, g, KC * GB)
                em_ready.wait(dve, g, 1)

                def chained(ins):
                    vstep.did(ins)
                    vstep.wait(dve, g)

                def wide(ap):
                    return ap.unsqueeze(2).broadcast_to([P, GB * HX, HD])

                chained(dve.tensor_copy(hm[:, :], hall[:, :, HD]))
                chained(dve.scalar_tensor_tensor(hn[:, :], hm[:, :], -1.0, hm[:, :], ALU.mult, ALU.max))
                chained(dve.tensor_tensor(hn[:, :], hn[:, :], em[:, :, :].rearrange("p b h -> p (b h)"), ALU.max))
                chained(dve.tensor_scalar(hn[:, :], hn[:, :], EPS_MLSTM, None, ALU.add))
                chained(dve.reciprocal(hn[:, :], hn[:, :]))
                chained(dve.tensor_tensor(hv[:], hall[:, :, 0:HD], wide(hn[:, :]), ALU.mult))
                chained(dve.tensor_reduce(hm[:, :], hv[:], AX.X, ALU.add))
                chained(dve.tensor_scalar(hm[:, :], hm[:, :], 1.0 / HD, None, ALU.mult))
                dve.tensor_tensor(hc[:], hv[:], wide(hm[:, :]), ALU.subtract).then_inc(h_centred.sem, 1)
                h_squared.wait(dve, g, 1)
                dve.tensor_reduce(hm[:, :], hs[:], AX.X, ALU.add).then_inc(h_var.sem, 1)
                h_rstd.wait(dve, g, 1)
                chained(dve.tensor_tensor(hc[:], hc[:], wide(hm[:, :]), ALU.mult))
                hrow = hc.rearrange("p (b h) e -> p b (h e)", b=GB)
                chained(dve.tensor_tensor(hrow, hrow, lnw[:, :].unsqueeze(1).broadcast_to([P, GB, D]), ALU.mult))
                chained(dve.tensor_tensor(xg[:, :, :], xg[:, :, :], hrow, ALU.add))
                norm(1, lambda: None)

                normed.wait(dve, g, 2 * GB)
                stored.wait(dve, g, 0)
                dve.tensor_copy(pre[:, :], xg[0:E0, 0, :]).then_inc(pre_ready.sem, 1)

                def each(ap):
                    return ap.unsqueeze(2).broadcast_to([P, GB, E0])

                bank = tiles.wait(dve, g, ("rt",))
                logits = bank[:, 0:GB * E0].rearrange("p (b e) -> p b e", b=GB)
                chained(dve.tensor_reduce(rmx[:, :], logits, AX.X, ALU.max))
                dve.tensor_tensor(pr[:, :, :], logits, each(rmx[:, :]), ALU.subtract).then_inc(rt_shift.sem, 1)
                rt_exp.wait(dve, g, 1)
                chained(dve.tensor_reduce(rmx[:, :], pr[:, :, :], AX.X, ALU.add))
                chained(dve.reciprocal(rmx[:, :], rmx[:, :]))
                chained(dve.tensor_tensor(pr[:, :, :], pr[:, :, :], each(rmx[:, :]), ALU.mult))
                dve.tensor_copy(held[:, 1:2], held[:, 0:1])
                for b in range(GB):
                    ins = dve.max(top[:, b, :], pr[:, b, :])
                chained(ins)
                dve.tensor_copy(held[:, 1:2], held[:, 0:1])
                for b in range(GB):
                    ins = dve.max_index(topi[:, b, :], top[:, b, :], pr[:, b, :])
                chained(ins)
                chained(dve.tensor_copy(topf[:, :, :], topi[:, :, :]))
                chained(dve.tensor_tensor(rmx[:, :], top[:, :, 0], top[:, :, 1], ALU.add))
                chained(dve.reciprocal(rmx[:, :], rmx[:, :]))
                chained(dve.tensor_tensor(top[:, :, 0:2], top[:, :, 0:2],
                                          rmx[:, :].unsqueeze(2).broadcast_to([P, GB, 2]), ALU.mult))
                for b in range(GB):
                    for k in range(2):
                        ins = dve.tensor_scalar(eq[:, k, :], iota[:, :], topf[:, b, k:k + 1], top[:, b, k:k + 1],
                                                ALU.is_equal, ALU.mult)
                    chained(ins)
                    ins = dve.tensor_tensor(gate[:, b, :], eq[:, 0, :], eq[:, 1, :], ALU.add)
                    if b < GB - 1:
                        chained(ins)
                ins.then_inc(routed.sem, 1)

                for n in range(KC + GB):
                    h_exp.wait(dve, g, n + 1)
                    chained(dve.tensor_scalar(se[:, n % 2, :], se[:, n % 2, :], 1.0, None, ALU.add))
                    chained(dve.reciprocal(sr, se[:, n % 2, :]))
                    bank = tiles.bank(("f1", n) if n < KC else ("f2", n - KC))
                    out = h1[:, n, :] if n < KC else h2[:, n - KC, :]
                    dve.tensor_tensor(out, bank[:, :], sr, ALU.mult).then_inc(h_ready.sem, 1)
                bank = tiles.wait(dve, g, ("fa",))
                dve.tensor_tensor(fsum[:, :], bank[0:E0, :], fsum[:, :], ALU.add).then_inc(f_added.sem, 1)
                norm(2, lambda: None)
            vstep.close("layer 0, vector")


def build_row_fix(nc, t):
    with ExitStack() as ctx:
        def sb(name, shape, dt=F32):
            return ctx.enter_context(nc.sbuf_tensor("b_" + name, shape, dt))

        w2, fs, ft = sb("w2", [P, KC, D]), sb("fs", [P, D]), sb("ft", [P, KC, P])
        ident, rows = sb("ident", [P, P]), sb("rows", [E0, D])
        stats, mom, rstd, eps = sb("stats", [E0, 6]), sb("mom", [E0, 2]), sb("rstd", [E0, 1]), sb("eps", [E0, 1])
        bank = ctx.enter_context(nc.psum_tensor("b_bank", [P, 512], F32))
        out = ctx.enter_context(nc.psum_tensor("b_out", [P, 512], F32))
        cleared, loaded, turned, copied, product, fixed, scaled, stored = (
            ctx.enter_context(nc.semaphore("b_" + n))
            for n in ("cleared", "loaded", "turned", "copied", "product", "fixed", "scaled", "stored"))
        step = ctx.enter_context(nc.semaphore("b_step"))
        block = ctx.enter_context(nc.Block())

        @block.sync
        def _(sp):
            sp.dma_start(w2[:], t["w20"]).then_inc(loaded, 16)
            sp.dma_start(ident[:], t["ident"]).then_inc(loaded, 16)
            sp.dma_start(rows[:], t["pre"][0]).then_inc(loaded, 16)
            sp.wait_ge(cleared, 2)
            sp.dma_start(fs[0:E0, :], t["fsum"]).then_inc(loaded, 16)
            sp.wait_ge(step, 5)
            sp.dma_start(t["x3"][0][0:E0, 0, :], rows[:]).then_inc(stored, 16)
            sp.wait_ge(stored, 16)

        @block.gpsimd
        def _(pool):
            pool.memset(fs[:], 0.0).then_inc(cleared, 1)
            pool.memset(eps[:], EPS_LN).then_inc(cleared, 1)

        @block.tensor
        def _(pe):
            pe.wait_ge(loaded, 64)
            for c in range(KC):
                ins = pe.transpose(bank[:, c * P:(c + 1) * P], fs[:, c * P:(c + 1) * P], ident[:, :])
            ins.then_inc(turned, 1)
            pe.wait_ge(copied, 1)
            for c in range(KC):
                ins = pe.matmul(out[:, :], ft[:, c, :], w2[:, c, :], start=(c == 0), stop=(c == KC - 1))
            ins.then_inc(product, 1)

        @block.vector
        def _(dve):
            dve.wait_ge(turned, 1)
            dve.tensor_copy(ft[:].rearrange("p c t -> p (c t)"), bank[:, :]).then_inc(copied, 1)
            dve.wait_ge(product, 1)
            dve.tensor_tensor(rows[:, :], out[0:E0, :], rows[:, :], ALU.add).then_inc(step, 1)
            dve.wait_ge(step, 1)
            dve.bn_stats(stats[:, :], rows[:, :]).then_inc(step, 1)
            dve.wait_ge(step, 2)
            dve.bn_aggr(mom[:, :], stats[:, :]).then_inc(step, 1)
            dve.wait_ge(scaled, 2)
            dve.tensor_scalar(rows[:, :], rows[:, :], mom[:, 0:1], rstd[:, 0:1],
                              ALU.subtract, ALU.mult).then_inc(step, 2)

        @block.scalar
        def _(act):
            act.wait_ge(cleared, 2)
            act.wait_ge(step, 3)
            act.activation(rstd[:, :], mom[:, 1:2], ACT.Ln, bias=eps[:, 0:1]).then_inc(scaled, 1)
            act.wait_ge(scaled, 1)
            act.activation(rstd[:, :], rstd[:, :], ACT.Exp, scale=-0.5).then_inc(scaled, 1)


def build_layer1(nc, t):
    with ExitStack() as ctx:
        def sb(name, shape, dt=F32):
            return ctx.enter_context(nc.sbuf_tensor("c_" + name, shape, dt))

        def signal(name, per, unit=1):
            return Signal(ctx.enter_context(nc.semaphore("c_" + name)), per, unit)

        PARTS = 3
        TERMS = ((0, 0), (0, 1), (1, 0), (1, 1), (0, 2), (2, 0))
        TR = len(TERMS) * CD
        SR = TR + PARTS
        LC = D // P

        banks = [ctx.enter_context(nc.psum_tensor(f"c_bank{i}", [P, 1024], F32)) for i in range(3)]
        pv = ctx.enter_context(nc.psum_tensor("c_pv", [P, 2, 512], F32))

        wq, wk, wv, wo = (sb(n, [P, KC, D]) for n in ("wq", "wk", "wv", "wo"))
        cos, sin = sb("cos", [P, CD]), sb("sin", [P, CD])
        decay = sb("decay", [P, HX, P])
        rmsw = sb("rmsw", [P, KC])
        gamma = sb("gamma", [P, 1])
        ident, ones = sb("ident", [P, P]), sb("ones", [P, P])
        perm = sb("perm", [P, 4, P])
        eps = sb("eps", [P, 1])
        held = sb("held", [P, 2])

        xg = sb("xg", [P, GB, D])
        area = sb("area", [P, 20480])
        yq = area[:, 0:2048].rearrange("p (b n) -> p b n", b=GB)
        yk = area[:, 2048:4096].rearrange("p (b n) -> p b n", b=GB)
        v = area[:, 4096:6144].rearrange("p (b n) -> p b n", b=GB)
        kT = area[:, 6144:8192].rearrange("p (b c n) -> p b c n", b=GB, c=KC)
        qT = area[:, 8192:10240].rearrange("p (b c n) -> p b c n", b=GB, c=KC)
        sm = area[:, 10240:14336].rearrange("p (u c r q) -> p u c r q", u=2, c=KC, r=HR)
        sq = yq.rearrange("p b (c q) -> p b c q", c=KC)
        at = yk.rearrange("p b (c q) -> p b c q", c=KC)
        r1 = area[:, 16384:17408].rearrange("p (u n) -> p u n", u=2)
        r2 = area[:, 17408:18432].rearrange("p (u n) -> p u n", u=2)
        xT = area[:, 18432:20480].rearrange("p (c t) -> p c t", c=KC)
        xz = sb("xz", [P, 2, KC, HR, P])
        probs = area[:, 0:4096].rearrange("p (u l n) -> p u l n", u=2, l=LC)
        ov = area[:, 4096:5120].rearrange("p (o n) -> p o n", o=2)
        rec = area[:, 5120:5632]
        cres = area[:, 5632:6144]
        qres = area[:, 6144:6656]
        cgr = area[:, 6656:8704].rearrange("p (b n) -> p b n", b=GB)
        cT = area[:, 8704:10752].rearrange("p (l t) -> p l t", l=LC)
        mx = sb("mx", [P, 2, P])
        mrow = sb("mrow", [P, P])
        qs = sb("qs", [P, 2, CH, D], BF16)
        ks = sb("ks", [P, 2, CH, D], BF16)
        qp = area[:, 10752:12288].bitcast(BF16).rearrange("p (u k n) -> p u k n", u=2, k=PARTS)
        kp = area[:, 12288:13824].bitcast(BF16).rearrange("p (u k n) -> p u k n", u=2, k=PARTS)
        mp = sb("mp", [P, 2, PARTS, P], BF16)
        vt = sb("vt", [P, LC, GB, CH, 32])
        stats, mom = sb("stats", [P, GB, 6]), sb("mom", [P, GB, 2])
        rstd, lnv, rms = sb("rstd", [P, GB]), sb("lnv", [P, GB]), sb("rms", [P, GB])

        NW, NC = 11, 7
        weights, consts = signal("weights", 0, 16), signal("consts", 0)
        x_in, c_in, cT_in = signal("x_in", 1, 16), signal("c_in", 1, 16), signal("cT_in", 1, 16)
        xT_ready, v_ready = signal("xT_ready", KC), signal("v_ready", GB)
        rot_parts, rotated = signal("rot_parts", 2 * GB), signal("rotated", 2 * GB)
        turned, spread_part, spread = signal("turned", 2 * GB), signal("spread_part", 3 * GB), signal("spread", GB)
        masked = signal("masked", KC * GB)
        squared, scaled, rms_ready, y_added = (signal(n, k) for n, k in (
            ("squared", GB), ("scaled", GB), ("rms_ready", 1), ("y_added", GB)))
        moments, rstd_ready, normed = signal("moments", 2), signal("rstd_ready", 2), signal("normed", 2 * GB)
        q_part, q_left, q_ready = signal("q_part", 2 * GB), signal("q_left", GB), signal("q_ready", GB)
        k_ready, vt_ready = signal("k_ready", GB), signal("vt_ready", 1)
        k_step = signal("k_step", 3 * GB)
        q_out, k_out, m_out = (signal(n, GB, 16) for n in ("q_out", "k_out", "m_out"))
        qs_in = [signal(f"qs_in{u}", len(TERMS) * GB // 2, 16) for u in range(2)]
        ks_in = [signal(f"ks_in{u}", len(TERMS) * GB // 2, 16) for u in range(2)]
        ms_in = [signal(f"ms_in{u}", GB // 2, 16) for u in range(2)]
        maxed, m_ready = signal("maxed", 2 * CH * GB), signal("m_ready", GB)
        exped = signal("exped", 2 * CH * GB)
        pv_done, pv_copied, rec_ready, added = (signal(n, GB) for n in ("pv_done", "pv_copied", "rec_ready", "added"))
        stored = signal("stored", 1, 16)

        order = [("xt", c) for c in range(KC)]
        for b in range(GB):
            order += [("q", b), ("k", b), ("v", b)]
        for b in range(GB):
            order += [("qt", b), ("kt", b)]
        for b in range(GB):
            order += [("s", b, c) for c in range(KC)]
            if b:
                order += [("a", b - 1)]
        order += [("a", GB - 1), ("ss",)] + [("y", b) for b in range(GB)]
        order += [("p", 0, h, u) for h in range(CH) for u in range(2)] + [("mt", 0)]
        for b in range(GB):
            for h in range(CH):
                order += [("e", b, h, u) for u in range(2)]
                if b + 1 < GB:
                    order += [("p", b + 1, h, u) for u in range(2)]
            if b + 1 < GB:
                order += [("mt", b + 1)]
            order += [("den", b), ("ret", b)]

        def drained(key):
            kind, *n = key
            return {
                "xt": lambda: (xT_ready, n[0] + 1),
                "q": lambda: (rot_parts, 2 * n[0] + 1),
                "k": lambda: (rot_parts, 2 * n[0] + 2),
                "v": lambda: (v_ready, n[0] + 1),
                "qt": lambda: (turned, 2 * n[0] + 1),
                "kt": lambda: (turned, 2 * n[0] + 2),
                "s": lambda: (masked, KC * n[0] + n[1] + 1),
                "a": lambda: (scaled, n[0] + 1),
                "ss": lambda: (rms_ready, 1),
                "y": lambda: (y_added, n[0] + 1),
                "p": lambda: (maxed, 2 * CH * n[0] + 2 * n[1] + n[2] + 1),
                "mt": lambda: (m_ready, n[0] + 1),
                "e": lambda: (exped, 2 * CH * n[0] + 2 * n[1] + n[2] + 1),
                "den": lambda: (rec_ready, n[0] + 1),
                "ret": lambda: (added, n[0] + 1),
            }[kind]()

        tiles = Tiles(banks, ctx.enter_context(nc.semaphore("c_filled")), order, drained)
        vstep = Steps(ctx.enter_context(nc.semaphore("c_vector_step")), 26)
        astep = Steps(ctx.enter_context(nc.semaphore("c_scalar_step")), 3)
        block = ctx.enter_context(nc.Block())

        @block.sync
        def _(sp):
            for dst, src in ((ident, "ident"), (wq, "wq1"), (cos, "cos1"), (sin, "sin1"), (wk, "wk1"), (wv, "wv1"),
                             (decay, "decay1"), (rmsw, "rms1"), (wo, "wo1"), (perm, "perm"), (gamma, "gamma1")):
                sp.dma_start(dst[:], t[src]).then_inc(weights.sem, 16)
            with sp.Fori(0, GROUPS) as g:
                stored.wait(sp, g, 0)
                sp.dma_start(xg[:, :, :], t["x3"][g]).then_inc(x_in.sem, 16)
                y_added.wait(sp, g, GB)
                sp.dma_start(cgr, t["c"][g]).then_inc(c_in.sem, 16)
                sp.dma_start(cT, t["cT"][g]).then_inc(cT_in.sem, 16)

                def out(b, ready, part, parked, done):
                    ready.wait(sp, g, b + 1)
                    sp.dma_start(parked[b % 2], part[:, b % 2]).then_inc(done.sem, 16)

                def stack(b, parked, done, side, dst, ins):
                    done.wait(sp, g, b + 1)
                    if side:
                        exped.wait(sp, g, 2 * CH * max(b - 1, 0))
                    for n, pair in enumerate(TERMS):
                        sp.dma_start(dst[CD * n:CD * n + CD, b % 2],
                                     parked[b % 2].rearrange("(h d) k l -> k d h l", d=CD)[pair[side]])\
                          .then_inc(ins[b % 2].sem, 16)

                def operands(b):
                    out(b, k_ready, kp, t["kpark"], k_out)
                    out(b, q_ready, qp, t["qpark"], q_out)
                    stack(b, t["kpark"], k_out, 1, ks, ks_in)
                    stack(b, t["qpark"], q_out, 0, qs, qs_in)

                def maxima(b):
                    m_ready.wait(sp, g, b + 1)
                    sp.dma_start(t["mpark"][b % 2].rearrange("k (x q) -> x k q", x=CH * LC), mp[0:CH * LC, b % 2])\
                      .then_inc(m_out.sem, 16)
                    m_out.wait(sp, g, b + 1)
                    sp.dma_start(qs[TR:SR, b % 2].rearrange("k h l -> k (h l)"), t["mpark"][b % 2])\
                      .then_inc(ms_in[b % 2].sem, 16)

                operands(0)
                operands(1)
                maxima(0)
                for b in range(1, GB):
                    maxima(b)
                    if b + 1 < GB:
                        operands(b + 1)
                normed.wait(sp, g, 2 * GB)
                sp.dma_start(t["x5"][g], xg[:, :, :]).then_inc(stored.sem, 16)
            sp.wait_ge(stored.sem, 16 * GROUPS)

        @block.gpsimd
        def _(pool):
            pool.memset(xz[:], 0.0).then_inc(consts.sem, 1)
            pool.memset(vt[:], 0.0).then_inc(consts.sem, 1)
            pool.memset(ones[:], 1.0).then_inc(consts.sem, 1)
            pool.memset(ks[:], 1.0).then_inc(consts.sem, 1)
            pool.memset(eps[:], EPS_LN).then_inc(consts.sem, 1)
            pool.memset(mx[:], 0.0).then_inc(consts.sem, 1)
            pool.wait_ge(consts.sem, 6)
            pool.memset(vt[:, :, :, :, CD], 1.0).then_inc(consts.sem, 1)
            pool.wait_ge(consts.sem, NC)
            with pool.Fori(0, GROUPS) as g:
                vt_ready.wait(pool, g, 0)
                k_ready.wait(pool, g, 0)
                for b in range(GB):
                    for i in range(2):
                        n = 2 * b + i
                        rot_parts.wait(pool, g, n + 1)
                        pool.tensor_tensor((yq, yk)[i][:, b, :], r1[:, i, :], r2[:, i, :],
                                           ALU.add).then_inc(rotated.sem, 1)
                rotated.wait(pool, g, 2 * GB)
                for b in range(GB):
                    turned.wait(pool, g, 2 * b + 1)
                    masked.wait(pool, g, KC * max(b - 1, 0))
                    for r in range(HR):
                        rows = slice(HD * r, HD * r + HD)
                        if r == 0:
                            spread.wait(pool, g, b)
                        else:
                            spread_part.wait(pool, g, (HR - 1) * b + r)
                        pool.tensor_tensor(xz[rows, b % 2, :, r, :], qT[rows, b],
                                           ones[rows, :].unsqueeze(1).broadcast_to([HD, KC, P]), ALU.mult)\
                            .then_inc((spread if r == HR - 1 else spread_part).sem, 1)
                spread.wait(pool, g, GB)
                cT_in.wait(pool, g, 1)
                for l in range(LC):
                    src = cT[:, l, :].rearrange("p (b h d) -> p b h d", b=GB, h=CH)
                    ins = pool.tensor_tensor(vt[:, l, :, :, 0:CD], src,
                                             ones[:, 0:1].unsqueeze(2).unsqueeze(3).broadcast_to([P, GB, CH, CD]),
                                             ALU.mult)
                ins.then_inc(vt_ready.sem, 1)
                c_in.wait(pool, g, 1)
                for b in range(GB):
                    u = b % 2
                    q_out.wait(pool, g, 0)
                    k_out.wait(pool, g, max(b - 1, 0))
                    one = ones[:, 0:1].broadcast_to([P, D])
                    if b:
                        k_ready.wait(pool, g, b)
                    pool.tensor_tensor(kp[:, u, 0, :], cgr[:, b, :], one, ALU.mult).then_inc(k_step.sem, 1)
                    k_step.wait(pool, g, 3 * b + 1)
                    pool.tensor_tensor(cres, cgr[:, b, :], kp[:, u, 0, :], ALU.subtract).then_inc(k_step.sem, 1)
                    k_step.wait(pool, g, 3 * b + 2)
                    pool.tensor_tensor(kp[:, u, 1, :], cres, one, ALU.mult).then_inc(k_step.sem, 1)
                    k_step.wait(pool, g, 3 * b + 3)
                    pool.tensor_tensor(kp[:, u, 2, :], cres, kp[:, u, 1, :], ALU.subtract).then_inc(k_ready.sem, 1)

        @block.scalar
        def _(act):
            act.wait_ge(weights.sem, 16 * NW)
            act.wait_ge(consts.sem, NC)
            with act.Fori(0, GROUPS) as g:
                astep.n = 0

                def root(src, signal, count, ready, scale=1.0):
                    signal.wait(act, g, count)
                    astep.did(act.activation(lnv[:, :], src, ACT.Ln, bias=eps[:, 0:1], scale=scale))
                    astep.wait(act, g)

                for c in range(KC):
                    bank = tiles.wait(act, g, ("xt", c))
                    act.activation(xT[:, c, :], bank[:, 0:512], ACT.Copy).then_inc(xT_ready.sem, 1)
                for b in range(GB):
                    bank = tiles.wait(act, g, ("v", b))
                    act.activation(v[:, b, :], bank[:, 0:512], ACT.Copy).then_inc(v_ready.sem, 1)
                for b in range(GB):
                    for i in range(2):
                        bank = tiles.wait(act, g, (("qt", "kt")[i], b))
                        act.activation((qT, kT)[i][:, b], bank[:, 0:512].rearrange("p (c n) -> p c n", c=KC),
                                       ACT.Copy).then_inc(turned.sem, 1)
                for b in range(GB):
                    bank = tiles.wait(act, g, ("a", b))
                    act.activation(sq[:, b], bank[:, 0:512].rearrange("p (c n) -> p c n", c=KC),
                                   ACT.Square).then_inc(squared.sem, 1)
                bank = tiles.wait(act, g, ("ss",))
                astep.did(act.activation(lnv[:, :], bank[:, 0:GB * P].rearrange("p (b n) -> p b n", b=GB)[:, :, 0],
                                         ACT.Ln, bias=eps[:, 0:1], scale=1.0 / D))
                astep.wait(act, g)
                act.activation(rms[:, :], lnv[:, :], ACT.Exp, scale=-0.5).then_inc(rms_ready.sem, 1)

                def norm(i):
                    moments.wait(act, g, i + 1)
                    rms_ready.wait(act, g, 1)
                    rstd_ready.wait(act, g, i)
                    astep.did(act.activation(lnv[:, :], mom[:, :, 1], ACT.Ln, bias=eps[:, 0:1]))
                    astep.wait(act, g)
                    act.activation(rstd[:, :], lnv[:, :], ACT.Exp, scale=-0.5).then_inc(rstd_ready.sem, 1)

                norm(0)

                def parts(b):
                    u = b % 2
                    normed.wait(act, g, b + 1)
                    q_out.wait(act, g, max(b - 1, 0))
                    act.activation(qp[:, u, 0, :], xg[:, b, :], ACT.Copy).then_inc(q_part.sem, 1)
                    q_left.wait(act, g, b + 1)
                    act.activation(qp[:, u, 1, :], qres, ACT.Copy).then_inc(q_part.sem, 1)

                parts(0)
                parts(1)
                for b in range(GB):
                    for h in range(CH):
                        if h == 2 and b + 2 < GB:
                            parts(b + 2)
                        for u in range(2):
                            bank = tiles.wait(act, g, ("e", b, h, u))
                            act.activation(probs[:, h % 2, 2 * u:2 * u + 2, :],
                                           bank[:, :].rearrange("p (l n) -> p l n", l=2), ACT.Exp,
                                           scale=float(CD) ** -0.5).then_inc(exped.sem, 1)
                    pv_done.wait(act, g, b + 1)
                    act.activation(ov, pv[:, :, :], ACT.Copy).then_inc(pv_copied.sem, 1)
                norm(1)
            astep.close("layer 1, scalar")

        @block.tensor
        def _(pe):
            pe.wait_ge(weights.sem, 16 * NW)
            pe.wait_ge(consts.sem, NC)
            with pe.Fori(0, GROUPS) as g:
                x_in.wait(pe, g, 1)
                for c in range(KC):
                    bank = tiles.start(pe, g, ("xt", c))
                    for b in range(GB):
                        ins = pe.transpose(bank[:, b * P:(b + 1) * P], xg[:, b, c * P:(c + 1) * P], ident[:, :])
                    tiles.done(ins)
                for b in range(GB):
                    for kind, w in (("q", wq), ("k", wk), ("v", wv)):
                        bank = tiles.start(pe, g, (kind, b), [(xT_ready, KC)])
                        for c in range(KC):
                            ins = pe.matmul(bank[:, 0:512], xT[:, c, b * P:(b + 1) * P], w[:, c, :],
                                            start=(c == 0), stop=(c == KC - 1))
                        tiles.done(ins)
                for b in range(GB):
                    for i in range(2):
                        bank = tiles.start(pe, g, (("qt", "kt")[i], b), [(rotated, 2 * b + i + 1)])
                        for c in range(KC):
                            ins = pe.transpose(bank[:, c * P:(c + 1) * P], (yq, yk)[i][:, b, c * P:(c + 1) * P],
                                               ident[:, :])
                        tiles.done(ins)

                def attend(b):
                    bank = tiles.start(pe, g, ("a", b), [(masked, KC * (b + 1))])
                    v_ready.wait(pe, g, GB)
                    for c in range(KC):
                        for r in range(HR):
                            at0 = HD * (HR * c + r)
                            ins = pe.matmul(bank[HD * r:HD * r + HD, c * P:(c + 1) * P], v[:, b, at0:at0 + HD],
                                            sm[:, b % 2, c, r, :], start=True, stop=True)
                    tiles.done(ins)

                for b in range(GB):
                    for c in range(KC):
                        bank = tiles.start(pe, g, ("s", b, c), [(spread, b + 1), (turned, 2 * b + 2)])
                        tiles.done(pe.matmul(bank[:, 0:512], kT[:, b, c, :], xz[:, b % 2, c], start=True, stop=True))
                    if b:
                        attend(b - 1)
                attend(GB - 1)
                bank = tiles.start(pe, g, ("ss",))
                for b in range(GB):
                    squared.wait(pe, g, b + 1)
                    for c in range(KC):
                        ins = pe.matmul(bank[:, b * P:(b + 1) * P], sq[:, b, c, :], ones[:, :],
                                        start=(c == 0), stop=(c == KC - 1))
                tiles.done(ins)
                for b in range(GB):
                    bank = tiles.start(pe, g, ("y", b), [(scaled, b + 1)])
                    for c in range(KC):
                        ins = pe.matmul(bank[:, 0:512], at[:, b, c, :], wo[:, c, :],
                                        start=(c == 0), stop=(c == KC - 1))
                    tiles.done(ins)

                def first(b, h):
                    if h == 0:
                        n = len(TERMS) * (b // 2 + 1)
                        qs_in[b % 2].wait(pe, g, n)
                        ks_in[b % 2].wait(pe, g, n)
                    for u in range(2):
                        bank = tiles.start(pe, g, ("p", b, h, u))
                        for i in range(2):
                            at0 = (2 * u + i) * P
                            ins = pe.matmul(bank[:, 512 * i:512 * i + 512], qs[0:TR, b % 2, h, at0:at0 + P],
                                            ks[0:TR, b % 2, h, :], start=True, stop=True)
                        tiles.done(ins)

                def turn_max(b):
                    bank = tiles.start(pe, g, ("mt", b), [(maxed, 2 * CH * (b + 1))])
                    tiles.done(pe.transpose(bank[:, 0:P], mx[:, b % 2, :], ident[:, :]))

                def second(b, h):
                    if h == 0:
                        ms_in[b % 2].wait(pe, g, b // 2 + 1)
                    for u in range(2):
                        bank = tiles.start(pe, g, ("e", b, h, u))
                        for i in range(2):
                            at0 = (2 * u + i) * P
                            ins = pe.matmul(bank[:, 512 * i:512 * i + 512], ks[0:SR, b % 2, h, at0:at0 + P],
                                            qs[0:SR, b % 2, h, :], start=True, stop=True)
                        tiles.done(ins)

                def values(b, h):
                    exped.wait(pe, g, 2 * CH * b + 2 * h + 2)
                    if h == 0:
                        vt_ready.wait(pe, g, 1)
                        pv_copied.wait(pe, g, b)
                    rows = slice(32 * (h // 2), 32 * (h // 2) + 32)
                    for l in range(LC):
                        ins = pe.matmul(pv[rows, h % 2, :], vt[:, l, b, h, :], probs[:, h % 2, l, :],
                                        start=(l == 0), stop=(l == LC - 1))
                    if h == CH - 1:
                        ins.then_inc(pv_done.sem, 1)

                for h in range(CH):
                    first(0, h)
                turn_max(0)
                for b in range(GB):
                    for h in range(CH):
                        second(b, h)
                        if b + 1 < GB:
                            first(b + 1, h)
                        if h:
                            values(b, h - 1)
                    values(b, CH - 1)
                    if b + 1 < GB:
                        turn_max(b + 1)
                    for kind, at0 in (("den", 2), ("ret", 0)):
                        bank = tiles.start(pe, g, (kind, b), [(pv_copied, b + 1)])
                        for o in range(2):
                            ins = pe.matmul(bank[:, 0:512], perm[:, at0 + o, :], ov[:, o, :],
                                            start=(o == 0), stop=(o == 1))
                        tiles.done(ins)

        @block.vector
        def _(dve):
            dve.wait_ge(weights.sem, 16 * NW)
            dve.wait_ge(consts.sem, NC)
            with dve.Fori(0, GROUPS) as g:
                vstep.n = 0

                def chained(ins):
                    vstep.did(ins)
                    vstep.wait(dve, g)

                for b in range(GB):
                    for i in range(2):
                        bank = tiles.wait(dve, g, (("q", "k")[i], b))
                        rotated.wait(dve, g, max(2 * b + i - 1, 0))
                        view = bank[:, 0:512].rearrange("p (h e d) -> p h e d", h=HX, e=2)
                        one = r1[:, i, :].rearrange("p (h d) -> p h d", d=CD)
                        two = r2[:, i, :].rearrange("p (h e d) -> p h e d", h=HX, e=2)
                        dve.tensor_tensor(one, bank[:, 0:512].rearrange("p (h d) -> p h d", d=CD),
                                          cos[:, :].unsqueeze(1).broadcast_to([P, 2 * HX, CD]), ALU.mult)
                        table = sin[:, :].unsqueeze(1).broadcast_to([P, HX, CD])
                        dve.tensor_tensor(two[:, :, 0, :], view[:, :, 1, :], table, ALU.mult)
                        dve.scalar_tensor_tensor(two[:, :, 1, :], view[:, :, 0, :], -1.0, table, ALU.mult,
                                                 ALU.mult).then_inc(rot_parts.sem, 1)

                def scale_out(b):
                    bank = tiles.wait(dve, g, ("a", b))
                    squared.wait(dve, g, b + 1)
                    dve.tensor_tensor(at[:, b], bank[:, 0:512].rearrange("p (c n) -> p c n", c=KC),
                                      rmsw[:, :].unsqueeze(2).broadcast_to([P, KC, P]),
                                      ALU.mult).then_inc(scaled.sem, 1)

                for b in range(GB):
                    for c in range(KC):
                        bank = tiles.wait(dve, g, ("s", b, c))
                        dve.tensor_tensor(sm[:, b % 2, c], bank[:, 0:512].rearrange("p (r n) -> p r n", r=HR),
                                          decay[:, HR * c:HR * c + HR, :], ALU.mult).then_inc(masked.sem, 1)
                    if b:
                        scale_out(b - 1)
                scale_out(GB - 1)
                rms_ready.wait(dve, g, 1)
                for b in range(GB):
                    bank = tiles.wait(dve, g, ("y", b))
                    dve.scalar_tensor_tensor(xg[:, b, :], bank[:, 0:512], rms[:, b:b + 1], xg[:, b, :],
                                             ALU.mult, ALU.add).then_inc(y_added.sem, 1)

                def norm(i, last):
                    last()
                    for b in range(GB):
                        ins = dve.bn_stats(stats[:, b, :], xg[:, b, :])
                    chained(ins)
                    dve.tensor_copy(held[:, 1:2], ones[:, 0:1])
                    for b in range(GB):
                        ins = dve.bn_aggr(mom[:, b, :], stats[:, b, :])
                    ins.then_inc(moments.sem, 1)
                    rstd_ready.wait(dve, g, i + 1)
                    for b in range(GB):
                        dve.tensor_scalar(xg[:, b, :], xg[:, b, :], mom[:, b, 0:1], rstd[:, b:b + 1],
                                          ALU.subtract, ALU.mult).then_inc(normed.sem, 1)

                norm(0, lambda: y_added.wait(dve, g, GB))

                def parts(b):
                    u = b % 2
                    q_ready.wait(dve, g, b)
                    q_part.wait(dve, g, 2 * b + 1)
                    dve.tensor_tensor(qres, xg[:, b, :], qp[:, u, 0, :], ALU.subtract).then_inc(q_left.sem, 1)
                    q_part.wait(dve, g, 2 * b + 2)
                    dve.tensor_tensor(qp[:, u, 2, :], qres, qp[:, u, 1, :], ALU.subtract).then_inc(q_ready.sem, 1)

                def maxima(b, h):
                    for u in range(2):
                        bank = tiles.wait(dve, g, ("p", b, h, u))
                        at0 = LC * h + 2 * u
                        dve.tensor_reduce(mx[:, b % 2, at0:at0 + 2], bank[:, :].rearrange("p (i n) -> p i n", i=2),
                                          AX.X, ALU.max).then_inc(maxed.sem, 1)

                def max_parts(b):
                    u, rows = b % 2, slice(0, CH * LC)
                    bank = tiles.wait(dve, g, ("mt", b))
                    m_out.wait(dve, g, max(b - 1, 0))
                    chained(dve.tensor_scalar(mrow[rows, :], bank[rows, 0:P], -1.0, None, ALU.mult))
                    chained(dve.tensor_copy(mp[rows, u, 0, :], mrow[rows, :]))
                    chained(dve.tensor_tensor(mrow[rows, :], mrow[rows, :], mp[rows, u, 0, :], ALU.subtract))
                    chained(dve.tensor_copy(mp[rows, u, 1, :], mrow[rows, :]))
                    dve.tensor_tensor(mp[rows, u, 2, :], mrow[rows, :], mp[rows, u, 1, :],
                                      ALU.subtract).then_inc(m_ready.sem, 1)

                def finish(b):
                    bank = tiles.wait(dve, g, ("den", b))
                    added.wait(dve, g, b)
                    chained(dve.reciprocal(rec, bank[:, 0:512]))
                    dve.tensor_scalar(rec, rec, gamma[:, 0:1], None, ALU.mult).then_inc(rec_ready.sem, 1)
                    rec_ready.wait(dve, g, b + 1)
                    bank = tiles.wait(dve, g, ("ret", b))
                    chained(dve.tensor_tensor(rec, bank[:, 0:512], rec, ALU.mult))
                    dve.tensor_tensor(xg[:, b, :], xg[:, b, :], rec, ALU.add).then_inc(added.sem, 1)

                parts(0)
                parts(1)
                for h in range(CH):
                    maxima(0, h)
                max_parts(0)
                for b in range(GB):
                    for h in range(CH):
                        if h == 2 and b + 2 < GB:
                            parts(b + 2)
                        if b + 1 < GB:
                            maxima(b + 1, h)
                    if b + 1 < GB:
                        max_parts(b + 1)
                    finish(b)
                norm(1, lambda: added.wait(dve, g, GB))
            vstep.close("layer 1, vector")


def build_experts(nc, t):
    with ExitStack() as ctx:
        def sb(name, shape, dt=F32):
            return ctx.enter_context(nc.sbuf_tensor("d_" + name, shape, dt))

        def semaphore(name):
            return ctx.enter_context(nc.semaphore("d_" + name))

        def signal(name, per=0, unit=1):
            return Signal(semaphore(name), per, unit)

        NGR, TOPG, TOPK = 4, 2, 4
        EG = NE // NGR
        TOKENS = SEQS * P
        BLOCKS = TOKENS * TOPK // P + NE
        LIST = BLOCKS + 2
        inner = chunks_of(FI)
        shared = chunks_of(FS)
        NI, NS = len(inner), len(shared)
        FP = NI * P

        banks = [ctx.enter_context(nc.psum_tensor(f"d_bank{i}", [P, 512], F32)) for i in range(BANKS)]
        y = sb("y", [P, SEQS, D])
        xT = sb("xT", [P, KC, TOKENS])
        ws1, ws3 = sb("ws1", [P, KC, FS]), sb("ws3", [P, KC, FS])
        ws2 = sb("ws2", [P, NS, D])
        hs = sb("hs", [P, NS, GT])
        gated = sb("gated", [P, 2, GT])
        wg = sb("wg", [P, KC, NE])
        w13 = sb("w13", [P, 2, 2, KC, FI])
        w2 = sb("w2", [P, 2, NI, D])
        xrow, xcol = sb("xrow", [P, 2, D]), sb("xcol", [P, 2, KC, P])
        gate = sb("gate", [P, 2, FI])
        hrow, hid = sb("hrow", [P, 2, FP]), sb("hid", [P, 2, FP])
        yrow = sb("yrow", [P, 2, D])
        SLOTS = 8
        back = sb("back", [P, SLOTS, D])

        iota, ident, causal, ones = sb("iota", [P, NE]), sb("ident", [P, P]), sb("causal", [P, P]), sb("ones", [P, P])
        steps_of = sb("steps_of", [P, SEQS - 1])
        block_no = sb("block_no", [1, BLOCKS + 1])
        token_no = sb("token_no", [P, SEQS], U32)
        eps = sb("eps", [P, 1])
        pr = sb("pr", [P, SEQS, NE])
        sel = sb("sel", [P, SEQS, NE])
        comb = sb("comb", [P, SEQS, NE])
        rmx = sb("rmx", [P, SEQS])
        grp = sb("grp", [P, SEQS, 8])
        top, topf = sb("top", [P, SEQS, 8]), sb("topf", [P, SEQS, 8])
        topi = sb("topi", [P, SEQS, 8], U32)
        eq = sb("eq", [P, SEQS, NE])
        before = sb("before", [P, SEQS, NE])
        count, base, more = sb("count", [P, NE]), sb("base", [P, NE]), sb("more", [P, NE, SEQS - 1])
        unit = sb("unit", [P, NE])
        slot = sb("slot", [P, TOPK, SEQS])
        slot_no = sb("slot_no", [P, TOPK, SEQS], U32)
        quot, rest = sb("quot", [P, TOPK, SEQS], U32), sb("rest", [P, TOPK, SEQS], U32)
        quotf, restf = sb("quotf", [P, TOPK, SEQS]), sb("restf", [P, TOPK, SEQS])
        place = sb("place", [P, TOPK, SEQS], U32)
        row_no = sb("row_no", [P, TOPK, SEQS], U32)
        past = sb("past", [1, BLOCKS + 1, NE - 1])
        owner, held = sb("owner", [1, BLOCKS + 1]), sb("held", [1, BLOCKS + 1])
        change = sb("change", [1, BLOCKS + 1])
        owner_no = sb("owner_no", [1, BLOCKS + 1], I32)
        fetch_no = sb("fetch_no", [1, BLOCKS + 1], I32)
        empty = sb("empty", [P, LIST], U32)
        tokens = sb("tokens", [P, LIST], U32)
        index = sb("index", [P, 2], U32)
        stats, mom, rstd = sb("stats", [P, SEQS, 6]), sb("mom", [P, SEQS, 2]), sb("rstd", [P, SEQS])

        loaded = [signal(f"loaded{g}", 0, 16) for g in range(GROUPS)]
        weights, consts, shared_in = signal("weights"), signal("consts"), signal("shared_in")
        xT_ready, rt_shift, rt_exp = signal("xT_ready"), signal("rt_shift"), signal("rt_exp")
        chosen_ready, placed, owners = signal("chosen_ready"), signal("placed"), signal("owners")
        list_clear, list_filled, list_in = signal("list_clear"), signal("list_filled"), signal("list_in")
        s_gated, s_h, s_added = signal("s_gated"), signal("s_h"), signal("s_added")
        moments, rstd_ready, normed = signal("moments"), signal("rstd_ready"), signal("normed")
        out_stored = signal("out_stored")
        expert_in = signal("expert_in")
        AHEAD = 2
        y_added = signal("y_added")
        COMBINED = range(SEQS)
        CONSTS = 7
        xcol_ready, gate_ready, hrow_ready, hid_ready, yrow_ready = (
            signal(n) for n in ("xcol_ready", "gate_ready", "hrow_ready", "hid_ready", "yrow_ready"))
        gathered = [signal(f"gathered{v}") for v in range(2)]
        row_stored = [signal(f"row_stored{v}") for v in range(2)]
        index_ready, pool_step = signal("index_ready"), signal("pool_step")
        returned = [signal(f"returned{n}") for n in range(SLOTS)]
        filled = signal("loop_filled")
        vstep = Steps(semaphore("vector_step"), 0)

        turned_bank, hidden_bank, gate_banks, up_banks, down_banks = banks[0], banks[1], banks[2:4], banks[4:6], banks[6:8]

        def turned(j):
            return 5 * j + 1

        def gate_up(j):
            return 5 * j + 7

        def up_done(j):
            return 5 * j + 9

        def hidden_turned(j):
            return 5 * j + 13

        def down_done(j):
            return 5 * j + 15

        def shared_tiles(groups):
            order = []
            for g in groups:
                order += [(kind, g, c) for c in range(NS) for kind in ("sg", "su")]
                order += [("sy", g, b) for b in range(GB)]
            return order

        def drained(key):
            kind, *n = key
            return {
                "xt": lambda: (xT_ready, n[0] + 1),
                "rt": lambda: (rt_shift, 1),
                "rank": lambda: (placed, 1),
                "sg": lambda: (s_gated, NS * n[0] + n[1] + 1),
                "su": lambda: (s_h, NS * n[0] + n[1] + 1),
                "sy": lambda: (s_added, GB * n[0] + n[1] + 1),
            }[kind]()

        EARLY, LATE = (0, 1), (2, 3)
        early = shared_tiles(EARLY)
        order = [("xt", b) for b in range(SEQS)] + [("rt",)] + early[:2 * NS] + [("rank",)] + early[2 * NS:]
        first = Tiles(banks, semaphore("filled"), order, drained)
        last = Tiles(banks, semaphore("filled2"), shared_tiles(LATE), drained)
        x_rows = t["x5"].rearrange("g p b d -> (g p b) d")
        list_rows = t["slots"].rearrange("p j -> (p j)").unsqueeze(1)
        result_rows = t["results"].rearrange("j p d -> (j p) d")
        block = ctx.enter_context(nc.Block())

        def load_number(eng, row, n):
            return eng.value_load(row[0:1, bass.ds(n, 1)], min_val=0, max_val=NE - 1)

        def load_expert(sp, e, at):
            sp.dma_start(w13[:, at], t["w131"][e]).then_inc(expert_in.sem, 16)
            sp.dma_start(w2[:, at], t["w21"][e]).then_inc(expert_in.sem, 16)

        @block.sync
        def _(sp):
            sp.dma_start(ident[:], t["ident"]).then_inc(weights.sem, 16)
            for g in range(GROUPS):
                sp.dma_start(y[:, GB * g:GB * (g + 1), :], t["x5"][g]).then_inc(loaded[g].sem, 16)
            for dst, src in ((wg, "wg1"), (iota, "iota1"), (causal, "causal"), (steps_of, "steps_of"),
                             (block_no, "block_no"), (token_no, "token_no")):
                sp.dma_start(dst[:], t[src]).then_inc(weights.sem, 16)
            for dst, src in ((ws1, "ws1"), (ws3, "ws3"), (ws2, "ws2")):
                sp.dma_start(dst[:], t[src]).then_inc(shared_in.sem, 16)
            sp.wait_ge(consts.sem, CONSTS)
            sp.dma_start(t["slots"], empty[:]).then_inc(list_clear.sem, 16)
            load_expert(sp, 0, 0)
            sp.wait_ge(list_filled.sem, 16 * TOPK * SEQS)
            sp.dma_start(tokens[:], t["slots"]).then_inc(list_in.sem, 16)
            sp.wait_ge(expert_in.sem, 32)
            load_expert(sp, 1, 1)
            sp.wait_ge(owners.sem, 1)
            for v in range(2):
                sp.sem_inc(row_stored[v].sem, 16)
            with sp.Fori(0, BLOCKS // 2) as i:
                for v in range(2):
                    j = 2 * i + v
                    fetch = load_number(sp, fetch_no, j + 1)
                    sp.wait_ge(yrow_ready.sem, AHEAD + 1 + j)
                    sp.dma_start(t["results"][j], yrow[:, v]).then_inc(row_stored[v].sem, 16)
                    with sp.If(fetch > 0):
                        sp.wait_ge(expert_in.sem, 32 * fetch)
                        load_expert(sp, fetch, fetch % 2)
            sp.wait_ge(yrow_ready.sem, AHEAD + 1 + BLOCKS)
            sp.dma_start(t["results"][BLOCKS], yrow[:, 0]).then_inc(row_stored[0].sem, 16)
            for b in range(SEQS):
                sp.wait_ge(normed.sem, b + 1)
                sp.dma_start(t["out"][b], y[:, b, :]).then_inc(out_stored.sem, 16)
            sp.wait_ge(out_stored.sem, 16 * SEQS)

        @block.gpsimd
        def _(pool):
            pool.memset(eps[:], EPS_LN).then_inc(consts.sem, 1)
            pool.memset(hs[:], 0.0).then_inc(consts.sem, 1)
            pool.memset(grp[:], -1.0).then_inc(consts.sem, 1)
            pool.memset(ones[:], 1.0).then_inc(consts.sem, 1)
            pool.memset(unit[:], 1.0).then_inc(consts.sem, 1)
            pool.memset(empty[:], 0).then_inc(consts.sem, 1)
            pool.memset(hrow[:], 0.0).then_inc(consts.sem, 1)
            pool.wait_ge(weights.sem, 16 * 7)
            pool.wait_ge(list_clear.sem, 16)
            pool.wait_ge(placed.sem, 2)
            for k in range(TOPK):
                for b in range(SEQS):
                    pool.indirect_dma_start(list_rows, bass.IndirectOffsetOnAxis(ap=place[:, k, b:b + 1], axis=0),
                                            token_no[:, b:b + 1], None).then_inc(list_filled.sem, 16)
            pool.wait_ge(list_in.sem, 16)

            def gather(j, v, held):
                if held is not None:
                    pool.wait_ge(xcol_ready.sem, held)
                    pool.sem_inc(pool_step.sem, 1)
                pool.tensor_copy(index[:, v:v + 1], tokens[:, bass.ds(j, 1)]).then_inc(index_ready.sem, 1)
                pool.wait_ge(index_ready.sem, j + 1)
                pool.sem_inc(pool_step.sem, 1)
                pool.indirect_dma_start(xrow[:, v], None, x_rows,
                                        bass.IndirectOffsetOnAxis(ap=index[:, v:v + 1], axis=0))\
                    .then_inc(gathered[v].sem, 16)

            gather(0, 0, None)
            with pool.Fori(0, BLOCKS // 2) as i:
                for v in range(2):
                    j = 2 * i + v
                    gather(j + 1, 1 - v, AHEAD + j)
            pool.wait_ge(row_stored[0].sem, 16 * (BLOCKS // 2 + 2))
            pool.wait_ge(row_stored[1].sem, 16 * (BLOCKS // 2 + 1))
            for n, (b, k) in enumerate((b, k) for b in COMBINED for k in range(TOPK)):
                if n >= SLOTS:
                    pool.wait_ge(y_added.sem, n - SLOTS + 1)
                pool.indirect_dma_start(back[:, n % SLOTS], None, result_rows,
                                        bass.IndirectOffsetOnAxis(ap=row_no[:, k, b:b + 1], axis=0))\
                    .then_inc(returned[n % SLOTS].sem, 16)

        @block.scalar
        def _(act):
            act.wait_ge(consts.sem, CONSTS)
            for b in range(SEQS):
                bank = first.wait(act, 0, ("xt", b))
                act.activation(xT[:, :, b * P:(b + 1) * P], bank[:, :].rearrange("p (c n) -> p c n", c=KC),
                               ACT.Copy).then_inc(xT_ready.sem, 1)
            act.wait_ge(rt_shift.sem, 1)
            act.activation(pr[:], pr[:], ACT.Exp).then_inc(rt_exp.sem, 1)

            def shared_gates(tiles, groups):
                for g in groups:
                    for c, (_, m) in enumerate(shared):
                        n = NS * g + c
                        bank = tiles.wait(act, 0, ("sg", g, c))
                        if n >= 2:
                            act.wait_ge(s_h.sem, n - 1)
                        act.activation(gated[0:m, n % 2, :], bank[0:m, :], ACT.Silu).then_inc(s_gated.sem, 1)

            shared_gates(first, EARLY)
            act.sem_inc(gate_ready.sem, AHEAD)
            act.sem_inc(yrow_ready.sem, AHEAD)

            def rows_out(v, m, done):
                act.wait_ge(filled.sem, done)
                act.wait_ge(row_stored[v].sem, 16 * (m + 1))
                act.activation(yrow[:, v], down_banks[v][:, :], ACT.Copy).then_inc(yrow_ready.sem, 1)

            with act.Fori(0, BLOCKS // 2) as i:
                for v in range(2):
                    j = 2 * i + v
                    act.wait_ge(filled.sem, gate_up(j))
                    act.wait_ge(hrow_ready.sem, AHEAD + j - 1)
                    act.activation(gate[:, v], gate_banks[v][:, 0:FI], ACT.Silu).then_inc(gate_ready.sem, 1)
                    rows_out(v, i, down_done(j - 1))
            rows_out(0, BLOCKS // 2, 5 * BLOCKS + 7)
            shared_gates(last, LATE)
            act.wait_ge(moments.sem, 1)
            act.activation(rstd[:, :], mom[:, :, 1], ACT.Ln, bias=eps[:, 0:1]).then_inc(rstd_ready.sem, 1)
            act.wait_ge(rstd_ready.sem, 1)
            act.activation(rstd[:, :], rstd[:, :], ACT.Exp, scale=-0.5).then_inc(rstd_ready.sem, 1)

        @block.tensor
        def _(pe):
            def up(tiles, key, w, width, group):
                bank = tiles.start(pe, 0, key)
                c0, m = width
                for c in range(KC):
                    ins = pe.matmul(bank[0:m, :], w[:, c, c0:c0 + m], xT[:, c, GT * group:GT * (group + 1)],
                                    start=(c == 0), stop=(c == KC - 1))
                tiles.done(ins)

            def shared_ups(tiles, g):
                for c in range(NS):
                    up(tiles, ("sg", g, c), ws1, shared[c], g)
                    up(tiles, ("su", g, c), ws3, shared[c], g)

            def shared_downs(tiles, g):
                for b in range(GB):
                    bank = tiles.start(pe, 0, ("sy", g, b), [(s_h, NS * (g + 1))])
                    for c in range(NS):
                        ins = pe.matmul(bank[:, :], hs[:, c, b * P:(b + 1) * P], ws2[:, c, :],
                                        start=(c == 0), stop=(c == NS - 1))
                    tiles.done(ins)

            pe.wait_ge(weights.sem, 16 * 7)
            for b in range(SEQS):
                if b % GB == 0:
                    pe.wait_ge(loaded[b // GB].sem, 16)
                bank = first.start(pe, 0, ("xt", b))
                for c in range(KC):
                    ins = pe.transpose(bank[:, c * P:(c + 1) * P], y[:, b, c * P:(c + 1) * P], ident[:, :])
                first.done(ins)
            bank = first.start(pe, 0, ("rt",), [(xT_ready, SEQS)])
            for b in range(SEQS):
                for c in range(KC):
                    ins = pe.matmul(bank[:, b * NE:(b + 1) * NE], xT[:, c, b * P:(b + 1) * P], wg[:, c, :],
                                    start=(c == 0), stop=(c == KC - 1))
            first.done(ins)
            pe.wait_ge(shared_in.sem, 48)
            pe.wait_ge(consts.sem, CONSTS)
            shared_ups(first, EARLY[0])
            bank = first.start(pe, 0, ("rank",), [(chosen_ready, 1)])
            pairs = sel[:].rearrange("p b e -> p (b e)")
            pe.matmul(bank[:, 0:SEQS * NE], causal[:, :], pairs, start=True, stop=True)
            ins = pe.matmul(bank[:, SEQS * NE:2 * SEQS * NE], ones[:, :], pairs, start=True, stop=True)
            first.done(ins)
            shared_downs(first, EARLY[0])
            for g in EARLY[1:]:
                shared_ups(first, g)
                shared_downs(first, g)

            def turn(v):
                for c in range(KC):
                    ins = pe.transpose(turned_bank[:, c * P:(c + 1) * P], xrow[:, v, c * P:(c + 1) * P], ident[:, :])
                ins.then_inc(filled.sem, 1)

            def turn_hidden(v):
                for c in range(NI):
                    ins = pe.transpose(hidden_bank[:, c * P:(c + 1) * P], hrow[:, v, c * P:(c + 1) * P], ident[:, :])
                ins.then_inc(filled.sem, 1)

            def up_rows(bank, v, which, at):
                for k in range(KC):
                    ins = pe.matmul(bank[:, 0:FI], xcol[:, v, k, :],
                                    w13[:, bass.ds(at, 1), which, k, :].rearrange("p a n -> p (a n)"),
                                    start=(k == 0), stop=(k == KC - 1))
                ins.then_inc(filled.sem, 1)

            def down(bank, v, at):
                for c in range(NI):
                    ins = pe.matmul(bank[:, :], hid[:, v, c * P:(c + 1) * P],
                                    w2[:, bass.ds(at, 1), c, :].rearrange("p a n -> p (a n)"),
                                    start=(c == 0), stop=(c == NI - 1))
                ins.then_inc(filled.sem, 1)

            pe.wait_ge(s_added.sem, GB * len(EARLY))
            pe.wait_ge(gathered[0].sem, 16)
            turn(0)
            pe.wait_ge(xcol_ready.sem, AHEAD + 1)
            pe.sem_inc(filled.sem, 4)
            pe.wait_ge(owners.sem, 1)
            with pe.Fori(0, BLOCKS // 2) as i:
                for v in range(2):
                    j = 2 * i + v
                    expert = load_number(pe, owner_no, j + 1)
                    last_at = load_number(pe, owner_no, j) % 2
                    pe.wait_ge(gathered[1 - v].sem, 16 * (i + 1 + v))
                    pe.wait_ge(xcol_ready.sem, AHEAD + j + 1)
                    turn(1 - v)
                    pe.wait_ge(expert_in.sem, 32 * (expert + 1))
                    pe.wait_ge(gate_ready.sem, AHEAD + j - 1)
                    up_rows(gate_banks[v], v, 0, expert % 2)
                    pe.wait_ge(hrow_ready.sem, AHEAD + j)
                    pe.wait_ge(hid_ready.sem, AHEAD + j)
                    turn_hidden(1 - v)
                    up_rows(up_banks[v], v, 1, expert % 2)
                    pe.wait_ge(hid_ready.sem, AHEAD + 1 + j)
                    pe.wait_ge(yrow_ready.sem, AHEAD + j - 1)
                    down(down_banks[v], 1 - v, last_at)
            pe.wait_ge(hrow_ready.sem, AHEAD + BLOCKS)
            pe.wait_ge(hid_ready.sem, AHEAD + BLOCKS)
            turn_hidden(1)
            pe.wait_ge(hid_ready.sem, AHEAD + 1 + BLOCKS)
            pe.wait_ge(yrow_ready.sem, AHEAD + BLOCKS - 1)
            down(down_banks[0], 1, (NE - 1) % 2)
            pe.wait_ge(yrow_ready.sem, AHEAD + BLOCKS + 1)
            pe.wait_ge(xcol_ready.sem, AHEAD + BLOCKS + 1)
            for g in LATE:
                shared_ups(last, g)
                shared_downs(last, g)

        @block.vector
        def _(dve):
            dve.wait_ge(consts.sem, CONSTS)
            dve.wait_ge(weights.sem, 16 * 7)

            def chained(ins):
                vstep.did(ins)
                vstep.wait(dve, 0)

            def wide(ap, n=NE):
                return ap.unsqueeze(2).broadcast_to([P, SEQS, n])

            bank = first.wait(dve, 0, ("rt",))
            logits = bank[:, 0:SEQS * NE].rearrange("p (b e) -> p b e", b=SEQS)
            chained(dve.tensor_reduce(rmx[:, :], logits, AX.X, ALU.max))
            dve.tensor_tensor(pr[:], logits, wide(rmx[:, :]), ALU.subtract).then_inc(rt_shift.sem, 1)
            dve.wait_ge(rt_exp.sem, 1)
            chained(dve.tensor_reduce(rmx[:, :], pr[:], AX.X, ALU.add))
            chained(dve.reciprocal(rmx[:, :], rmx[:, :]))
            chained(dve.tensor_tensor(pr[:], pr[:], wide(rmx[:, :]), ALU.mult))

            def chosen(out, src, width, count):
                for b in range(SEQS):
                    ins = dve.max(top[:, b, :], src[:, b, :])
                chained(ins)
                for b in range(SEQS):
                    ins = dve.max_index(topi[:, b, :], top[:, b, :], src[:, b, :])
                chained(ins)
                chained(dve.tensor_copy(topf[:], topi[:]))
                for k in range(count):
                    into = out if k == 0 else eq[:, :, 0:width]
                    chained(at_choice(into, k, width))
                    if k:
                        chained(dve.tensor_tensor(out, out, eq[:, :, 0:width], ALU.add))

            def at_choice(out, k, width=NE):
                return dve.tensor_tensor(out, iota[:, 0:width].unsqueeze(1).broadcast_to([P, SEQS, width]),
                                         wide(topf[:, :, k], width), ALU.is_equal)

            chained(dve.tensor_reduce(grp[:, :, 0:NGR], pr[:].rearrange("p b (g e) -> p b g e", e=EG), AX.X, ALU.max))
            chosen(sel[:, :, 0:NGR], grp[:], NGR, TOPG)
            mask = sel[:, :, 0:NGR]
            chained(dve.tensor_tensor(comb[:].rearrange("p b (g e) -> p b g e", e=EG),
                                      pr[:].rearrange("p b (g e) -> p b g e", e=EG),
                                      mask.unsqueeze(3).broadcast_to([P, SEQS, NGR, EG]), ALU.mult))
            chained(dve.tensor_scalar(grp[:, :, 0:NGR], mask, 1.0, None, ALU.subtract))
            chained(dve.tensor_tensor(comb[:].rearrange("p b (g e) -> p b g e", e=EG),
                                      comb[:].rearrange("p b (g e) -> p b g e", e=EG),
                                      grp[:, :, 0:NGR].unsqueeze(3).broadcast_to([P, SEQS, NGR, EG]), ALU.add))
            chosen(sel[:], comb[:], NE, TOPK)
            dve.sem_inc(chosen_ready.sem, 1)

            added = {}
            total = [0]

            def add_to_y(b, ins):
                total[0] += 1
                added[b] = (y_added, total[0])
                ins.then_inc(y_added.sem, 1)

            def shared_hidden(tiles, g, c):
                n, m = NS * g + c, shared[c][1]
                bank = tiles.wait(dve, 0, ("su", g, c))
                dve.wait_ge(s_gated.sem, n + 1)
                dve.tensor_tensor(hs[0:m, c, :], bank[0:m, :], gated[0:m, n % 2, :], ALU.mult).then_inc(s_h.sem, 1)

            def shared_add(tiles, g, b):
                bank = tiles.wait(dve, 0, ("sy", g, b))
                s = GB * g + b
                if s in added:
                    dve.wait_ge(added[s][0].sem, added[s][1])
                dve.tensor_tensor(y[:, s, :], bank[:, :], y[:, s, :], ALU.add).then_inc(s_added.sem, 1)
                added[s] = (s_added, s + 1)

            for c in range(NS):
                shared_hidden(first, EARLY[0], c)

            bank = first.wait(dve, 0, ("rank",))
            rank = bank[:, 0:SEQS * NE].rearrange("p (b e) -> p b e", b=SEQS)
            pairs = bank[:, SEQS * NE:2 * SEQS * NE].rearrange("p (b e) -> p b e", b=SEQS)
            chained(dve.memset(before[:, 0, :], 0.0))
            for b in range(1, SEQS):
                chained(dve.tensor_tensor(before[:, b, :], before[:, b - 1, :], pairs[:, b - 1, :], ALU.add))
            chained(dve.tensor_tensor(count[:, :], before[:, SEQS - 1, :], pairs[:, SEQS - 1, :], ALU.add))
            chained(dve.tensor_tensor(more[:], count[:, :].unsqueeze(2).broadcast_to([P, NE, SEQS - 1]),
                                      steps_of[:, :].unsqueeze(1).broadcast_to([P, NE, SEQS - 1]), ALU.is_gt))
            chained(dve.tensor_reduce(count[:, :], more[:], AX.X, ALU.add))
            chained(dve.tensor_scalar(count[:, :], count[:, :], 1.0, None, ALU.add))
            chained(dve.tensor_tensor_scan(base[:, :], unit[:, :], count[:, :], 0.0, ALU.mult, ALU.add))
            chained(dve.tensor_tensor(base[:, :], base[:, :], count[:, :], ALU.subtract))
            chained(dve.tensor_tensor(past[:], base[0:1, 1:NE].unsqueeze(1).broadcast_to([1, BLOCKS + 1, NE - 1]),
                                      block_no[:, :].unsqueeze(2).broadcast_to([1, BLOCKS + 1, NE - 1]), ALU.is_le))
            chained(dve.tensor_reduce(owner[:, :], past[:], AX.X, ALU.add))
            chained(dve.tensor_copy(owner_no[:, :], owner[:, :]))
            chained(dve.tensor_scalar(held[:, :], owner[:, :], float(NE - 2), None, ALU.min))
            chained(dve.memset(change[:, 0:1], 0.0))
            chained(dve.tensor_tensor(change[:, 1:], held[:, 1:], held[:, 0:BLOCKS], ALU.subtract))
            chained(dve.tensor_scalar(held[:, :], held[:, :], 1.0, None, ALU.add))
            chained(dve.tensor_tensor(change[:, :], change[:, :], held[:, :], ALU.mult))
            dve.tensor_copy(fetch_no[:, :], change[:, :]).then_inc(owners.sem, 1)
            chained(dve.tensor_scalar(base[:, :], base[:, :], float(P), -1.0, ALU.mult, ALU.add))
            chained(dve.tensor_tensor(before[:], before[:], rank, ALU.add))
            chained(dve.tensor_tensor(before[:], before[:], base[:, :].unsqueeze(1).broadcast_to([P, SEQS, NE]), ALU.add))
            dve.sem_inc(placed.sem, 1)
            for k in range(TOPK):
                chained(at_choice(eq[:], k))
                chained(dve.tensor_tensor(eq[:], eq[:], before[:], ALU.mult))
                chained(dve.tensor_reduce(slot[:, k, :], eq[:], AX.X, ALU.add))
            chained(dve.tensor_copy(slot_no[:], slot[:]))
            chained(dve.tensor_scalar(quot[:], slot_no[:], P.bit_length() - 1, None, ALU.logical_shift_right))
            chained(dve.tensor_scalar(rest[:], slot_no[:], P - 1, None, ALU.bitwise_and))
            chained(dve.tensor_copy(quotf[:], quot[:]))
            chained(dve.tensor_copy(restf[:], rest[:]))
            chained(dve.scalar_tensor_tensor(quotf[:], restf[:], float(LIST), quotf[:], ALU.mult, ALU.add))
            chained(dve.tensor_copy(place[:], quotf[:]))
            chained(dve.tensor_scalar(slot[:], slot[:], float(P), None, ALU.add))
            dve.tensor_copy(row_no[:], slot[:]).then_inc(placed.sem, 1)

            for b in range(GB):
                shared_add(first, EARLY[0], b)
            for g in EARLY[1:]:
                for c in range(NS):
                    shared_hidden(first, g, c)
                for b in range(GB):
                    shared_add(first, g, b)
            dve.sem_inc(xcol_ready.sem, AHEAD)
            dve.sem_inc(hrow_ready.sem, AHEAD)
            dve.sem_inc(hid_ready.sem, AHEAD)

            def columns(v):
                dve.tensor_copy(xcol[:, v].rearrange("p c n -> p (c n)"), turned_bank[:, :]).then_inc(xcol_ready.sem, 1)

            def hidden_columns(v):
                dve.tensor_copy(hid[:, v], hidden_bank[:, 0:FP]).then_inc(hid_ready.sem, 1)

            dve.wait_ge(filled.sem, turned(0))
            columns(0)
            with dve.Fori(0, BLOCKS // 2) as i:
                for v in range(2):
                    j = 2 * i + v
                    dve.wait_ge(filled.sem, turned(j + 1))
                    columns(1 - v)
                    dve.wait_ge(filled.sem, hidden_turned(j - 1))
                    hidden_columns(1 - v)
                    dve.wait_ge(filled.sem, up_done(j))
                    dve.wait_ge(gate_ready.sem, AHEAD + j + 1)
                    dve.tensor_tensor(hrow[:, v, 0:FI], up_banks[v][:, 0:FI], gate[:, v],
                                      ALU.mult).then_inc(hrow_ready.sem, 1)
            dve.wait_ge(filled.sem, 5 * BLOCKS + 6)
            hidden_columns(1)

            combine = [(n, b, k) for n, (b, k) in enumerate((b, k) for b in COMBINED for k in range(TOPK))]

            def combine_one():
                n, b, k = combine.pop(0)
                dve.wait_ge(returned[n % SLOTS].sem, 16 * (n // SLOTS + 1))
                if b in added:
                    dve.wait_ge(added[b][0].sem, added[b][1])
                add_to_y(b, dve.scalar_tensor_tensor(y[:, b, :], back[:, n % SLOTS], top[:, b, k:k + 1], y[:, b, :],
                                                     ALU.mult, ALU.add))

            for g in LATE:
                for c in range(NS):
                    shared_hidden(last, g, c)
                    for _ in range(4):
                        combine_one()
                for b in range(GB):
                    shared_add(last, g, b)
            while combine:
                combine_one()
            dve.wait_ge(y_added.sem, TOPK * SEQS)
            dve.wait_ge(s_added.sem, SEQS)
            for b in range(SEQS):
                ins = dve.bn_stats(stats[:, b, :], y[:, b, :])
            chained(ins)
            for b in range(SEQS):
                ins = dve.bn_aggr(mom[:, b, :], stats[:, b, :])
            ins.then_inc(moments.sem, 1)
            dve.wait_ge(rstd_ready.sem, 2)
            for b in range(SEQS):
                dve.tensor_scalar(y[:, b, :], y[:, b, :], mom[:, b, 0:1], rstd[:, b:b + 1],
                                  ALU.subtract, ALU.mult).then_inc(normed.sem, 1)


def build_program(nc, t):
    t = dict(t)
    scratch = (("x3", [GROUPS, P, GB, D], F32), ("pre", [GROUPS, E0, D], F32), ("fsum", [E0, D], F32),
               ("x5", [GROUPS, P, GB, D], F32), ("kpark", [2, P, 3, D], BF16), ("qpark", [2, P, 3, D], BF16),
               ("mpark", [2, 3, CH * D], BF16),
               ("slots", [P, SEQS * 4 + NE + 2], U32), ("results", [SEQS * 4 + NE + 1, P, D], F32))
    for name, shape, dt in scratch:
        t[name] = nc.dram_tensor("scratch_" + name, shape, dt, kind="Internal").ap()
    build_layer0(nc, t)
    build_row_fix(nc, t)
    build_layer1(nc, t)
    build_experts(nc, t)


def chunks_of(n):
    return [(a, min(P, n - a)) for a in range(0, n, P)]


def by_group(a):
    return np.ascontiguousarray(a.reshape(GROUPS, GB, P, D).transpose(0, 2, 1, 3))


def by_feature(a):
    return np.ascontiguousarray(a.reshape(GROUPS, GT, KC, P).transpose(0, 3, 2, 1))


def rows_of(a):
    return np.ascontiguousarray(a.reshape(-1, P, a.shape[-1]).transpose(1, 0, 2))


def constants():
    t = {}
    f = np.float32
    inv = (1.0 / f(10000.0) ** (np.arange(0, P, 2, dtype=f) / f(P))).astype(f)
    angle = np.outer(inv, np.arange(P, dtype=f)).astype(f)
    t["cos0"] = np.concatenate([np.cos(angle), np.cos(angle)]).astype(f)
    t["sin0"] = np.concatenate([np.sin(angle), -np.sin(angle)]).astype(f)
    k, q = np.arange(P)[:, None], np.arange(P)[None, :]
    t["causal"] = (q >= k).astype(f)
    t["barred"] = np.where(q >= k, 0.0, BIG).astype(f)
    t["ident"] = np.eye(P, dtype=f)
    sel = np.zeros((P, HX, P), f)
    sel[64 + np.arange(HX), np.arange(HX)] = 1
    t["sel"] = sel
    t["iota"] = np.broadcast_to(np.arange(E0, dtype=f), (P, E0)).copy()
    t["iota1"] = np.broadcast_to(np.arange(NE, dtype=f), (P, NE)).copy()
    t["steps_of"] = np.broadcast_to(P * np.arange(1, SEQS, dtype=f), (P, SEQS - 1)).copy()
    t["block_no"] = np.arange(-1, SEQS * 4 + NE, dtype=f)[None, :].copy()
    seq = np.arange(SEQS)[None, :]
    t["token_no"] = (seq // GB * GT + np.arange(P)[:, None] * GB + seq % GB).astype(np.uint32)
    freq = np.concatenate([f(1 / 1024.0) ** np.linspace(0, 1, HD // 4, dtype=f), np.zeros(HD // 4, f)]).astype(f)
    theta = (np.arange(P, dtype=f)[:, None] * freq[None, :]).astype(f)
    t["cos1"], t["sin1"] = np.cos(theta).astype(f), np.sin(theta).astype(f)
    first = 2.0 ** (-2.0 ** (-(np.log2(HX) - 3)))
    slopes = np.array([first * first ** i for i in range(HX)])
    dist = (q - k)[:, None, :]
    t["decay1"] = np.where(dist >= 0, np.exp(-slopes[None, :, None] * np.maximum(dist, 0)), 0.0).astype(f)
    perm = np.zeros((P, 4, P), f)
    for j in range(4):
        for d in range(CD):
            for odd in range(2):
                perm[32 * j + d, odd, 32 * j + CD * odd + d] = 1
                perm[32 * j + CD, 2 + odd, 32 * j + CD * odd + d] = 1
    t["perm"] = perm
    return t


def tables(i):
    t = constants()
    a = {k: np.asarray(v) for k, v in i.items()}
    t["x"], t["xT"] = by_group(a["x"]), by_feature(a["x"])
    t["c"], t["cT"] = by_group(a["ctx_2048"]), by_feature(a["ctx_2048"])
    t["wk0"], t["wv0"] = (rows_of(a["L0_attn_" + n].T) for n in ("Wk", "Wv"))
    t["wq0"] = np.stack([rows_of(w) for w in np.split(a["L0_attn_Wq"].T, KV0, axis=1)])
    t["wo0"] = np.stack([rows_of(w) for w in np.split(a["L0_attn_Wo"].T, KV0, axis=0)])
    t["wi0"], t["wf0"] = rows_of(a["L0_xattn_Wi"]), rows_of(a["L0_xattn_Wf"])
    bias = np.zeros((P, 2), np.float32)
    bias[0:HX, 0], bias[32:32 + HX, 0] = a["L0_xattn_bi"], a["L0_xattn_bf"]
    t["bias0"] = bias
    t["lnw0"] = np.broadcast_to(a["L0_xattn_ln_scale"], (P, D)).copy()
    t["w10"], t["w30"], t["w20"] = (rows_of(a["L0_ffn_" + n].T) for n in ("w1", "w3", "w2"))
    t["wr0"] = rows_of(a["L0_ffn_wr"].T)
    for n in ("q", "k", "v", "o"):
        t[f"w{n}1"] = rows_of(a[f"L1_attn_W{n}"])
    t["rms1"] = np.ascontiguousarray(a["L1_attn_rms_w"].reshape(KC, P).T)
    t["gamma1"] = np.broadcast_to(a["L1_xattn_gamma"], (P, 1)).copy()
    t["wg1"] = rows_of(a["L1_ffn_Wg"].T)
    both = np.stack([a["L1_ffn_W1"], a["L1_ffn_W3"]], axis=1)
    t["w131"] = np.ascontiguousarray(
        both.transpose(0, 3, 1, 2).reshape(NE, KC, P, 2, FI).transpose(0, 2, 3, 1, 4))
    t["ws1"], t["ws3"] = (rows_of(a["L1_ffn_" + n].T) for n in ("Ws1", "Ws3"))

    def padded(w):
        return rows_of(np.concatenate([w.T, np.zeros((-w.shape[1] % P, D), w.dtype)]))

    t["w21"] = np.stack([padded(w) for w in a["L1_ffn_W2"]])
    t["ws2"] = padded(a["L1_ffn_Ws2"])
    return t


def kernel(**inputs):
    import concourse.bacc as bacc
    from concourse.bass_utils import run_bass_kernel_spmd

    nc = bacc.Bacc("TRN2", target_bir_lowering=False, num_devices=1)
    arrays, t = {}, {}
    for name, a in tables(inputs).items():
        arrays[f"in_{name}"] = a
        t[name] = nc.dram_tensor(f"in_{name}", a.shape, mybir.dt.from_np(a.dtype), kind="ExternalInput").ap()
    t["out"] = nc.dram_tensor("out_x", [SEQS, P, D], F32, kind="ExternalOutput").ap()
    build_program(nc, t)
    result = run_bass_kernel_spmd(nc, [arrays], core_ids=[0])
    return result.results[0]["out_x"]
```

```python
from contextlib import ExitStack

import numpy as np

import concourse.bass as bass
from concourse import mybir

F32 = mybir.dt.float32
BF16 = mybir.dt.bfloat16
U32 = mybir.dt.uint32
I32 = mybir.dt.int32
ALU = mybir.AluOpType
ACT = mybir.ActivationFunctionType
AX = mybir.AxisListType

P = 128
SEQS = 16
D = 512
KC = D // P
GROUPS = 4
GB = SEQS // GROUPS
GT = GB * P
BANKS = 8

H0 = 16
KV0 = 4
REP = H0 // KV0
HX = 16
HD = 32
HR = P // HD
VS = HD + 1
EPS_DEN = 1e-6
EPS_LN = 1e-5
EPS_MLSTM = 1e-6
BIG = 1e30

E0 = 8
NE = 16
FI = 352
FS = 704
CH = 8
CD = P // CH


class Signal:

    def __init__(self, sem, per=0, unit=1, base=0):
        self.sem, self.per, self.unit, self.base = sem, per * unit, unit, base

    def wait(self, eng, turn, count):
        value = self.base + turn * self.per + count * self.unit
        if not (isinstance(value, int) and value == 0):
            eng.wait_ge(self.sem, value)


def start_signals(nc, signals):
    with nc.Block() as block:
        @block.gpsimd
        def _(pool):
            for s in signals:
                pool.sem_inc(s.sem, s.base)


class Steps:

    def __init__(self, sem, per):
        self.sem, self.per, self.n = sem, per, 0

    def did(self, ins):
        self.n += 1
        ins.then_inc(self.sem, 1)

    def wait(self, eng, turn):
        eng.wait_ge(self.sem, turn * self.per + self.n)

    def close(self, name):
        if self.n != self.per:
            raise ValueError(f"{name}: {self.n} steps")


class Tiles:

    def __init__(self, banks, filled, order, drained):
        self.banks, self.order, self.drained = banks, order, drained
        self.at = {key: n for n, key in enumerate(order)}
        self.filled = Signal(filled, len(order))
        self.slots = -(-len(order) // len(banks)) * len(banks)

    def bank(self, key):
        return self.banks[self.at[key] % len(self.banks)]

    def start(self, pe, turn, key, needs=()):
        n = self.at[key] - len(self.banks)
        if n >= 0:
            sig, count = self.drained(self.order[n])
        elif isinstance(turn, int):
            sig, count = None, 0
        else:
            n += self.slots
            n = n if n < len(self.order) else n - len(self.banks)
            sig, count = self.drained(self.order[n])[0], 0
        needs = list(needs)
        if sig and not any(s is sig and c >= count for s, c in needs):
            needs = [(s, c) for s, c in needs if s is not sig] + [(sig, count)]
        for s, c in needs:
            s.wait(pe, turn, c)
        return self.bank(key)

    def done(self, ins):
        ins.then_inc(self.filled.sem, 1)

    def wait(self, eng, turn, key):
        self.filled.wait(eng, turn, self.at[key] + 1)
        return self.bank(key)


def build_layer0(nc, t):
    with ExitStack() as ctx:
        def sb(name, shape, dt=F32):
            return ctx.enter_context(nc.sbuf_tensor("a_" + name, shape, dt))

        looped = []

        def signal(name, per, unit=1):
            s = Signal(ctx.enter_context(nc.semaphore("a_" + name)), per, unit, base=unit if per else 0)
            if per:
                looped.append(s)
            return s

        banks = [ctx.enter_context(nc.psum_tensor(f"a_bank{i}", [P, 512], F32)) for i in range(BANKS)]

        wq = sb("wq", [P, 2, KC, D])
        wk = sb("wk", [P, KC, KV0 * P])
        wv = sb("wv", [P, KC, KV0 * P])
        wo = sb("wo", [P, 2, REP, D])
        w1, w3 = wq[:, 0], wq[:, 1]
        wr = sb("wr", [P, KC, E0])
        wi = sb("wi", [P, 3 * KC, HX])
        wf = sb("wf", [P, 3 * KC, HX])
        bias = sb("bias", [P, 2])
        lnw = sb("lnw", [P, D])
        cos = sb("cos", [P, P])
        sin = sb("sin", [P, P])
        causal = sb("causal", [P, P])
        barred = sb("barred", [P, P])
        ident = sb("ident", [P, P])
        sel = sb("sel", [P, HX, P])
        iota = sb("iota", [P, E0])
        ones = sb("ones", [P, P])

        xg = sb("xg", [P, GB, D])
        xT = sb("xT", [P, KC, GT])
        cT = sb("cT", [P, KC, GT])
        scratch = sb("scratch", [P, 10240])
        kf = scratch[:, 0:2048].rearrange("p (j t) -> p j t", j=KV0)
        v = scratch[:, 2048:4096].rearrange("p (b t) -> p b t", b=GB)
        qf = scratch[:, 4096:8192].rearrange("p (u r t) -> p u r t", u=2, r=REP)
        st = scratch[:, 8192:10240].rearrange("p (b t) -> p b t", b=GB)
        scratch2 = sb("scratch2", [P, 8192])
        ot = scratch2[:, 0:2048].rearrange("p (b r t) -> p b r t", b=GB, r=REP)
        rt1 = scratch2[:, 2048:3072].rearrange("p (u t) -> p u t", u=2)
        rt2 = scratch2[:, 3072:4096].rearrange("p (u t) -> p u t", u=2)
        ry = scratch2[:, 4096:5120].rearrange("p (u t) -> p u t", u=2)
        ee = scratch2[:, 5120:6144].rearrange("p (u t) -> p u t", u=2)
        dn = scratch2[:, 7168:8192].rearrange("p (u t) -> p u t", u=2)
        xz = sb("xz", [P, 2, GB, HR, P])
        dec = scratch[:, 0:4096].rearrange("p (u r b s) -> p u r b s", u=2, r=HR, b=GB)
        cc = scratch[:, 4096:8192].rearrange("p (u b r s) -> p u b r s", u=2, b=GB, r=HR)
        hc = scratch2[:, 0:2048].rearrange("p (c b r e) -> p c b r e", c=KC, b=GB, r=HR)
        hs = scratch2[:, 2048:4096].rearrange("p (c b r e) -> p c b r e", c=KC, b=GB, r=HR)
        ho = scratch2[:, 4096:4096 + GB * HX * VS].rearrange("p (b h e) -> p b h e", b=GB, h=HX)
        va = sb("va", [P, GB * HX * VS + P - VS])
        ga = sb("ga", [P, GT])
        gi, gf, g1, g2 = (scratch[0:HX, 8192 + GT * n:8192 + GT * (n + 1)] for n in range(4))
        g3 = scratch2[0:HX, 0:GT]
        am = sb("am", [P, GB, 48])
        em = sb("em", [P, GB, HX])
        hn = sb("hn", [P, KC, GB, HR])
        hm = sb("hm", [P, KC, GB, HR])
        hr = sb("hr", [P, KC, GB, HR])
        h1 = scratch[:, 0:2048].rearrange("p (c t) -> p c t", c=KC)
        h2 = scratch[:, 2048:4096].rearrange("p (b t) -> p b t", b=GB)
        pr = sb("pr", [P, GB, E0])
        rmx = sb("rmx", [P, GB])
        top = sb("top", [P, GB, 8])
        topi = sb("topi", [P, GB, 8], U32)
        topf = sb("topf", [P, GB, 8])
        eq = sb("eq", [P, 2, E0])
        gate = sb("gate", [P, GB, E0])
        fsum = sb("fsum", [E0, D])
        pre = sb("pre", [E0, D])
        stats = sb("stats", [P, GB, 6])
        mom = sb("mom", [P, GB, 2])
        lnv = sb("lnv", [P, GB])
        rstd = sb("rstd", [P, GB])
        eps = sb("eps", [P, 2])
        held = sb("held", [P, 2])

        NF = KV0 + H0
        weights = signal("weights", 0, 16)
        late, NW, NL = signal("late", 0, 16), 6, 7
        wq_in = [signal(f"wq_in{u}", KV0 // 2 + 1, 16) for u in range(2)]
        wo_in = [signal(f"wo_in{u}", KV0 // 2, 16) for u in range(2)]
        x_in, xT_in, c_in, cT_in = (signal(n, 1, 16) for n in ("x_in", "xT_in", "c_in", "cT_in"))
        consts = signal("consts", 0)
        wsum = signal("wsum", 0)
        rope_parts, rope_sum = signal("rope_parts", NF), signal("rope_sum", NF)
        elu_parts, feature = signal("elu_parts", NF), signal("feature", NF)
        v_ready = signal("v_ready", GB)
        masked, den_copied = signal("masked", KV0 * GB), signal("den_copied", KV0 * GB)
        o_scaled, y_added = signal("o_scaled", KV0 * GB), signal("y_added", KV0 * GB)
        moments, rstd_ready, normed = signal("moments", 3), signal("rstd_ready", 3), signal("normed", 3 * GB)
        xT_ready = signal("xT_ready", 2 * KC)
        xz_spread, xz_ready = signal("xz_spread", KC * (HR - 1)), signal("xz_ready", KC)
        gates_copied, gate_abs, gate_log = signal("gates_copied", 1), signal("gate_abs", 1), signal("gate_log", 1)
        gates_ready, gt_copied = signal("gates_ready", 1), signal("gt_copied", 1)
        em_ready = signal("em_ready", 1)
        decay_arg, decay = signal("decay_arg", HX), signal("decay", HX)
        c_ready, ho_ready = signal("c_ready", KC * GB), signal("ho_ready", KC * GB)
        h_centred, h_squared = signal("h_centred", KC), signal("h_squared", KC)
        h_rstd, h_var = signal("h_rstd", 2), signal("h_var", 2)
        weighed = signal("weighed", KC - 1)
        rt_shift, rt_exp, routed = signal("rt_shift", 1), signal("rt_exp", 1), signal("routed", 1)
        h_ready = signal("h_ready", KC + GB)
        f_added, pre_ready = signal("f_added", 1), signal("pre_ready", 1)
        stored = signal("stored", 2, 16)
        fstored = signal("fstored", 0, 16)

        order = [("k", j) for j in range(KV0)] + [("v", b) for b in range(GB)]
        order += [("q", r) for r in range(REP)]
        for j in range(KV0):
            if j + 1 < KV0:
                order += [("q", REP * (j + 1) + r) for r in range(REP)]
            order += [("s", j, b) for b in range(GB)]
            if j:
                order += [("y", j - 1, b) for b in range(GB)]
            order += [(kind, j, b) for b in range(GB) for kind in ("d", "o")]
        order += [("y", KV0 - 1, b) for b in range(GB)]
        order += [("xt", 0, c) for c in range(KC)] + [("gate",), ("gt",)]
        order += [("cb", h) for h in range(HR)]
        for c in range(KC):
            if c + 1 < KC:
                order += [("cb", HR * (c + 1) + r) for r in range(HR)]
            order += [("qk", c, b) for b in range(GB)]
            if c:
                order += [("ho", c - 1, b) for b in range(GB)]
        order += [("ho", KC - 1, b) for b in range(GB)]
        order += [("xt", 1, c) for c in range(KC)] + [("rt",)]
        order += [("f1", c) for c in range(KC)] + [("f2", b) for b in range(GB)] + [("fa",)]

        def drained(key):
            kind, *n = key
            return {
                "k": lambda: (rope_parts, n[0] + 1),
                "v": lambda: (v_ready, n[0] + 1),
                "q": lambda: (rope_parts, KV0 + n[0] + 1),
                "s": lambda: (masked, GB * n[0] + n[1] + 1),
                "d": lambda: (den_copied, GB * n[0] + n[1] + 1),
                "o": lambda: (o_scaled, GB * n[0] + n[1] + 1),
                "y": lambda: (y_added, GB * n[0] + n[1] + 1),
                "xt": lambda: (xT_ready, KC * n[0] + n[1] + 1),
                "gate": lambda: (gates_copied, 1),
                "gt": lambda: (gt_copied, 1),
                "cb": lambda: (decay_arg, n[0] + 1),
                "qk": lambda: (c_ready, GB * n[0] + n[1] + 1),
                "ho": lambda: (ho_ready, GB * n[0] + n[1] + 1),
                "rt": lambda: (rt_shift, 1),
                "f1": lambda: (h_ready, n[0] + 1),
                "f2": lambda: (h_ready, KC + n[0] + 1),
                "fa": lambda: (f_added, 1),
            }[kind]()

        tiles = Tiles(banks, ctx.enter_context(nc.semaphore("a_filled")), order, drained)
        vstep = Steps(ctx.enter_context(nc.semaphore("a_vector_step")), 82)
        astep = Steps(ctx.enter_context(nc.semaphore("a_scalar_step")), 26)
        start_signals(nc, looped)
        block = ctx.enter_context(nc.Block())

        def weigh(eng, c):
            part = hc[:, c].rearrange("p b r e -> p b (r e)")
            cols = slice(P * c, P * (c + 1))
            return eng.tensor_tensor(part, part, lnw[:, cols].unsqueeze(1).broadcast_to([P, GB, P]), ALU.mult)

        def by_batch(ap):
            return ap.unsqueeze(1).broadcast_to([ap.shape[0], GB, P])

        @block.sync
        def _(sp):
            for dst, src in ((wk, "wk0"), (cos, "cos0"), (sin, "sin0"), (wi, "wi0"), (wf, "wf0"), (wv, "wv0")):
                sp.dma_start(dst[:], t[src]).then_inc(weights.sem, 16)
            sp.wait_ge(consts.sem, 10)
            with sp.Fori(0, GROUPS) as g:
                h_ready.wait(sp, g, 0)
                sp.dma_start(xT[:, :, :], t["xT"][g]).then_inc(xT_in.sem, 16)
                for j in range(2):
                    sp.dma_start(wq[:, j], t["wq0"][j]).then_inc(wq_in[j].sem, 16)
                    sp.dma_start(wo[:, j], t["wo0"][j]).then_inc(wo_in[j].sem, 16)
                sp.dma_start(cT[:, :, :], t["cT"][g]).then_inc(cT_in.sem, 16)
                sp.dma_start(va[:, 0:GB * HX * VS].rearrange("p (n e) -> p n e", e=VS)[:, :, 0:HD],
                             t["c"][g].rearrange("p b (h e) -> p (b h) e", e=HD)).then_inc(c_in.sem, 16)
                stored.wait(sp, g, 0)
                sp.dma_start(xg[:, :, :], t["x"][g]).then_inc(x_in.sem, 16)
                for j in range(2, KV0 + 2):
                    feature.wait(sp, g, KV0 + REP * (j - 1))
                    src = t["wq0"][j] if j < KV0 else t[("w10", "w30")[j - KV0]]
                    sp.dma_start(wq[:, j % 2], src).then_inc(wq_in[j % 2].sem, 16)
                    if j < KV0:
                        y_added.wait(sp, g, GB * (j - 1))
                        sp.dma_start(wo[:, j % 2], t["wo0"][j]).then_inc(wo_in[j % 2].sem, 16)
            f_added.wait(sp, GROUPS, 0)
            sp.dma_start(t["fsum"], fsum[:, :]).then_inc(fstored.sem, 16)
            sp.wait_ge(fstored.sem, 16)
            stored.wait(sp, GROUPS, 0)

        @block.gpsimd
        def _(pool):
            pool.memset(ident[:, :], 0.0).then_inc(consts.sem, 1)
            pool.memset(ones[:, :], 1.0).then_inc(consts.sem, 1)
            pool.memset(xz[:], 0.0).then_inc(consts.sem, 1)
            pool.memset(va[:], 1.0).then_inc(consts.sem, 1)
            pool.memset(ga[:], 0.0).then_inc(consts.sem, 1)
            pool.memset(fsum[:], 0.0).then_inc(consts.sem, 1)
            pool.memset(eps[:, 0:1], EPS_LN).then_inc(consts.sem, 1)
            pool.memset(eps[:, 1:2], EPS_MLSTM).then_inc(consts.sem, 1)
            pool.memset(held[:], 0.0).then_inc(consts.sem, 1)
            pool.wait_ge(consts.sem, 9)
            pool.affine_select(out=ident[:, :], in_=ident[:, :], compare_op=ALU.not_equal, fill=1.0,
                               base=0, pattern=[[-1, P]], channel_multiplier=1).then_inc(consts.sem, 1)
            pool.wait_ge(consts.sem, 10)
            pool.wait_ge(weights.sem, 16 * NW)
            for w in (wi, wf):
                pool.tensor_tensor(w[:, KC:2 * KC, :], w[:, KC:2 * KC, :], w[:, 2 * KC:3 * KC, :],
                                   ALU.add).then_inc(wsum.sem, 1)
            pool.wait_ge(wsum.sem, 2)
            with pool.Fori(0, GROUPS) as g:
                xz_ready.wait(pool, g, 0)

                def rope(n):
                    rope_parts.wait(pool, g, n + 1)
                    feature.wait(pool, g, max(n - 1, 0))
                    pool.tensor_tensor(ry[:, n % 2, :], rt1[:, n % 2, :], rt2[:, n % 2, :],
                                       ALU.add).then_inc(rope_sum.sem, 1)

                for n in range(NF):
                    rope(n)
                for c in range(KC):
                    xT_ready.wait(pool, g, c + 1)
                    c_ready.wait(pool, g, GB * max(c - 1, 0))
                    for r in range(HR):
                        rows = slice(HD * r, HD * r + HD)
                        src = xT[rows, c, :].rearrange("p (b s) -> p b s", b=GB)
                        if r == 0:
                            xz_ready.wait(pool, g, c)
                        else:
                            xz_spread.wait(pool, g, (HR - 1) * c + r)
                        ins = pool.tensor_tensor(xz[rows, c % 2, :, r, :], src, by_batch(ones[rows, :]), ALU.mult)
                        ins.then_inc(xz_ready.sem if r == HR - 1 else xz_spread.sem, 1)
                pool.wait_ge(late.sem, 16 * NL)
                xz_ready.wait(pool, g, KC)
                for c in range(KC - 1):
                    h_squared.wait(pool, g, c + 1)
                    weigh(pool, c).then_inc(weighed.sem, 1)

        @block.scalar
        def _(act):
            act.wait_ge(weights.sem, 16 * NW)
            for dst, src in ((causal, "causal"), (bias, "bias0"), (barred, "barred"), (sel, "sel"), (lnw, "lnw0"),
                             (wr, "wr0"), (iota, "iota")):
                act.dma_start(dst[:], t[src]).then_inc(late.sem, 16)
            act.wait_ge(consts.sem, 10)
            with act.Fori(0, GROUPS) as g:
                astep.n = 0

                def elu(n):
                    rope_sum.wait(act, g, n + 1)
                    feature.wait(act, g, max(n - 1, 0))
                    astep.did(act.activation(ee[:, n % 2, :], ry[:, n % 2, :], ACT.Relu, scale=-1.0))
                    astep.wait(act, g)
                    act.activation(ee[:, n % 2, :], ee[:, n % 2, :], ACT.Exp, scale=-1.0).then_inc(elu_parts.sem, 1)

                def norm(i):
                    moments.wait(act, g, i + 1)
                    astep.did(act.activation(lnv[:, :], mom[:, :, 1], ACT.Ln, bias=eps[:, 0:1]))
                    astep.wait(act, g)
                    act.activation(rstd[:, :], lnv[:, :], ACT.Exp, scale=-0.5).then_inc(rstd_ready.sem, 1)

                def turned(i):
                    for c in range(KC):
                        bank = tiles.wait(act, g, ("xt", i, c))
                        if i == 1:
                            xz_ready.wait(act, g, KC)
                        act.activation(xT[:, c, :], bank[:, :], ACT.Copy).then_inc(xT_ready.sem, 1)

                for j in range(KV0):
                    elu(j)
                for b in range(GB):
                    bank = tiles.wait(act, g, ("v", b))
                    act.activation(v[:, b, :], bank[:, :], ACT.Copy).then_inc(v_ready.sem, 1)
                for r in range(REP):
                    elu(KV0 + r)
                for j in range(KV0):
                    if j + 1 < KV0:
                        for r in range(REP):
                            elu(KV0 + REP * (j + 1) + r)
                    for b in range(GB):
                        n = GB * j + b
                        bank = tiles.wait(act, g, ("d", j, b))
                        o_scaled.wait(act, g, max(n - 1, 0))
                        act.activation(dn[:, n % 2, :], bank[:, :], ACT.Copy,
                                       bias=EPS_DEN).then_inc(den_copied.sem, 1)
                norm(0)
                turned(0)
                act.wait_ge(late.sem, 16 * NL)
                bank = tiles.wait(act, g, ("gate",))
                act.activation(gi[:, :], bank[0:HX, :], ACT.Identity, bias=bias[0:HX, 0:1])
                act.activation(gf[:, :], bank[32:32 + HX, :], ACT.Identity,
                               bias=bias[32:32 + HX, 0:1]).then_inc(gates_copied.sem, 1)
                gate_abs.wait(act, g, 1)
                astep.did(act.activation(g2[:, :], g2[:, :], ACT.Exp, scale=-1.0))
                astep.wait(act, g)
                act.activation(g2[:, :], g2[:, :], ACT.Ln, bias=1.0).then_inc(gate_log.sem, 1)
                gt_copied.wait(act, g, 1)
                act.activation(em[:, :, :], am[:, :, 32:48], ACT.Exp).then_inc(em_ready.sem, 1)

                def decays(c):
                    for r in range(HR):
                        decay_arg.wait(act, g, HR * c + r + 1)
                        act.activation(dec[:, c % 2, r, :, :], dec[:, c % 2, r, :, :], ACT.Exp,
                                       scale=-1.0).then_inc(decay.sem, 1)

                def heads(c):
                    for b in range(GB):
                        bank = tiles.wait(act, g, ("ho", c, b))
                        act.activation(ho[:, b, HR * c:HR * c + HR, :],
                                       bank[:, :].rearrange("p (r e) -> p r e", r=HR)[:, :, 0:VS],
                                       ACT.Copy).then_inc(ho_ready.sem, 1)

                def squares(c):
                    h_centred.wait(act, g, c + 1)
                    act.activation(hs[:, c], hc[:, c], ACT.Square).then_inc(h_squared.sem, 1)

                decays(0)
                for c in range(KC):
                    if c + 1 < KC:
                        decays(c + 1)
                    if c:
                        heads(c - 1)
                    if c > 1:
                        squares(c - 2)

                def head_roots(i, chunks):
                    h_var.wait(act, g, i + 1)
                    astep.did(act.activation(hr[:, chunks], hr[:, chunks], ACT.Ln, scale=1.0 / HD, bias=eps[:, 1:2]))
                    astep.wait(act, g)
                    act.activation(hr[:, chunks], hr[:, chunks], ACT.Exp, scale=-0.5).then_inc(h_rstd.sem, 1)

                squares(KC - 2)
                heads(KC - 1)
                head_roots(0, slice(0, KC - 1))
                squares(KC - 1)
                head_roots(1, slice(KC - 1, KC))
                norm(1)
                turned(1)
                rt_shift.wait(act, g, 1)
                act.activation(pr[:], pr[:], ACT.Exp).then_inc(rt_exp.sem, 1)
                for n in range(KC + GB):
                    bank = tiles.wait(act, g, ("f1", n) if n < KC else ("f2", n - KC))
                    out = h1[:, n, :] if n < KC else h2[:, n - KC, :]
                    act.activation(out, bank[:, :], ACT.Silu).then_inc(h_ready.sem, 1)
                norm(2)
                pre_ready.wait(act, g, 1)
                act.dma_start(t["pre"][g], pre[:, :]).then_inc(stored.sem, 16)
                normed.wait(act, g, 3 * GB)
                act.dma_start(t["x3"][g], xg[:, :, :]).then_inc(stored.sem, 16)
            astep.close("layer 0, scalar")

        @block.tensor
        def _(pe):
            pe.wait_ge(weights.sem, 16 * NW)

            with pe.Fori(0, GROUPS) as g:
                def chunks(key, lhs, rhs, n=KC, needs=()):
                    bank = tiles.start(pe, g, key, needs)
                    for c in range(n):
                        ins = pe.matmul(bank[:, :], lhs(c), rhs(c), start=(c == 0), stop=(c == n - 1))
                    tiles.done(ins)

                def queries(j):
                    wq_in[j % 2].wait(pe, g, j // 2 + 1)
                    for r in range(REP):
                        h = REP * j + r
                        chunks(("q", h), lambda c: wq[:, j % 2, c, r * P:(r + 1) * P], lambda c: xT[:, c, :])

                def outputs(j):
                    wo_in[j % 2].wait(pe, g, j // 2 + 1)
                    for b in range(GB):
                        chunks(("y", j, b), lambda r: ot[:, b, r, :], lambda r: wo[:, j % 2, r, :], REP,
                               [(o_scaled, GB * j + b + 1)])

                def turn_x(i):
                    for c in range(KC):
                        bank = tiles.start(pe, g, ("xt", i, c))
                        for b in range(GB):
                            if c == 0:
                                normed.wait(pe, g, GB * i + b + 1)
                            ins = pe.transpose(bank[:, b * P:(b + 1) * P], xg[:, b, c * P:(c + 1) * P], ident[:, :])
                        tiles.done(ins)

                xT_in.wait(pe, g, 1)
                for j in range(KV0):
                    chunks(("k", j), lambda c: wk[:, c, j * P:(j + 1) * P], lambda c: xT[:, c, :])
                for b in range(GB):
                    chunks(("v", b), lambda c: xT[:, c, b * P:(b + 1) * P], lambda c: wv[:, c, :])
                queries(0)
                for j in range(KV0):
                    if j + 1 < KV0:
                        queries(j + 1)
                    for b in range(GB):
                        cols = slice(b * P, (b + 1) * P)
                        bank = tiles.start(pe, g, ("s", j, b), [(feature, KV0 + REP * (j + 1))])
                        tiles.done(pe.matmul(bank[:, :], kf[:, j, cols], qf[:, j % 2, :, cols],
                                             start=True, stop=True))
                    if j:
                        outputs(j - 1)
                    v_ready.wait(pe, g, GB)
                    for b in range(GB):
                        bank = tiles.start(pe, g, ("d", j, b), [(masked, GB * j + b + 1)])
                        tiles.done(pe.matmul(bank[:, :], ones[:, :], st[:, b, :], start=True, stop=True))
                        bank = tiles.start(pe, g, ("o", j, b))
                        tiles.done(pe.matmul(bank[:, :], v[:, b, j * P:(j + 1) * P], st[:, b, :],
                                             start=True, stop=True))
                outputs(KV0 - 1)

                turn_x(0)
                bank = tiles.start(pe, g, ("gate",), [(xT_ready, KC)])
                cT_in.wait(pe, g, 1)
                pe.wait_ge(wsum.sem, 2)
                for at, w in ((0, wi), (32, wf)):
                    for c in range(2 * KC):
                        src = xT[:, c, :] if c < KC else cT[:, c - KC, :]
                        ins = pe.matmul(bank[at:at + HX, :], w[:, c, :], src, start=(c == 0), stop=(c == 2 * KC - 1))
                tiles.done(ins)
                gates_ready.wait(pe, g, 1)
                bank = tiles.start(pe, g, ("gt",))
                for b in range(GB):
                    ins = pe.transpose(bank[:, b * P:(b + 1) * P], ga[:, b * P:(b + 1) * P], ident[:, :])
                tiles.done(ins)

                pe.wait_ge(late.sem, 16 * NL)

                def spread(c):
                    for r in range(HR):
                        h = HR * c + r
                        bank = tiles.start(pe, g, ("cb", h))
                        tiles.done(pe.matmul(bank[:, :], sel[:, h, :], ga[:, :], start=True, stop=True))

                def values(c):
                    c_in.wait(pe, g, 1)
                    for b in range(GB):
                        bank = tiles.start(pe, g, ("ho", c, b), [(c_ready, GB * c + b + 1)])
                        for r in range(HR):
                            at = VS * (HX * b + HR * c + r)
                            ins = pe.matmul(bank[:, r * P:(r + 1) * P], cc[:, c % 2, b, r, :],
                                            va[:, at:at + P], start=True, stop=True)
                        tiles.done(ins)

                spread(0)
                for c in range(KC):
                    if c + 1 < KC:
                        spread(c + 1)
                    xz_ready.wait(pe, g, c + 1)
                    for b in range(GB):
                        bank = tiles.start(pe, g, ("qk", c, b))
                        tiles.done(pe.matmul(bank[:, :], cT[:, c, b * P:(b + 1) * P], xz[:, c % 2, b, :, :],
                                             start=True, stop=True))
                    if c:
                        values(c - 1)
                values(KC - 1)

                turn_x(1)
                bank = tiles.start(pe, g, ("rt",), [(xT_ready, 2 * KC)])
                for b in range(GB):
                    for c in range(KC):
                        ins = pe.matmul(bank[:, b * E0:(b + 1) * E0], xT[:, c, b * P:(b + 1) * P], wr[:, c, :],
                                        start=(c == 0), stop=(c == KC - 1))
                tiles.done(ins)
                wq_in[0].wait(pe, g, KV0 // 2 + 1)
                for i in range(KC):
                    chunks(("f1", i), lambda c: w1[:, c, i * P:(i + 1) * P], lambda c: xT[:, c, :])
                wq_in[1].wait(pe, g, KV0 // 2 + 1)
                for b in range(GB):
                    chunks(("f2", b), lambda c: h1[:, c, b * P:(b + 1) * P], lambda c: w3[:, c, :],
                           needs=[(h_ready, KC)])
                routed.wait(pe, g, 1)
                bank = tiles.start(pe, g, ("fa",), [(h_ready, KC + GB)])
                for b in range(GB):
                    ins = pe.matmul(bank[0:E0, :], gate[:, b, :], h2[:, b, :], start=(b == 0), stop=(b == GB - 1))
                tiles.done(ins)

        @block.vector
        def _(dve):
            dve.wait_ge(weights.sem, 16 * NW)
            dve.wait_ge(consts.sem, 10)
            with dve.Fori(0, GROUPS) as g:
                vstep.n = 0

                def parts(n):
                    bank = tiles.wait(dve, g, ("k", n) if n < KV0 else ("q", n - KV0))
                    rope_sum.wait(dve, g, max(n - 1, 0))
                    view = bank[:, :].rearrange("p (b s) -> p b s", b=GB)
                    u = n % 2
                    dve.tensor_tensor(rt1[:, u, :].rearrange("p (b s) -> p b s", b=GB), view,
                                      by_batch(cos[:, :]), ALU.mult)
                    for to, of in ((0, 64), (64, 0)):
                        ins = dve.tensor_tensor(
                            rt2[to:to + 64, u, :].rearrange("p (b s) -> p b s", b=GB), view[of:of + 64],
                            by_batch(sin[of:of + 64, :]), ALU.mult)
                    ins.then_inc(rope_parts.sem, 1)

                def features(n):
                    elu_parts.wait(dve, g, n + 1)
                    j, r = divmod(n - KV0, REP)
                    out = kf[:, n, :] if n < KV0 else qf[:, j % 2, r, :]
                    dve.scalar_tensor_tensor(out, ry[:, n % 2, :], 0.0, ee[:, n % 2, :], ALU.max,
                                             ALU.add).then_inc(feature.sem, 1)

                def run_of(first, count):
                    for n in range(first, first + count):
                        parts(n)
                        if n > first:
                            features(n - 1)
                    features(first + count - 1)

                def added(j):
                    for b in range(GB):
                        bank = tiles.wait(dve, g, ("y", j, b))
                        if j:
                            y_added.wait(dve, g, GB * (j - 1) + b + 1)
                        dve.tensor_tensor(xg[:, b, :], bank[:, :], xg[:, b, :], ALU.add).then_inc(y_added.sem, 1)

                def norm(i, last):
                    last()
                    for b in range(GB):
                        ins = dve.bn_stats(stats[:, b, :], xg[:, b, :])
                    vstep.did(ins)
                    vstep.wait(dve, g)
                    dve.tensor_copy(held[:, 1:2], held[:, 0:1])
                    for b in range(GB):
                        ins = dve.bn_aggr(mom[:, b, :], stats[:, b, :])
                    ins.then_inc(moments.sem, 1)
                    rstd_ready.wait(dve, g, i + 1)
                    for b in range(GB):
                        dve.tensor_scalar(xg[:, b, :], xg[:, b, :], mom[:, b, 0:1], rstd[:, b:b + 1],
                                          ALU.subtract, ALU.mult).then_inc(normed.sem, 1)

                run_of(0, KV0)
                run_of(KV0, REP)
                x_in.wait(dve, g, 1)
                dve.wait_ge(late.sem, 16 * NL)
                for j in range(KV0):
                    if j + 1 < KV0:
                        run_of(KV0 + REP * (j + 1), REP)
                    for b in range(GB):
                        bank = tiles.wait(dve, g, ("s", j, b))
                        dve.tensor_tensor(st[:, b, :].rearrange("p (r q) -> p r q", r=REP),
                                          bank[:, :].rearrange("p (r q) -> p r q", r=REP),
                                          by_batch(causal[:, :]), ALU.mult).then_inc(masked.sem, 1)
                    if j:
                        added(j - 1)
                    for b in range(GB):
                        n = GB * j + b
                        den_copied.wait(dve, g, n + 1)
                        vstep.did(dve.reciprocal(dn[:, n % 2, :], dn[:, n % 2, :]))
                        vstep.wait(dve, g)
                        bank = tiles.wait(dve, g, ("o", j, b))
                        dve.tensor_tensor(ot[:, b, :, :], bank[:, :].rearrange("p (r q) -> p r q", r=REP),
                                          dn[:, n % 2, :].rearrange("p (r q) -> p r q", r=REP),
                                          ALU.mult).then_inc(o_scaled.sem, 1)
                added(KV0 - 1)
                norm(0, lambda: y_added.wait(dve, g, KV0 * GB))

                gates_copied.wait(dve, g, 1)
                vstep.did(dve.tensor_scalar(g1[:, :], gf[:, :], 0.0, None, ALU.min))
                dve.scalar_tensor_tensor(g2[:, :], gf[:, :], -1.0, gf[:, :], ALU.mult,
                                         ALU.max).then_inc(gate_abs.sem, 1)
                gate_log.wait(dve, g, 1)
                vstep.wait(dve, g)
                vstep.did(dve.tensor_tensor(g1[:, :], g1[:, :], g2[:, :], ALU.subtract))
                vstep.wait(dve, g)
                for b in range(GB):
                    cols = slice(b * P, (b + 1) * P)
                    ins = dve.tensor_tensor_scan(g3[:, cols], ones[0:HX, :], g1[:, cols], 0.0, ALU.mult, ALU.add)
                vstep.did(ins)
                vstep.wait(dve, g)
                vstep.did(dve.tensor_tensor(ga[0:HX, :], gi[:, :], g3[:, :], ALU.subtract))
                vstep.wait(dve, g)
                for b in range(GB):
                    cols = slice(b * P, (b + 1) * P)
                    ins = dve.tensor_tensor_scan(g1[:, cols], ones[0:HX, :], ga[0:HX, cols], -3e38,
                                                 ALU.mult, ALU.max)
                vstep.did(ins)
                vstep.wait(dve, g)
                dve.scalar_tensor_tensor(ga[32:32 + HX, :], g3[:, :], -1.0, g1[:, :], ALU.mult, ALU.subtract)
                dve.tensor_copy(ga[64:64 + HX, :], g1[:, :]).then_inc(gates_ready.sem, 1)
                bank = tiles.wait(dve, g, ("gt",))
                dve.tensor_copy(am[:, :, :], bank[:, :].rearrange("p (b n) -> p b n", b=GB)[:, :, 0:48])\
                   .then_inc(gt_copied.sem, 1)
                gt_copied.wait(dve, g, 1)

                def decay_args(c):
                    c_ready.wait(dve, g, GB * max(c - 1, 0))
                    for r in range(HR):
                        h = HR * c + r
                        bank = tiles.wait(dve, g, ("cb", h))
                        for b in range(GB):
                            ins = dve.scalar_tensor_tensor(
                                dec[:, c % 2, r, b, :], bank[:, b * P:(b + 1) * P], am[:, b, h:h + 1],
                                barred[:, :], ALU.subtract, ALU.max)
                        ins.then_inc(decay_arg.sem, 1)

                def chained(ins):
                    vstep.did(ins)
                    vstep.wait(dve, g)

                def wide(ap):
                    return ap.unsqueeze(3).broadcast_to([P, GB, HR, HD])

                def heads(c):
                    ho_ready.wait(dve, g, GB * (c + 1))
                    part = ho[:, :, HR * c:HR * c + HR, :]
                    chained(dve.tensor_copy(hm[:, c], part[:, :, :, HD]))
                    chained(dve.scalar_tensor_tensor(hn[:, c], hm[:, c], -1.0, hm[:, c], ALU.mult, ALU.max))
                    if c == 0:
                        em_ready.wait(dve, g, 1)
                    chained(dve.tensor_tensor(hn[:, c], hn[:, c], em[:, :, HR * c:HR * c + HR], ALU.max))
                    chained(dve.tensor_scalar(hn[:, c], hn[:, c], EPS_MLSTM, None, ALU.add))
                    chained(dve.reciprocal(hn[:, c], hn[:, c]))
                    chained(dve.tensor_tensor(hc[:, c], part[:, :, :, 0:HD], wide(hn[:, c]), ALU.mult))
                    chained(dve.tensor_reduce(hm[:, c], hc[:, c], AX.X, ALU.add))
                    chained(dve.tensor_scalar(hm[:, c], hm[:, c], 1.0 / HD, None, ALU.mult))
                    dve.tensor_tensor(hc[:, c], hc[:, c], wide(hm[:, c]), ALU.subtract).then_inc(h_centred.sem, 1)

                def variance(c):
                    h_squared.wait(dve, g, c + 1)
                    ins = dve.tensor_reduce(hr[:, c], hs[:, c], AX.X, ALU.add)
                    if c == KC - 1:
                        vstep.did(weigh(dve, c))
                    return ins

                def add_heads(chunks):
                    for c in chunks:
                        vstep.did(dve.tensor_tensor(hc[:, c], hc[:, c], wide(hr[:, c]), ALU.mult))
                    for c in chunks:
                        vstep.wait(dve, g)
                        cols = slice(P * c, P * (c + 1))
                        vstep.did(dve.tensor_tensor(xg[:, :, cols], xg[:, :, cols],
                                                    hc[:, c].rearrange("p b r e -> p b (r e)"), ALU.add))

                decay_args(0)
                for c in range(KC):
                    if c + 1 < KC:
                        decay_args(c + 1)
                    decay.wait(dve, g, HR * (c + 1))
                    for b in range(GB):
                        bank = tiles.wait(dve, g, ("qk", c, b))
                        dve.scalar_tensor_tensor(
                            cc[:, c % 2, b, :, :], bank[:, :].rearrange("p (r s) -> p r s", r=HR),
                            float(HD) ** -0.5, dec[:, c % 2, :, b, :], ALU.mult, ALU.mult).then_inc(c_ready.sem, 1)
                    if c:
                        heads(c - 1)
                    if c > 1:
                        variance(c - 2)
                variance(KC - 2).then_inc(h_var.sem, 1)
                heads(KC - 1)
                h_rstd.wait(dve, g, 1)
                weighed.wait(dve, g, KC - 1)
                add_heads(range(KC - 1))
                variance(KC - 1).then_inc(h_var.sem, 1)
                h_rstd.wait(dve, g, 2)
                vstep.wait(dve, g)
                add_heads(range(KC - 1, KC))
                vstep.wait(dve, g)
                norm(1, lambda: None)

                normed.wait(dve, g, 2 * GB)
                stored.wait(dve, g, 0)
                dve.tensor_copy(pre[:, :], xg[0:E0, 0, :]).then_inc(pre_ready.sem, 1)

                def each(ap):
                    return ap.unsqueeze(2).broadcast_to([P, GB, E0])

                bank = tiles.wait(dve, g, ("rt",))
                logits = bank[:, 0:GB * E0].rearrange("p (b e) -> p b e", b=GB)
                chained(dve.tensor_reduce(rmx[:, :], logits, AX.X, ALU.max))
                dve.tensor_tensor(pr[:, :, :], logits, each(rmx[:, :]), ALU.subtract).then_inc(rt_shift.sem, 1)
                rt_exp.wait(dve, g, 1)
                chained(dve.tensor_reduce(rmx[:, :], pr[:, :, :], AX.X, ALU.add))
                chained(dve.reciprocal(rmx[:, :], rmx[:, :]))
                chained(dve.tensor_tensor(pr[:, :, :], pr[:, :, :], each(rmx[:, :]), ALU.mult))
                dve.tensor_copy(held[:, 1:2], held[:, 0:1])
                for b in range(GB):
                    ins = dve.max(top[:, b, :], pr[:, b, :])
                chained(ins)
                dve.tensor_copy(held[:, 1:2], held[:, 0:1])
                for b in range(GB):
                    ins = dve.max_index(topi[:, b, :], top[:, b, :], pr[:, b, :])
                chained(ins)
                chained(dve.tensor_copy(topf[:, :, :], topi[:, :, :]))
                chained(dve.tensor_tensor(rmx[:, :], top[:, :, 0], top[:, :, 1], ALU.add))
                chained(dve.reciprocal(rmx[:, :], rmx[:, :]))
                chained(dve.tensor_tensor(top[:, :, 0:2], top[:, :, 0:2],
                                          rmx[:, :].unsqueeze(2).broadcast_to([P, GB, 2]), ALU.mult))
                for b in range(GB):
                    for k in range(2):
                        ins = dve.tensor_scalar(eq[:, k, :], iota[:, :], topf[:, b, k:k + 1], top[:, b, k:k + 1],
                                                ALU.is_equal, ALU.mult)
                    chained(ins)
                    ins = dve.tensor_tensor(gate[:, b, :], eq[:, 0, :], eq[:, 1, :], ALU.add)
                    if b < GB - 1:
                        chained(ins)
                ins.then_inc(routed.sem, 1)

                bank = tiles.wait(dve, g, ("fa",))
                dve.tensor_tensor(fsum[:, :], bank[0:E0, :], fsum[:, :], ALU.add).then_inc(f_added.sem, 1)
                norm(2, lambda: None)
            vstep.close("layer 0, vector")


def build_row_fix(nc, t):
    with ExitStack() as ctx:
        def sb(name, shape, dt=F32):
            return ctx.enter_context(nc.sbuf_tensor("b_" + name, shape, dt))

        w2, fs, ft = sb("w2", [P, KC, D]), sb("fs", [P, D]), sb("ft", [P, KC, P])
        ident, rows = sb("ident", [P, P]), sb("rows", [E0, D])
        stats, mom, rstd, eps = sb("stats", [E0, 6]), sb("mom", [E0, 2]), sb("rstd", [E0, 1]), sb("eps", [E0, 1])
        bank = ctx.enter_context(nc.psum_tensor("b_bank", [P, 512], F32))
        out = ctx.enter_context(nc.psum_tensor("b_out", [P, 512], F32))
        cleared, loaded, turned, copied, product, fixed, scaled, stored = (
            ctx.enter_context(nc.semaphore("b_" + n))
            for n in ("cleared", "loaded", "turned", "copied", "product", "fixed", "scaled", "stored"))
        step = ctx.enter_context(nc.semaphore("b_step"))
        block = ctx.enter_context(nc.Block())

        @block.sync
        def _(sp):
            sp.dma_start(w2[:], t["w20"]).then_inc(loaded, 16)
            sp.dma_start(ident[:], t["ident"]).then_inc(loaded, 16)
            sp.dma_start(rows[:], t["pre"][0]).then_inc(loaded, 16)
            sp.wait_ge(cleared, 2)
            sp.dma_start(fs[0:E0, :], t["fsum"]).then_inc(loaded, 16)
            sp.wait_ge(step, 5)
            sp.dma_start(t["x3"][0][0:E0, 0, :], rows[:]).then_inc(stored, 16)
            sp.wait_ge(stored, 16)

        @block.gpsimd
        def _(pool):
            pool.memset(fs[:], 0.0).then_inc(cleared, 1)
            pool.memset(eps[:], EPS_LN).then_inc(cleared, 1)

        @block.tensor
        def _(pe):
            pe.wait_ge(loaded, 64)
            for c in range(KC):
                ins = pe.transpose(bank[:, c * P:(c + 1) * P], fs[:, c * P:(c + 1) * P], ident[:, :])
            ins.then_inc(turned, 1)
            pe.wait_ge(copied, 1)
            for c in range(KC):
                ins = pe.matmul(out[:, :], ft[:, c, :], w2[:, c, :], start=(c == 0), stop=(c == KC - 1))
            ins.then_inc(product, 1)

        @block.vector
        def _(dve):
            dve.wait_ge(turned, 1)
            dve.tensor_copy(ft[:].rearrange("p c t -> p (c t)"), bank[:, :]).then_inc(copied, 1)
            dve.wait_ge(product, 1)
            dve.tensor_tensor(rows[:, :], out[0:E0, :], rows[:, :], ALU.add).then_inc(step, 1)
            dve.wait_ge(step, 1)
            dve.bn_stats(stats[:, :], rows[:, :]).then_inc(step, 1)
            dve.wait_ge(step, 2)
            dve.bn_aggr(mom[:, :], stats[:, :]).then_inc(step, 1)
            dve.wait_ge(scaled, 2)
            dve.tensor_scalar(rows[:, :], rows[:, :], mom[:, 0:1], rstd[:, 0:1],
                              ALU.subtract, ALU.mult).then_inc(step, 2)

        @block.scalar
        def _(act):
            act.wait_ge(cleared, 2)
            act.wait_ge(step, 3)
            act.activation(rstd[:, :], mom[:, 1:2], ACT.Ln, bias=eps[:, 0:1]).then_inc(scaled, 1)
            act.wait_ge(scaled, 1)
            act.activation(rstd[:, :], rstd[:, :], ACT.Exp, scale=-0.5).then_inc(scaled, 1)


def build_layer1(nc, t):
    with ExitStack() as ctx:
        def sb(name, shape, dt=F32):
            return ctx.enter_context(nc.sbuf_tensor("c_" + name, shape, dt))

        looped = []

        def signal(name, per, unit=1):
            s = Signal(ctx.enter_context(nc.semaphore("c_" + name)), per, unit, base=unit if per else 0)
            if per:
                looped.append(s)
            return s

        PARTS = 3
        TERMS = ((0, 0), (0, 1), (1, 0), (1, 1), (0, 2), (2, 0))
        TR = len(TERMS) * CD
        SR = TR + PARTS
        LC = D // P

        pair_banks = [ctx.enter_context(nc.psum_tensor(f"c_pair{i}", [P, 1024], F32)) for i in range(2)]
        banks = [ctx.enter_context(nc.psum_tensor(f"c_bank{i}", [P, 512], F32)) for i in range(3)]
        pv = ctx.enter_context(nc.psum_tensor("c_pv", [P, 512], F32))

        wq, wk, wv, wo = (sb(n, [P, KC, D]) for n in ("wq", "wk", "wv", "wo"))
        cos, sin = sb("cos", [P, CD]), sb("sin", [P, CD])
        decay = sb("decay", [P, HX, P])
        rmsw = sb("rmsw", [P, KC])
        gamma = sb("gamma", [P, 1])
        ident, ones = sb("ident", [P, P]), sb("ones", [P, P])
        eps = sb("eps", [P, 1])
        held = sb("held", [P, 2])

        xin, xg = sb("xin", [P, GB, D]), sb("xg", [P, GB, D])
        area = sb("area", [P, 20480])
        yq = area[:, 0:2048].rearrange("p (b n) -> p b n", b=GB)
        yk = area[:, 2048:4096].rearrange("p (b n) -> p b n", b=GB)
        v = area[:, 4096:6144].rearrange("p (b n) -> p b n", b=GB)
        kT = area[:, 6144:8192].rearrange("p (b c n) -> p b c n", b=GB, c=KC)
        qT = area[:, 8192:10240].rearrange("p (b c n) -> p b c n", b=GB, c=KC)
        sm = area[:, 10240:14336].rearrange("p (u c r q) -> p u c r q", u=2, c=KC, r=HR)
        sq = yq.rearrange("p b (c q) -> p b c q", c=KC)
        at = yk.rearrange("p b (c q) -> p b c q", c=KC)
        r1 = area[:, 16384:17408].rearrange("p (u n) -> p u n", u=2)
        r2 = area[:, 17408:18432].rearrange("p (u n) -> p u n", u=2)
        xT = area[:, 18432:20480].rearrange("p (c t) -> p c t", c=KC)
        xz = sb("xz", [P, 2, KC, HR, P])
        RING = 6
        QUAD = 4
        probs = area[:, 0:12288].rearrange("p (n l q) -> p n l q", n=RING, l=LC)
        ov = area[:, 12288:13312].rearrange("p (o n) -> p o n", o=2)
        fin = area[:, 13312:14336].rearrange("p (o n) -> p o n", o=2)
        kp = area[:, 14336:15872].bitcast(BF16).rearrange("p (u k n) -> p u k n", u=2, k=PARTS)
        cres = area[:, 15872:16384]
        cT = area[:, 16384:18432].rearrange("p (l t) -> p l t", l=LC)
        qp = area[:, 18432:19968].bitcast(BF16).rearrange("p (u k n) -> p u k n", u=2, k=PARTS)
        qres = area[:, 19968:20480]
        cgr = sb("cgr", [P, GB, D])
        mx = sb("mx", [P, 2, P])
        mrow = sb("mrow", [P, P])
        qs = sb("qs", [P, 2, CH, D], BF16)
        ks = sb("ks", [P, 2, CH, D], BF16)
        mp = sb("mp", [P, 2, PARTS, P], BF16)
        vflat = sb("vt", [P, LC * GB * CH * (CD + 1) + 32 - CD - 1])
        vt = vflat[:, 0:LC * GB * CH * (CD + 1)].rearrange("p (l b h e) -> p l b h e", l=LC, b=GB, h=CH)
        stats, mom = sb("stats", [P, GB, 6]), sb("mom", [P, GB, 2])
        rstd, lnv, rms = sb("rstd", [P, GB]), sb("lnv", [P, GB]), sb("rms", [P, GB])

        NW, NL, NC = 5, 4, 8
        ident_in, weights, late = (signal(n, 0, 16) for n in ("ident_in", "weights", "late"))
        consts = signal("consts", 0)
        x_in, c_in, cT_in = signal("x_in", 1, 16), signal("c_in", 1, 16), signal("cT_in", 1, 16)
        xT_ready, v_ready = signal("xT_ready", KC), signal("v_ready", GB)
        rot_parts, rotated = signal("rot_parts", 2 * GB), signal("rotated", 2 * GB)
        turned, spread_part, spread = signal("turned", 2 * GB), signal("spread_part", 3 * GB), signal("spread", GB)
        masked = signal("masked", KC * GB)
        squared, scaled, rms_ready, y_added = (signal(n, k) for n, k in (
            ("squared", GB), ("scaled", GB), ("rms_ready", 1), ("y_added", GB)))
        moments, rstd_ready, normed = signal("moments", 3), signal("rstd_ready", 3), signal("normed", 2 * GB)
        q_part, q_left, q_ready = signal("q_part", 2 * GB), signal("q_left", GB), signal("q_ready", GB)
        k_ready, vt_ready = signal("k_ready", GB), signal("vt_ready", 1)
        k_step = signal("k_step", 3 * GB)
        q_out, k_out = (signal(n, GB, 16) for n in ("q_out", "k_out"))
        stacked = [[signal(f"stacked{u}{v}", 2 * len(TERMS) * GB // 2, 16) for v in range(2)] for u in range(2)]
        ms_in = [signal(f"ms_in{u}", PARTS * GB // 2, 16) for u in range(2)]
        maxed, m_ready = signal("maxed", 2 * CH * GB), signal("m_ready", GB)
        exped = signal("exped", LC * CH * GB)
        pv_done = signal("pv_done", 2 * GB)
        pv_copied = signal("pv_copied", 2 * GB)
        added = signal("added", GB)
        ov_out, fin_in = signal("ov_out", GB, 16), signal("fin_in", 4 * GB, 16)
        stored = signal("stored", 1, 16)

        order = []
        projections = [("v", b) for b in range(3)] + [("q", 0), ("k", 0), ("v", 3)]
        projections += [(kind, b) for b in range(1, GB) for kind in ("q", "k")]
        order += [("v", b) for b in range(GB)]
        for b in range(GB):
            order += [("qt", b), ("kt", b)]
        for b in range(GB):
            order += [("s", b, c) for c in range(KC)]
            if b:
                order += [("a", b - 1)]
        order += [("a", GB - 1), ("ss",)] + [("y", b) for b in range(GB)]
        AHEAD = (2, 1, 1, 1, 1, 1, 1, 0)
        FINISH = 7
        LAST_MAX = 6
        next_heads = [range(sum(AHEAD[:h]), sum(AHEAD[:h + 1])) for h in range(CH)]
        pair_order = [(kind, b) for b in range(GB) for kind in ("q", "k")]
        pair_order += [("p", 0, h, u) for h in range(CH) for u in range(2)] + [("mt", 0)]
        for b in range(GB):
            for h in range(CH):
                order += [("e", b, h, l) for l in range(LC)]
                if b + 1 < GB:
                    pair_order += [("p", b + 1, n, u) for n in next_heads[h] for u in range(2)]
                    if h == LAST_MAX:
                        pair_order += [("mt", b + 1)]

        turn_in = [("xt", c) for c in range(KC)]
        order += turn_in

        def drained(key):
            kind, *n = key
            return {
                "xt": lambda: (xT_ready, KC + n[0] + 1),
                "q": lambda: (rot_parts, 2 * n[0] + 1),
                "k": lambda: (rot_parts, 2 * n[0] + 2),
                "v": lambda: (v_ready, n[0] + 1),
                "qt": lambda: (turned, 2 * n[0] + 1),
                "kt": lambda: (turned, 2 * n[0] + 2),
                "s": lambda: (masked, KC * n[0] + n[1] + 1),
                "a": lambda: (scaled, n[0] + 1),
                "ss": lambda: (rms_ready, 1),
                "y": lambda: (y_added, n[0] + 1),
                "p": lambda: (maxed, 2 * CH * n[0] + 2 * n[1] + n[2] + 1),
                "mt": lambda: (m_ready, n[0] + 1),
                "e": lambda: (exped, LC * (CH * n[0] + n[1]) + n[2] + 1),
            }[kind]()

        tiles = Tiles(banks, ctx.enter_context(nc.semaphore("c_filled")), order, drained)
        early = Tiles(banks, ctx.enter_context(nc.semaphore("c_filled_early")), turn_in,
                      lambda key: (xT_ready, key[1] + 1))
        pairs = Tiles(pair_banks, ctx.enter_context(nc.semaphore("c_filled_pairs")), pair_order, drained)
        idle = signal("idle", 0)
        start_signals(nc, looped)
        vstep = Steps(ctx.enter_context(nc.semaphore("c_vector_step")), 23)
        astep = Steps(ctx.enter_context(nc.semaphore("c_scalar_step")), 4)
        block = ctx.enter_context(nc.Block())

        @block.sync
        def _(sp):
            sp.dma_start(ident[:], t["ident"]).then_inc(ident_in.sem, 16)
            sp.dma_start(xin[:, :, :], t["x3"][0]).then_inc(x_in.sem, 16)
            for dst, src in ((wq, "wq1"), (cos, "cos1"), (sin, "sin1"), (wk, "wk1"), (wv, "wv1")):
                sp.dma_start(dst[:], t[src]).then_inc(weights.sem, 16)
            for dst, src in ((decay, "decay1"), (rmsw, "rms1"), (wo, "wo1"), (gamma, "gamma1")):
                sp.dma_start(dst[:], t[src]).then_inc(late.sem, 16)
            with sp.Fori(0, GROUPS) as g:
                k_ready.wait(sp, g, 0)
                sp.dma_start(cgr[:, :, :], t["c"][g]).then_inc(c_in.sem, 16)

                def out(b, ready, part, parked, done):
                    ready.wait(sp, g, b + 1)
                    sp.dma_start(parked[b % 2], part[:, b % 2]).then_inc(done.sem, 16)

                def stack(b, half, parked, side, dst):
                    heads = slice(CH // 2 * half, CH // 2 * (half + 1))
                    for n, pair in enumerate(TERMS):
                        sp.dma_start(dst[CD * n:CD * n + CD, b % 2, heads],
                                     parked[b % 2].rearrange("(h d) k l -> k d h l", d=CD)[pair[side]][:, heads])\
                          .then_inc(stacked[b % 2][half].sem, 16)

                def keys(b, half):
                    stack(b, half, t["kpark"], 1, ks)

                def queries(b, half):
                    stack(b, half, t["qpark"], 0, qs)

                def maxima(b):
                    m_ready.wait(sp, g, b + 1)
                    for k in range(PARTS):
                        sp.dma_start(qs[TR + k:TR + k + 1, b % 2].rearrange("k h (c q) -> k (h c) q", c=LC),
                                     mp[0:CH * LC, b % 2, k, :]).then_inc(ms_in[b % 2].sem, 16)

                def results(b):
                    added.wait(sp, g, b)
                    sp.sem_inc(idle.sem, 1)
                    pv_copied.wait(sp, g, 2 * b + 2)
                    sp.dma_start(t["ovpark"][b % 2], ov).then_inc(ov_out.sem, 16)
                    ov_out.wait(sp, g, b + 1)
                    parked = t["ovpark"][b % 2].rearrange("(j e) o n -> o j e n", e=32)
                    for o in range(2):
                        rows = slice(QUAD * CD * o, QUAD * CD * (o + 1))
                        sp.dma_start(fin[rows, 0, :], parked[o, :, 0:CD, :]).then_inc(fin_in.sem, 16)
                        sp.dma_start(fin[rows, 1, :], parked[o, :, CD:CD + 1, :].broadcast_to([QUAD, CD, D]))\
                          .then_inc(fin_in.sem, 16)

                exped.wait(sp, g, 0)
                sp.sem_inc(idle.sem, 1)
                for b in range(2):
                    out(b, k_ready, kp, t["kpark"], k_out)
                    k_out.wait(sp, g, b + 1)
                    for half in range(2):
                        keys(b, half)
                for b in range(2):
                    out(b, q_ready, qp, t["qpark"], q_out)
                    q_out.wait(sp, g, b + 1)
                    for half in range(2):
                        queries(b, half)
                    if b == 0:
                        y_added.wait(sp, g, GB)
                        sp.dma_start(cT, t["cT"][g]).then_inc(cT_in.sem, 16)
                maxima(0)
                sp.dma_start(xin[:, :, :], t["x3"][(g + 1) % GROUPS]).then_inc(x_in.sem, 16)
                for b in range(1, GB):
                    if b > 1:
                        results(b - 2)
                    if b + 1 < GB:
                        out(b + 1, k_ready, kp, t["kpark"], k_out)
                        out(b + 1, q_ready, qp, t["qpark"], q_out)
                        k_out.wait(sp, g, b + 2)
                        sp.sem_inc(idle.sem, 1)
                        q_out.wait(sp, g, b + 2)
                        sp.sem_inc(idle.sem, 1)
                        tiles.wait(sp, g, ("e", b - 1, CH // 2 - 1, LC - 1))
                        keys(b + 1, 0)
                        queries(b + 1, 0)
                    maxima(b)
                    if b + 1 < GB:
                        tiles.wait(sp, g, ("e", b - 1, CH - 1, LC - 1))
                        keys(b + 1, 1)
                        queries(b + 1, 1)
                results(GB - 2)
                results(GB - 1)
                normed.wait(sp, g, 2 * GB)
                sp.dma_start(t["x5"][g], xg[:, :, :]).then_inc(stored.sem, 16)
            x_in.wait(sp, GROUPS, 1)
            stored.wait(sp, GROUPS, 0)

        @block.gpsimd
        def _(pool):
            pool.memset(xz[:], 0.0).then_inc(consts.sem, 1)
            pool.memset(vflat[:], 0.0).then_inc(consts.sem, 1)
            pool.memset(ones[:], 1.0).then_inc(consts.sem, 1)
            pool.memset(ks[:], 1.0).then_inc(consts.sem, 1)
            pool.memset(qs[:], 0.0).then_inc(consts.sem, 1)
            pool.memset(eps[:], EPS_LN).then_inc(consts.sem, 1)
            pool.memset(mx[:], 0.0).then_inc(consts.sem, 1)
            pool.wait_ge(consts.sem, 7)
            pool.memset(vt[:, :, :, :, CD], 1.0).then_inc(consts.sem, 1)
            pool.wait_ge(consts.sem, NC)
            with pool.Fori(0, GROUPS) as g:
                vt_ready.wait(pool, g, 0)
                k_ready.wait(pool, g, 0)
                for b in range(GB):
                    for i in range(2):
                        n = 2 * b + i
                        rot_parts.wait(pool, g, n + 1)
                        pool.tensor_tensor((yq, yk)[i][:, b, :], r1[:, i, :], r2[:, i, :],
                                           ALU.add).then_inc(rotated.sem, 1)
                rotated.wait(pool, g, 2 * GB)
                for b in range(GB):
                    turned.wait(pool, g, 2 * b + 1)
                    masked.wait(pool, g, KC * max(b - 1, 0))
                    for r in range(HR):
                        rows = slice(HD * r, HD * r + HD)
                        if r == 0:
                            spread.wait(pool, g, b)
                        else:
                            spread_part.wait(pool, g, (HR - 1) * b + r)
                        pool.tensor_tensor(xz[rows, b % 2, :, r, :], qT[rows, b],
                                           ones[rows, :].unsqueeze(1).broadcast_to([HD, KC, P]), ALU.mult)\
                            .then_inc((spread if r == HR - 1 else spread_part).sem, 1)
                spread.wait(pool, g, GB)
                def parts(b):
                    u = b % 2
                    k_out.wait(pool, g, max(b - 1, 0))
                    one = ones[:, 0:1].broadcast_to([P, D])
                    if b:
                        k_ready.wait(pool, g, b)
                    pool.tensor_tensor(kp[:, u, 0, :], cgr[:, b, :], one, ALU.mult).then_inc(k_step.sem, 1)
                    k_step.wait(pool, g, 3 * b + 1)
                    pool.tensor_tensor(cres, cgr[:, b, :], kp[:, u, 0, :], ALU.subtract).then_inc(k_step.sem, 1)
                    k_step.wait(pool, g, 3 * b + 2)
                    pool.tensor_tensor(kp[:, u, 1, :], cres, one, ALU.mult).then_inc(k_step.sem, 1)
                    k_step.wait(pool, g, 3 * b + 3)
                    pool.tensor_tensor(kp[:, u, 2, :], cres, kp[:, u, 1, :], ALU.subtract).then_inc(k_ready.sem, 1)

                c_in.wait(pool, g, 1)
                parts(0)
                parts(1)
                cT_in.wait(pool, g, 1)
                for l in range(LC):
                    src = cT[:, l, :].rearrange("p (b h d) -> p b h d", b=GB, h=CH)
                    ins = pool.tensor_tensor(vt[:, l, :, :, 0:CD], src,
                                             ones[:, 0:1].unsqueeze(2).unsqueeze(3).broadcast_to([P, GB, CH, CD]),
                                             ALU.mult)
                ins.then_inc(vt_ready.sem, 1)
                for b in range(2, GB):
                    parts(b)

        @block.scalar
        def _(act):
            act.wait_ge(consts.sem, NC)

            def turned_in(tiles, turn):
                for c in range(KC):
                    bank = tiles.wait(act, turn, ("xt", c))
                    act.activation(xT[:, c, :], bank[:, 0:512], ACT.Copy).then_inc(xT_ready.sem, 1)

            turned_in(early, 0)
            with act.Fori(0, GROUPS) as g:
                astep.n = 0

                def root(src, signal, count, ready, scale=1.0):
                    signal.wait(act, g, count)
                    astep.did(act.activation(lnv[:, :], src, ACT.Ln, bias=eps[:, 0:1], scale=scale))
                    astep.wait(act, g)

                for b in range(GB):
                    bank = tiles.wait(act, g, ("v", b))
                    act.activation(v[:, b, :], bank[:, 0:512], ACT.Copy).then_inc(v_ready.sem, 1)
                for b in range(GB):
                    for i in range(2):
                        bank = tiles.wait(act, g, (("qt", "kt")[i], b))
                        act.activation((qT, kT)[i][:, b], bank[:, 0:512].rearrange("p (c n) -> p c n", c=KC),
                                       ACT.Copy).then_inc(turned.sem, 1)
                for b in range(GB):
                    bank = tiles.wait(act, g, ("a", b))
                    act.activation(sq[:, b], bank[:, 0:512].rearrange("p (c n) -> p c n", c=KC),
                                   ACT.Square).then_inc(squared.sem, 1)
                bank = tiles.wait(act, g, ("ss",))
                astep.did(act.activation(lnv[:, :], bank[:, 0:GB * P].rearrange("p (b n) -> p b n", b=GB)[:, :, 0],
                                         ACT.Ln, bias=eps[:, 0:1], scale=1.0 / D))
                astep.wait(act, g)
                act.activation(rms[:, :], lnv[:, :], ACT.Exp, scale=-0.5).then_inc(rms_ready.sem, 1)

                def norm(i, seqs):
                    moments.wait(act, g, i + 1)
                    rms_ready.wait(act, g, 1)
                    rstd_ready.wait(act, g, i)
                    astep.did(act.activation(lnv[:, seqs], mom[:, seqs, 1], ACT.Ln, bias=eps[:, 0:1]))
                    astep.wait(act, g)
                    act.activation(rstd[:, seqs], lnv[:, seqs], ACT.Exp, scale=-0.5).then_inc(rstd_ready.sem, 1)

                norm(0, slice(0, 1))

                def parts(b):
                    u = b % 2
                    normed.wait(act, g, b + 1)
                    q_out.wait(act, g, max(b - 1, 0))
                    act.activation(qp[:, u, 0, :], xg[:, b, :], ACT.Copy).then_inc(q_part.sem, 1)
                    q_left.wait(act, g, b + 1)
                    act.activation(qp[:, u, 1, :], qres, ACT.Copy).then_inc(q_part.sem, 1)

                parts(0)
                norm(1, slice(1, GB))
                parts(1)
                def outputs(b, quad):
                    pv_done.wait(act, g, 2 * b + quad + 1)
                    ov_out.wait(act, g, b)
                    act.activation(ov[:, quad, :], pv[:, :], ACT.Copy).then_inc(pv_copied.sem, 1)

                for b in range(GB):
                    for h in range(CH):
                        if h == 2 and b + 2 < GB:
                            parts(b + 2)
                        n = CH * b + h
                        if n >= RING:
                            pv_done.wait(act, g, (n - RING) // QUAD + 1)
                        for l in range(LC):
                            bank = tiles.wait(act, g, ("e", b, h, l))
                            act.activation(probs[:, n % RING, l, :], bank[:, :], ACT.Exp,
                                           scale=float(CD) ** -0.5).then_inc(exped.sem, 1)
                        if h == 5:
                            outputs(b, 0)
                    outputs(b, 1)
                q_out.wait(act, g, GB)
                turned_in(tiles, g)
                norm(2, slice(0, GB))
            astep.close("layer 1, scalar")

        @block.tensor
        def _(pe):
            pe.wait_ge(ident_in.sem, 16)

            def turn_over(tiles, turn, loads):
                x_in.wait(pe, turn, loads)
                for c in range(KC):
                    bank = tiles.start(pe, turn, ("xt", c))
                    for b in range(GB):
                        ins = pe.transpose(bank[:, b * P:(b + 1) * P], xin[:, b, c * P:(c + 1) * P], ident[:, :])
                    tiles.done(ins)

            turn_over(early, 0, 1)
            pe.wait_ge(weights.sem, 16 * NW)
            pe.wait_ge(consts.sem, NC)
            with pe.Fori(0, GROUPS) as g:
                for kind, b in projections:
                    pool_of, w = {"q": (pairs, wq), "k": (pairs, wk), "v": (tiles, wv)}[kind]
                    bank = pool_of.start(pe, g, (kind, b), [(xT_ready, KC)])
                    for c in range(KC):
                        ins = pe.matmul(bank[:, 0:512], xT[:, c, b * P:(b + 1) * P], w[:, c, :],
                                        start=(c == 0), stop=(c == KC - 1))
                    pool_of.done(ins)
                for b in range(GB):
                    for i in range(2):
                        bank = tiles.start(pe, g, (("qt", "kt")[i], b), [(rotated, 2 * b + i + 1)])
                        for c in range(KC):
                            ins = pe.transpose(bank[:, c * P:(c + 1) * P], (yq, yk)[i][:, b, c * P:(c + 1) * P],
                                               ident[:, :])
                        tiles.done(ins)

                def attend(b):
                    bank = tiles.start(pe, g, ("a", b), [(masked, KC * (b + 1))])
                    v_ready.wait(pe, g, GB)
                    for c in range(KC):
                        for r in range(HR):
                            at0 = HD * (HR * c + r)
                            ins = pe.matmul(bank[HD * r:HD * r + HD, c * P:(c + 1) * P], v[:, b, at0:at0 + HD],
                                            sm[:, b % 2, c, r, :], start=True, stop=True)
                    tiles.done(ins)

                for b in range(GB):
                    for c in range(KC):
                        bank = tiles.start(pe, g, ("s", b, c), [(spread, b + 1), (turned, 2 * b + 2)])
                        tiles.done(pe.matmul(bank[:, 0:512], kT[:, b, c, :], xz[:, b % 2, c], start=True, stop=True))
                    if b:
                        attend(b - 1)
                attend(GB - 1)
                bank = tiles.start(pe, g, ("ss",))
                for b in range(GB):
                    squared.wait(pe, g, b + 1)
                    for c in range(KC):
                        ins = pe.matmul(bank[:, b * P:(b + 1) * P], sq[:, b, c, :], ones[:, :],
                                        start=(c == 0), stop=(c == KC - 1))
                tiles.done(ins)
                pe.wait_ge(late.sem, 16 * NL)
                for b in range(GB):
                    bank = tiles.start(pe, g, ("y", b), [(scaled, b + 1)])
                    for c in range(KC):
                        ins = pe.matmul(bank[:, 0:512], at[:, b, c, :], wo[:, c, :],
                                        start=(c == 0), stop=(c == KC - 1))
                    tiles.done(ins)

                def first(b, h, u):
                    if h % (CH // 2) == 0 and u == 0:
                        stacked[b % 2][2 * h // CH].wait(pe, g, 2 * len(TERMS) * (b // 2 + 1))
                    bank = pairs.start(pe, g, ("p", b, h, u))
                    for i in range(2):
                        at0 = (2 * u + i) * P
                        ins = pe.matmul(bank[:, 512 * i:512 * i + 512], qs[0:TR, b % 2, h, at0:at0 + P],
                                        ks[0:TR, b % 2, h, :], start=True, stop=True)
                    pairs.done(ins)

                def turn_max(b):
                    bank = pairs.start(pe, g, ("mt", b), [(maxed, 2 * CH * (b + 1))])
                    pairs.done(pe.transpose(bank[:, 0:P], mx[:, b % 2, :], ident[:, :]))

                def second(b, h, l):
                    if h == 0 and l == 0:
                        ms_in[b % 2].wait(pe, g, PARTS * (b // 2 + 1))
                    bank = tiles.start(pe, g, ("e", b, h, l))
                    tiles.done(pe.matmul(bank[:, :], ks[:, b % 2, h, l * P:(l + 1) * P], qs[:, b % 2, h, :],
                                         start=True, stop=True))

                def values(b, quad, l):
                    if l == 0:
                        exped.wait(pe, g, LC * (CH * b + QUAD * (quad + 1)))
                        vt_ready.wait(pe, g, 1)
                        pv_copied.wait(pe, g, 2 * b + quad)
                    for j in range(QUAD):
                        h = QUAD * quad + j
                        at0 = ((l * GB + b) * CH + h) * (CD + 1)
                        ins = pe.matmul(pv[32 * j:32 * j + 32, :], vflat[:, at0:at0 + 32],
                                        probs[:, (CH * b + h) % RING, l, :], start=(l == 0), stop=(l == LC - 1))
                    if l == LC - 1:
                        ins.then_inc(pv_done.sem, 1)

                for h in range(CH):
                    for u in range(2):
                        first(0, h, u)
                turn_max(0)
                for b in range(GB):
                    for h in range(CH):
                        between = [(values, b, 0, 2 * h - 8 + i) for i in range(2) if h in (4, 5)]
                        if b + 1 < GB:
                            between += [(first, b + 1, n, u) for n in next_heads[h] for u in range(2)]
                            if h == LAST_MAX:
                                between += [(turn_max, b + 1)]
                        half = (len(between) + 1) // 2
                        for pair, rest in ((0, between[:half]), (2, between[half:])):
                            second(b, h, pair)
                            second(b, h, pair + 1)
                            for step, *args in rest:
                                step(*args)
                    for l in range(LC):
                        values(b, 1, l)
                turn_over(tiles, g, 2)

        @block.vector
        def _(dve):
            dve.wait_ge(weights.sem, 16 * NW)
            dve.wait_ge(consts.sem, NC)
            with dve.Fori(0, GROUPS) as g:
                vstep.n = 0

                def chained(ins):
                    vstep.did(ins)
                    vstep.wait(dve, g)

                for b in range(GB):
                    for i in range(2):
                        bank = pairs.wait(dve, g, (("q", "k")[i], b))
                        rotated.wait(dve, g, max(2 * b + i - 1, 0))
                        view = bank[:, 0:512].rearrange("p (h e d) -> p h e d", h=HX, e=2)
                        one = r1[:, i, :].rearrange("p (h d) -> p h d", d=CD)
                        two = r2[:, i, :].rearrange("p (h e d) -> p h e d", h=HX, e=2)
                        dve.tensor_tensor(one, bank[:, 0:512].rearrange("p (h d) -> p h d", d=CD),
                                          cos[:, :].unsqueeze(1).broadcast_to([P, 2 * HX, CD]), ALU.mult)
                        table = sin[:, :].unsqueeze(1).broadcast_to([P, HX, CD])
                        dve.tensor_tensor(two[:, :, 0, :], view[:, :, 1, :], table, ALU.mult)
                        dve.scalar_tensor_tensor(two[:, :, 1, :], view[:, :, 0, :], -1.0, table, ALU.mult,
                                                 ALU.mult).then_inc(rot_parts.sem, 1)

                dve.wait_ge(late.sem, 16 * NL)

                def scale_out(b):
                    bank = tiles.wait(dve, g, ("a", b))
                    squared.wait(dve, g, b + 1)
                    dve.tensor_tensor(at[:, b], bank[:, 0:512].rearrange("p (c n) -> p c n", c=KC),
                                      rmsw[:, :].unsqueeze(2).broadcast_to([P, KC, P]),
                                      ALU.mult).then_inc(scaled.sem, 1)

                for b in range(GB):
                    for c in range(KC):
                        bank = tiles.wait(dve, g, ("s", b, c))
                        dve.tensor_tensor(sm[:, b % 2, c], bank[:, 0:512].rearrange("p (r n) -> p r n", r=HR),
                                          decay[:, HR * c:HR * c + HR, :], ALU.mult).then_inc(masked.sem, 1)
                    if b:
                        scale_out(b - 1)
                scale_out(GB - 1)
                rms_ready.wait(dve, g, 1)
                stored.wait(dve, g, 0)

                def add_y(b):
                    bank = tiles.wait(dve, g, ("y", b))
                    dve.scalar_tensor_tensor(xg[:, b, :], bank[:, 0:512], rms[:, b:b + 1], xin[:, b, :],
                                             ALU.mult, ALU.add).then_inc(y_added.sem, 1)

                def moments_of(seqs):
                    for b in seqs:
                        ins = dve.bn_stats(stats[:, b, :], xg[:, b, :])
                    chained(ins)
                    dve.tensor_copy(held[:, 1:2], ones[:, 0:1])
                    for b in seqs:
                        ins = dve.bn_aggr(mom[:, b, :], stats[:, b, :])
                    ins.then_inc(moments.sem, 1)

                def normalise(i, seqs):
                    rstd_ready.wait(dve, g, i + 1)
                    for b in seqs:
                        dve.tensor_scalar(xg[:, b, :], xg[:, b, :], mom[:, b, 0:1], rstd[:, b:b + 1],
                                          ALU.subtract, ALU.mult).then_inc(normed.sem, 1)

                def parts(b):
                    u = b % 2
                    q_ready.wait(dve, g, b)
                    q_part.wait(dve, g, 2 * b + 1)
                    dve.tensor_tensor(qres, xg[:, b, :], qp[:, u, 0, :], ALU.subtract).then_inc(q_left.sem, 1)
                    q_part.wait(dve, g, 2 * b + 2)
                    dve.tensor_tensor(qp[:, u, 2, :], qres, qp[:, u, 1, :], ALU.subtract).then_inc(q_ready.sem, 1)

                def maxima(b, h):
                    for u in range(2):
                        bank = pairs.wait(dve, g, ("p", b, h, u))
                        at0 = LC * h + 2 * u
                        dve.tensor_reduce(mx[:, b % 2, at0:at0 + 2], bank[:, :].rearrange("p (i n) -> p i n", i=2),
                                          AX.X, ALU.max).then_inc(maxed.sem, 1)

                def max_parts(b):
                    u, rows = b % 2, slice(0, CH * LC)
                    bank = pairs.wait(dve, g, ("mt", b))
                    if b > 1:
                        ms_in[u].wait(dve, g, PARTS * (b // 2))
                    else:
                        ms_in[u].wait(dve, g, 0)
                    chained(dve.tensor_scalar(mp[rows, u, 0, :], bank[rows, 0:P], -1.0, None, ALU.mult))
                    chained(dve.scalar_tensor_tensor(mrow[rows, :], bank[rows, 0:P], -1.0, mp[rows, u, 0, :],
                                                     ALU.mult, ALU.subtract))
                    chained(dve.tensor_copy(mp[rows, u, 1, :], mrow[rows, :]))
                    dve.tensor_tensor(mp[rows, u, 2, :], mrow[rows, :], mp[rows, u, 1, :],
                                      ALU.subtract).then_inc(m_ready.sem, 1)

                def finish(b):
                    fin_in.wait(dve, g, 4 * (b + 1))
                    chained(dve.reciprocal(fin[:, 1, :], fin[:, 1, :]))
                    chained(dve.scalar_tensor_tensor(fin[:, 0, :], fin[:, 0, :], gamma[:, 0:1], fin[:, 1, :],
                                                     ALU.mult, ALU.mult))
                    dve.tensor_tensor(xg[:, b, :], xg[:, b, :], fin[:, 0, :], ALU.add).then_inc(added.sem, 1)

                add_y(0)
                y_added.wait(dve, g, 1)
                dve.tensor_copy(held[:, 1:2], ones[:, 0:1])
                moments_of(range(1))
                add_y(1)
                add_y(2)
                normalise(0, range(1))
                parts(0)
                add_y(3)
                y_added.wait(dve, g, GB)
                dve.tensor_copy(held[:, 1:2], ones[:, 0:1])
                moments_of(range(1, GB))
                normalise(1, range(1, GB))
                parts(1)
                for h in range(CH):
                    maxima(0, h)
                max_parts(0)
                for b in range(GB):
                    for h in range(CH):
                        if h == 2 and b + 2 < GB:
                            parts(b + 2)
                        if b + 1 < GB:
                            for n in next_heads[h]:
                                maxima(b + 1, n)
                            if h == LAST_MAX:
                                max_parts(b + 1)
                        if b and h == FINISH:
                            finish(b - 1)
                finish(GB - 1)
                added.wait(dve, g, GB)
                dve.tensor_copy(held[:, 1:2], ones[:, 0:1])
                moments_of(range(GB))
                normalise(2, range(GB))
            vstep.close("layer 1, vector")


def build_experts(nc, t):
    with ExitStack() as ctx:
        def sb(name, shape, dt=F32):
            return ctx.enter_context(nc.sbuf_tensor("d_" + name, shape, dt))

        def semaphore(name):
            return ctx.enter_context(nc.semaphore("d_" + name))

        def signal(name, per=0, unit=1):
            return Signal(semaphore(name), per, unit)

        NGR, TOPG, TOPK = 4, 2, 4
        EG = NE // NGR
        TOKENS = SEQS * P
        BLOCKS = TOKENS * TOPK // P + NE
        LIST = BLOCKS + 2
        inner = chunks_of(FI)
        shared = chunks_of(FS)
        NI, NS = len(inner), len(shared)
        FP = NI * P

        banks = [ctx.enter_context(nc.psum_tensor(f"d_bank{i}", [P, 512], F32)) for i in range(BANKS)]
        y = sb("y", [P, SEQS, D])
        xT = sb("xT", [P, KC, TOKENS])
        ws1, ws3 = sb("ws1", [P, KC, FS]), sb("ws3", [P, KC, FS])
        ws2 = sb("ws2", [P, NS, D])
        hs = sb("hs", [P, NS, GT])
        gated = sb("gated", [P, 2, GT])
        wg = sb("wg", [P, KC, NE])
        w13 = sb("w13", [P, 2, 2, KC, FI])
        w2 = sb("w2", [P, 2, NI, D])
        xrow, xcol = sb("xrow", [P, 2, D]), sb("xcol", [P, 2, KC, P])
        gate = sb("gate", [P, 2, FI])
        hrow, hid = sb("hrow", [P, 2, FP]), sb("hid", [P, 2, FP])
        yrow = sb("yrow", [P, 2, D])
        SLOTS = 4
        back = sb("back", [P, SLOTS, D])

        iota, ident, causal, ones = sb("iota", [P, NE]), sb("ident", [P, P]), sb("causal", [P, P]), sb("ones", [P, P])
        steps_of = sb("steps_of", [P, SEQS - 1])
        block_no = sb("block_no", [1, BLOCKS + 1])
        token_no = sb("token_no", [P, SEQS], U32)
        eps = sb("eps", [P, 1])
        pr = sb("pr", [P, SEQS, NE])
        sel = sb("sel", [P, SEQS, NE])
        comb = sb("comb", [P, SEQS, NE])
        rmx = sb("rmx", [P, SEQS])
        grp = sb("grp", [P, SEQS, 8])
        top, topf = sb("top", [P, SEQS, 8]), sb("topf", [P, SEQS, 8])
        topi = sb("topi", [P, SEQS, 8], U32)
        eq = sb("eq", [P, SEQS, NE])
        before = sb("before", [P, SEQS, NE])
        count, base, more = sb("count", [P, NE]), sb("base", [P, NE]), sb("more", [P, NE, SEQS - 1])
        unit = sb("unit", [P, NE])
        slot = sb("slot", [P, TOPK, SEQS])
        slot_no = sb("slot_no", [P, TOPK, SEQS], U32)
        quot, rest = sb("quot", [P, TOPK, SEQS], U32), sb("rest", [P, TOPK, SEQS], U32)
        quotf, restf = sb("quotf", [P, TOPK, SEQS]), sb("restf", [P, TOPK, SEQS])
        place = sb("place", [P, TOPK, SEQS], U32)
        row_no = sb("row_no", [P, TOPK, SEQS], U32)
        past = sb("past", [1, BLOCKS + 1, NE - 1])
        owner, held = sb("owner", [1, BLOCKS + 1]), sb("held", [1, BLOCKS + 1])
        change = sb("change", [1, BLOCKS + 1])
        owner_no = sb("owner_no", [1, BLOCKS + 1], I32)
        fetch_no = sb("fetch_no", [1, BLOCKS + 1], I32)
        empty = sb("empty", [P, LIST], U32)
        tokens = sb("tokens", [P, LIST], U32)
        index = sb("index", [P, 2], U32)
        stats, mom, rstd = sb("stats", [P, SEQS, 6]), sb("mom", [P, SEQS, 2]), sb("rstd", [P, SEQS])

        loaded = [signal(f"loaded{g}", 0, 16) for g in range(GROUPS)]
        weights, consts, shared_in = signal("weights"), signal("consts"), signal("shared_in")
        xT_ready, rt_shift, rt_exp = signal("xT_ready"), signal("rt_shift"), signal("rt_exp")
        chosen_ready, placed, owners = signal("chosen_ready"), signal("placed"), signal("owners")
        list_clear, list_filled, list_in = signal("list_clear"), signal("list_filled"), signal("list_in")
        s_gated, s_h, s_added = signal("s_gated"), signal("s_h"), signal("s_added")
        moments, rstd_ready, normed = signal("moments"), signal("rstd_ready"), signal("normed")
        out_stored = signal("out_stored")
        expert_in = signal("expert_in")
        AHEAD = 2
        y_added = signal("y_added")
        COMBINED = range(SEQS)
        CONSTS = 7
        xcol_ready, gate_ready, hrow_ready, hid_ready, yrow_ready = (
            signal(n) for n in ("xcol_ready", "gate_ready", "hrow_ready", "hid_ready", "yrow_ready"))
        gathered = [signal(f"gathered{v}") for v in range(2)]
        row_stored = [signal(f"row_stored{v}") for v in range(2)]
        index_ready, pool_step = signal("index_ready"), signal("pool_step")
        returned = [signal(f"returned{n}") for n in range(SLOTS)]
        filled = signal("loop_filled")
        vstep = Steps(semaphore("vector_step"), 0)

        turned_bank, hidden_bank, gate_banks, up_banks, down_banks = banks[0], banks[1], banks[2:4], banks[4:6], banks[6:8]

        def turned(j):
            return 5 * j + 1

        def gate_up(j):
            return 5 * j + 7

        def up_done(j):
            return 5 * j + 9

        def hidden_turned(j):
            return 5 * j + 13

        def down_done(j):
            return 5 * j + 15

        def shared_tiles(groups):
            order = []
            for g in groups:
                order += [(kind, g, c) for c in range(NS) for kind in ("sg", "su")]
                order += [("sy", g, b) for b in range(GB)]
            return order

        def drained(key):
            kind, *n = key
            return {
                "xt": lambda: (xT_ready, n[0] + 1),
                "rt": lambda: (rt_shift, 1),
                "rank": lambda: (placed, 1),
                "sg": lambda: (s_gated, NS * n[0] + n[1] + 1),
                "su": lambda: (s_h, NS * n[0] + n[1] + 1),
                "sy": lambda: (s_added, GB * n[0] + n[1] + 1),
            }[kind]()

        EARLY, LATE = (0, 1), (2, 3)
        early = shared_tiles(EARLY)
        RANK_AT = NS // 2
        order = [("xt", b) for b in range(SEQS)] + [("rt",)]
        order += early[:2 * RANK_AT] + [("rank",)] + early[2 * RANK_AT:]
        READY = (range(0, SEQS - GB), range(SEQS - GB, SEQS))
        first = Tiles(banks, semaphore("filled"), order, drained)
        last = Tiles(banks, semaphore("filled2"), shared_tiles(LATE), drained)
        x_rows = t["x5"].rearrange("g p b d -> (g p b) d")
        list_rows = t["slots"].rearrange("p j -> (p j)").unsqueeze(1)
        result_rows = t["results"].rearrange("j p d -> (j p) d")
        block = ctx.enter_context(nc.Block())

        def load_number(eng, row, n):
            return eng.value_load(row[0:1, bass.ds(n, 1)], min_val=0, max_val=NE - 1)

        def load_expert(sp, e, at):
            sp.dma_start(w13[:, at], t["w131"][e]).then_inc(expert_in.sem, 16)
            sp.dma_start(w2[:, at], t["w21"][e]).then_inc(expert_in.sem, 16)

        @block.sync
        def _(sp):
            sp.dma_start(ident[:], t["ident"]).then_inc(weights.sem, 16)
            for dst, src in ((wg, "wg1"), (iota, "iota1"), (causal, "causal"), (steps_of, "steps_of"),
                             (block_no, "block_no"), (token_no, "token_no")):
                sp.dma_start(dst[:], t[src]).then_inc(weights.sem, 16)
            for g in range(GROUPS):
                sp.dma_start(y[:, GB * g:GB * (g + 1), :], t["x5"][g]).then_inc(loaded[g].sem, 16)
            for dst, src in ((ws1, "ws1"), (ws3, "ws3"), (ws2, "ws2")):
                sp.dma_start(dst[:], t[src]).then_inc(shared_in.sem, 16)
            sp.wait_ge(consts.sem, CONSTS)
            sp.dma_start(t["slots"], empty[:]).then_inc(list_clear.sem, 16)
            load_expert(sp, 0, 0)
            sp.wait_ge(list_filled.sem, 16 * TOPK * SEQS)
            sp.dma_start(tokens[:], t["slots"]).then_inc(list_in.sem, 16)
            sp.wait_ge(expert_in.sem, 32)
            load_expert(sp, 1, 1)
            sp.wait_ge(owners.sem, 1)
            for v in range(2):
                sp.sem_inc(row_stored[v].sem, 16)
            with sp.Fori(0, BLOCKS // 2) as i:
                for v in range(2):
                    j = 2 * i + v
                    fetch = load_number(sp, fetch_no, j + 1)
                    sp.wait_ge(yrow_ready.sem, AHEAD + 1 + j)
                    sp.dma_start(t["results"][j], yrow[:, v]).then_inc(row_stored[v].sem, 16)
                    with sp.If(fetch > 0):
                        sp.wait_ge(expert_in.sem, 32 * fetch)
                        load_expert(sp, fetch, fetch % 2)
            sp.wait_ge(yrow_ready.sem, AHEAD + 1 + BLOCKS)
            sp.dma_start(t["results"][BLOCKS], yrow[:, 0]).then_inc(row_stored[0].sem, 16)
            for b in range(SEQS):
                sp.wait_ge(normed.sem, b + 1)
                sp.dma_start(t["out"][b], y[:, b, :]).then_inc(out_stored.sem, 16)
            sp.wait_ge(out_stored.sem, 16 * SEQS)

        @block.gpsimd
        def _(pool):
            pool.memset(eps[:], EPS_LN).then_inc(consts.sem, 1)
            pool.memset(hs[:], 0.0).then_inc(consts.sem, 1)
            pool.memset(grp[:], -1.0).then_inc(consts.sem, 1)
            pool.memset(ones[:], 1.0).then_inc(consts.sem, 1)
            pool.memset(unit[:], 1.0).then_inc(consts.sem, 1)
            pool.memset(empty[:], 0).then_inc(consts.sem, 1)
            pool.memset(hrow[:], 0.0).then_inc(consts.sem, 1)
            pool.wait_ge(weights.sem, 16 * 7)
            pool.wait_ge(list_clear.sem, 16)
            pool.wait_ge(placed.sem, 2)
            for k in range(TOPK):
                for b in range(SEQS):
                    pool.indirect_dma_start(list_rows, bass.IndirectOffsetOnAxis(ap=place[:, k, b:b + 1], axis=0),
                                            token_no[:, b:b + 1], None).then_inc(list_filled.sem, 16)
            pool.wait_ge(list_in.sem, 16)

            def gather(j, v, held):
                if held is not None:
                    pool.wait_ge(xcol_ready.sem, held)
                    pool.sem_inc(pool_step.sem, 1)
                pool.tensor_copy(index[:, v:v + 1], tokens[:, bass.ds(j, 1)]).then_inc(index_ready.sem, 1)
                pool.wait_ge(index_ready.sem, j + 1)
                pool.sem_inc(pool_step.sem, 1)
                pool.indirect_dma_start(xrow[:, v], None, x_rows,
                                        bass.IndirectOffsetOnAxis(ap=index[:, v:v + 1], axis=0))\
                    .then_inc(gathered[v].sem, 16)

            gather(0, 0, None)
            with pool.Fori(0, BLOCKS // 2) as i:
                for v in range(2):
                    j = 2 * i + v
                    gather(j + 1, 1 - v, AHEAD + j)
            pool.wait_ge(row_stored[0].sem, 16 * (BLOCKS // 2 + 2))
            pool.wait_ge(row_stored[1].sem, 16 * (BLOCKS // 2 + 1))
            for n, (b, k) in enumerate((b, k) for b in COMBINED for k in range(TOPK)):
                if n >= SLOTS:
                    pool.wait_ge(y_added.sem, n - SLOTS + 1)
                pool.indirect_dma_start(back[:, n % SLOTS], None, result_rows,
                                        bass.IndirectOffsetOnAxis(ap=row_no[:, k, b:b + 1], axis=0))\
                    .then_inc(returned[n % SLOTS].sem, 16)

        @block.scalar
        def _(act):
            act.wait_ge(consts.sem, CONSTS)
            for b in range(SEQS):
                bank = first.wait(act, 0, ("xt", b))
                act.activation(xT[:, :, b * P:(b + 1) * P], bank[:, :].rearrange("p (c n) -> p c n", c=KC),
                               ACT.Copy).then_inc(xT_ready.sem, 1)
            act.wait_ge(rt_shift.sem, 1)
            act.activation(pr[:], pr[:], ACT.Exp).then_inc(rt_exp.sem, 1)

            def roots(i):
                seqs = slice(READY[i].start, READY[i].stop)
                act.wait_ge(moments.sem, i + 1)
                act.activation(rstd[:, seqs], mom[:, seqs, 1], ACT.Ln, bias=eps[:, 0:1]).then_inc(rstd_ready.sem, 1)
                act.wait_ge(rstd_ready.sem, 2 * i + 1)
                act.activation(rstd[:, seqs], rstd[:, seqs], ACT.Exp, scale=-0.5).then_inc(rstd_ready.sem, 1)

            def shared_gates(tiles, groups):
                for g in groups:
                    for c, (_, m) in enumerate(shared):
                        if g == LATE[-1] and c == NS - 1:
                            roots(0)
                        n = NS * g + c
                        bank = tiles.wait(act, 0, ("sg", g, c))
                        if n >= 2:
                            act.wait_ge(s_h.sem, n - 1)
                        act.activation(gated[0:m, n % 2, :], bank[0:m, :], ACT.Silu).then_inc(s_gated.sem, 1)

            shared_gates(first, EARLY)
            act.sem_inc(gate_ready.sem, AHEAD)
            act.sem_inc(yrow_ready.sem, AHEAD)

            def rows_out(v, m, done):
                act.wait_ge(filled.sem, done)
                act.wait_ge(row_stored[v].sem, 16 * (m + 1))
                act.activation(yrow[:, v], down_banks[v][:, :], ACT.Copy).then_inc(yrow_ready.sem, 1)

            with act.Fori(0, BLOCKS // 2) as i:
                for v in range(2):
                    j = 2 * i + v
                    act.wait_ge(filled.sem, gate_up(j))
                    act.wait_ge(hrow_ready.sem, AHEAD + j - 1)
                    act.activation(gate[:, v], gate_banks[v][:, 0:FI], ACT.Silu).then_inc(gate_ready.sem, 1)
                    rows_out(v, i, down_done(j - 1))
            rows_out(0, BLOCKS // 2, 5 * BLOCKS + 7)
            shared_gates(last, LATE)
            roots(1)

        @block.tensor
        def _(pe):
            def up(tiles, key, w, width, group):
                bank = tiles.start(pe, 0, key)
                c0, m = width
                for c in range(KC):
                    ins = pe.matmul(bank[0:m, :], w[:, c, c0:c0 + m], xT[:, c, GT * group:GT * (group + 1)],
                                    start=(c == 0), stop=(c == KC - 1))
                tiles.done(ins)

            def shared_ups(tiles, g, chunks=range(NS)):
                for c in chunks:
                    up(tiles, ("sg", g, c), ws1, shared[c], g)
                    up(tiles, ("su", g, c), ws3, shared[c], g)

            def shared_downs(tiles, g):
                for b in range(GB):
                    bank = tiles.start(pe, 0, ("sy", g, b), [(s_h, NS * (g + 1))])
                    for c in range(NS):
                        ins = pe.matmul(bank[:, :], hs[:, c, b * P:(b + 1) * P], ws2[:, c, :],
                                        start=(c == 0), stop=(c == NS - 1))
                    tiles.done(ins)

            pe.wait_ge(weights.sem, 16 * 7)
            for b in range(SEQS):
                if b % GB == 0:
                    pe.wait_ge(loaded[b // GB].sem, 16)
                bank = first.start(pe, 0, ("xt", b))
                for c in range(KC):
                    ins = pe.transpose(bank[:, c * P:(c + 1) * P], y[:, b, c * P:(c + 1) * P], ident[:, :])
                first.done(ins)
            bank = first.start(pe, 0, ("rt",), [(xT_ready, SEQS)])
            for b in range(SEQS):
                for c in range(KC):
                    ins = pe.matmul(bank[:, b * NE:(b + 1) * NE], xT[:, c, b * P:(b + 1) * P], wg[:, c, :],
                                    start=(c == 0), stop=(c == KC - 1))
            first.done(ins)
            pe.wait_ge(shared_in.sem, 48)
            pe.wait_ge(consts.sem, CONSTS)
            shared_ups(first, EARLY[0], range(RANK_AT))
            bank = first.start(pe, 0, ("rank",), [(chosen_ready, 1)])
            pairs = sel[:].rearrange("p b e -> p (b e)")
            pe.matmul(bank[:, 0:SEQS * NE], causal[:, :], pairs, start=True, stop=True)
            ins = pe.matmul(bank[:, SEQS * NE:2 * SEQS * NE], ones[:, :], pairs, start=True, stop=True)
            first.done(ins)
            shared_ups(first, EARLY[0], range(RANK_AT, NS))
            shared_downs(first, EARLY[0])
            for g in EARLY[1:]:
                shared_ups(first, g)
                shared_downs(first, g)

            def turn(v):
                for c in range(KC):
                    ins = pe.transpose(turned_bank[:, c * P:(c + 1) * P], xrow[:, v, c * P:(c + 1) * P], ident[:, :])
                ins.then_inc(filled.sem, 1)

            def turn_hidden(v):
                for c in range(NI):
                    ins = pe.transpose(hidden_bank[:, c * P:(c + 1) * P], hrow[:, v, c * P:(c + 1) * P], ident[:, :])
                ins.then_inc(filled.sem, 1)

            def up_rows(bank, v, which, at):
                for k in range(KC):
                    ins = pe.matmul(bank[:, 0:FI], xcol[:, v, k, :],
                                    w13[:, bass.ds(at, 1), which, k, :].rearrange("p a n -> p (a n)"),
                                    start=(k == 0), stop=(k == KC - 1))
                ins.then_inc(filled.sem, 1)

            def down(bank, v, at):
                for c in range(NI):
                    ins = pe.matmul(bank[:, :], hid[:, v, c * P:(c + 1) * P],
                                    w2[:, bass.ds(at, 1), c, :].rearrange("p a n -> p (a n)"),
                                    start=(c == 0), stop=(c == NI - 1))
                ins.then_inc(filled.sem, 1)

            pe.wait_ge(s_added.sem, GB * len(EARLY))
            pe.wait_ge(gathered[0].sem, 16)
            turn(0)
            pe.wait_ge(xcol_ready.sem, AHEAD + 1)
            pe.sem_inc(filled.sem, 4)
            pe.wait_ge(owners.sem, 1)
            with pe.Fori(0, BLOCKS // 2) as i:
                for v in range(2):
                    j = 2 * i + v
                    expert = load_number(pe, owner_no, j + 1)
                    last_at = load_number(pe, owner_no, j) % 2
                    pe.wait_ge(gathered[1 - v].sem, 16 * (i + 1 + v))
                    pe.wait_ge(xcol_ready.sem, AHEAD + j + 1)
                    turn(1 - v)
                    pe.wait_ge(expert_in.sem, 32 * (expert + 1))
                    pe.wait_ge(gate_ready.sem, AHEAD + j - 1)
                    up_rows(gate_banks[v], v, 0, expert % 2)
                    pe.wait_ge(hrow_ready.sem, AHEAD + j)
                    pe.wait_ge(hid_ready.sem, AHEAD + j)
                    turn_hidden(1 - v)
                    up_rows(up_banks[v], v, 1, expert % 2)
                    pe.wait_ge(hid_ready.sem, AHEAD + 1 + j)
                    pe.wait_ge(yrow_ready.sem, AHEAD + j - 1)
                    down(down_banks[v], 1 - v, last_at)
            pe.wait_ge(hrow_ready.sem, AHEAD + BLOCKS)
            pe.wait_ge(hid_ready.sem, AHEAD + BLOCKS)
            turn_hidden(1)
            pe.wait_ge(hid_ready.sem, AHEAD + 1 + BLOCKS)
            pe.wait_ge(yrow_ready.sem, AHEAD + BLOCKS - 1)
            down(down_banks[0], 1, (NE - 1) % 2)
            pe.wait_ge(yrow_ready.sem, AHEAD + BLOCKS + 1)
            pe.wait_ge(xcol_ready.sem, AHEAD + BLOCKS + 1)
            for g in LATE:
                shared_ups(last, g)
                shared_downs(last, g)

        @block.vector
        def _(dve):
            dve.wait_ge(consts.sem, CONSTS)
            dve.wait_ge(weights.sem, 16 * 7)

            def chained(ins):
                vstep.did(ins)
                vstep.wait(dve, 0)

            def wide(ap, n=NE):
                return ap.unsqueeze(2).broadcast_to([P, SEQS, n])

            bank = first.wait(dve, 0, ("rt",))
            logits = bank[:, 0:SEQS * NE].rearrange("p (b e) -> p b e", b=SEQS)
            chained(dve.tensor_reduce(rmx[:, :], logits, AX.X, ALU.max))
            dve.tensor_tensor(pr[:], logits, wide(rmx[:, :]), ALU.subtract).then_inc(rt_shift.sem, 1)
            dve.wait_ge(rt_exp.sem, 1)
            chained(dve.tensor_reduce(rmx[:, :], pr[:], AX.X, ALU.add))
            chained(dve.reciprocal(rmx[:, :], rmx[:, :]))
            chained(dve.tensor_tensor(pr[:], pr[:], wide(rmx[:, :]), ALU.mult))

            def chosen(out, src, width, count):
                for b in range(SEQS):
                    ins = dve.max(top[:, b, :], src[:, b, :])
                chained(ins)
                for b in range(SEQS):
                    ins = dve.max_index(topi[:, b, :], top[:, b, :], src[:, b, :])
                chained(ins)
                chained(dve.tensor_copy(topf[:], topi[:]))
                for k in range(count):
                    into = out if k == 0 else eq[:, :, 0:width]
                    chained(at_choice(into, k, width))
                    if k:
                        chained(dve.tensor_tensor(out, out, eq[:, :, 0:width], ALU.add))

            def at_choice(out, k, width=NE):
                return dve.tensor_tensor(out, iota[:, 0:width].unsqueeze(1).broadcast_to([P, SEQS, width]),
                                         wide(topf[:, :, k], width), ALU.is_equal)

            chained(dve.tensor_reduce(grp[:, :, 0:NGR], pr[:].rearrange("p b (g e) -> p b g e", e=EG), AX.X, ALU.max))
            chosen(sel[:, :, 0:NGR], grp[:], NGR, TOPG)
            mask = sel[:, :, 0:NGR]
            chained(dve.tensor_tensor(comb[:].rearrange("p b (g e) -> p b g e", e=EG),
                                      pr[:].rearrange("p b (g e) -> p b g e", e=EG),
                                      mask.unsqueeze(3).broadcast_to([P, SEQS, NGR, EG]), ALU.mult))
            chained(dve.tensor_scalar(grp[:, :, 0:NGR], mask, 1.0, None, ALU.subtract))
            chained(dve.tensor_tensor(comb[:].rearrange("p b (g e) -> p b g e", e=EG),
                                      comb[:].rearrange("p b (g e) -> p b g e", e=EG),
                                      grp[:, :, 0:NGR].unsqueeze(3).broadcast_to([P, SEQS, NGR, EG]), ALU.add))
            chosen(sel[:], comb[:], NE, TOPK)
            dve.sem_inc(chosen_ready.sem, 1)

            added = {}
            total = [0]

            def add_to_y(b, ins):
                total[0] += 1
                added[b] = (y_added, total[0])
                ins.then_inc(y_added.sem, 1)

            def shared_hidden(tiles, g, c):
                n, m = NS * g + c, shared[c][1]
                bank = tiles.wait(dve, 0, ("su", g, c))
                dve.wait_ge(s_gated.sem, n + 1)
                dve.tensor_tensor(hs[0:m, c, :], bank[0:m, :], gated[0:m, n % 2, :], ALU.mult).then_inc(s_h.sem, 1)

            def shared_add(tiles, g, b):
                bank = tiles.wait(dve, 0, ("sy", g, b))
                s = GB * g + b
                if s in added:
                    dve.wait_ge(added[s][0].sem, added[s][1])
                dve.tensor_tensor(y[:, s, :], bank[:, :], y[:, s, :], ALU.add).then_inc(s_added.sem, 1)
                added[s] = (s_added, s + 1)

            for c in range(RANK_AT):
                shared_hidden(first, EARLY[0], c)

            bank = first.wait(dve, 0, ("rank",))
            rank = bank[:, 0:SEQS * NE].rearrange("p (b e) -> p b e", b=SEQS)
            pairs = bank[:, SEQS * NE:2 * SEQS * NE].rearrange("p (b e) -> p b e", b=SEQS)
            chained(dve.memset(before[:, 0, :], 0.0))
            for b in range(1, SEQS):
                chained(dve.tensor_tensor(before[:, b, :], before[:, b - 1, :], pairs[:, b - 1, :], ALU.add))
            chained(dve.tensor_tensor(count[:, :], before[:, SEQS - 1, :], pairs[:, SEQS - 1, :], ALU.add))
            chained(dve.tensor_tensor(more[:], count[:, :].unsqueeze(2).broadcast_to([P, NE, SEQS - 1]),
                                      steps_of[:, :].unsqueeze(1).broadcast_to([P, NE, SEQS - 1]), ALU.is_gt))
            chained(dve.tensor_reduce(count[:, :], more[:], AX.X, ALU.add))
            chained(dve.tensor_scalar(count[:, :], count[:, :], 1.0, None, ALU.add))
            chained(dve.tensor_tensor_scan(base[:, :], unit[:, :], count[:, :], 0.0, ALU.mult, ALU.add))
            chained(dve.tensor_tensor(base[:, :], base[:, :], count[:, :], ALU.subtract))
            chained(dve.tensor_tensor(past[:], base[0:1, 1:NE].unsqueeze(1).broadcast_to([1, BLOCKS + 1, NE - 1]),
                                      block_no[:, :].unsqueeze(2).broadcast_to([1, BLOCKS + 1, NE - 1]), ALU.is_le))
            chained(dve.tensor_reduce(owner[:, :], past[:], AX.X, ALU.add))
            chained(dve.tensor_copy(owner_no[:, :], owner[:, :]))
            chained(dve.tensor_scalar(held[:, :], owner[:, :], float(NE - 2), None, ALU.min))
            chained(dve.memset(change[:, 0:1], 0.0))
            chained(dve.tensor_tensor(change[:, 1:], held[:, 1:], held[:, 0:BLOCKS], ALU.subtract))
            chained(dve.tensor_scalar(held[:, :], held[:, :], 1.0, None, ALU.add))
            chained(dve.tensor_tensor(change[:, :], change[:, :], held[:, :], ALU.mult))
            dve.tensor_copy(fetch_no[:, :], change[:, :]).then_inc(owners.sem, 1)
            chained(dve.tensor_scalar(base[:, :], base[:, :], float(P), -1.0, ALU.mult, ALU.add))
            chained(dve.tensor_tensor(before[:], before[:], rank, ALU.add))
            chained(dve.tensor_tensor(before[:], before[:], base[:, :].unsqueeze(1).broadcast_to([P, SEQS, NE]), ALU.add))
            dve.sem_inc(placed.sem, 1)
            for k in range(TOPK):
                chained(at_choice(eq[:], k))
                chained(dve.tensor_tensor(eq[:], eq[:], before[:], ALU.mult))
                chained(dve.tensor_reduce(slot[:, k, :], eq[:], AX.X, ALU.add))
            chained(dve.tensor_copy(slot_no[:], slot[:]))
            chained(dve.tensor_scalar(quot[:], slot_no[:], P.bit_length() - 1, None, ALU.logical_shift_right))
            chained(dve.tensor_scalar(rest[:], slot_no[:], P - 1, None, ALU.bitwise_and))
            chained(dve.tensor_copy(quotf[:], quot[:]))
            chained(dve.tensor_copy(restf[:], rest[:]))
            chained(dve.scalar_tensor_tensor(quotf[:], restf[:], float(LIST), quotf[:], ALU.mult, ALU.add))
            chained(dve.tensor_copy(place[:], quotf[:]))
            chained(dve.tensor_scalar(slot[:], slot[:], float(P), None, ALU.add))
            dve.tensor_copy(row_no[:], slot[:]).then_inc(placed.sem, 1)

            for c in range(RANK_AT, NS):
                shared_hidden(first, EARLY[0], c)
            for b in range(GB):
                shared_add(first, EARLY[0], b)
            for g in EARLY[1:]:
                for c in range(NS):
                    shared_hidden(first, g, c)
                for b in range(GB):
                    shared_add(first, g, b)
            dve.sem_inc(xcol_ready.sem, AHEAD)
            dve.sem_inc(hrow_ready.sem, AHEAD)
            dve.sem_inc(hid_ready.sem, AHEAD)

            def columns(v):
                dve.tensor_copy(xcol[:, v].rearrange("p c n -> p (c n)"), turned_bank[:, :]).then_inc(xcol_ready.sem, 1)

            def hidden_columns(v):
                dve.tensor_copy(hid[:, v], hidden_bank[:, 0:FP]).then_inc(hid_ready.sem, 1)

            dve.wait_ge(filled.sem, turned(0))
            columns(0)
            with dve.Fori(0, BLOCKS // 2) as i:
                for v in range(2):
                    j = 2 * i + v
                    dve.wait_ge(filled.sem, turned(j + 1))
                    columns(1 - v)
                    dve.wait_ge(filled.sem, hidden_turned(j - 1))
                    hidden_columns(1 - v)
                    dve.wait_ge(filled.sem, up_done(j))
                    dve.wait_ge(gate_ready.sem, AHEAD + j + 1)
                    dve.tensor_tensor(hrow[:, v, 0:FI], up_banks[v][:, 0:FI], gate[:, v],
                                      ALU.mult).then_inc(hrow_ready.sem, 1)
            dve.wait_ge(filled.sem, 5 * BLOCKS + 6)
            hidden_columns(1)

            combine = [(n, b, k) for n, (b, k) in enumerate((b, k) for b in COMBINED for k in range(TOPK))]

            def combine_one():
                n, b, k = combine.pop(0)
                dve.wait_ge(returned[n % SLOTS].sem, 16 * (n // SLOTS + 1))
                if b in added:
                    dve.wait_ge(added[b][0].sem, added[b][1])
                add_to_y(b, dve.scalar_tensor_tensor(y[:, b, :], back[:, n % SLOTS], top[:, b, k:k + 1], y[:, b, :],
                                                     ALU.mult, ALU.add))
                if b in READY[0] and k == TOPK - 1:
                    sums(b)

            def sums(b):
                dve.wait_ge(added[b][0].sem, added[b][1])
                vstep.did(dve.bn_stats(stats[:, b, :], y[:, b, :]))

            def moments_of(i):
                vstep.wait(dve, 0)
                for b in READY[i]:
                    ins = dve.bn_aggr(mom[:, b, :], stats[:, b, :])
                ins.then_inc(moments.sem, 1)

            def normalise(i, seqs):
                dve.wait_ge(rstd_ready.sem, 2 * (i + 1))
                for b in seqs:
                    dve.tensor_scalar(y[:, b, :], y[:, b, :], mom[:, b, 0:1], rstd[:, b:b + 1],
                                      ALU.subtract, ALU.mult).then_inc(normed.sem, 1)

            for g in LATE:
                for c in range(NS):
                    shared_hidden(last, g, c)
                    for _ in range(min(5, len(combine))):
                        combine_one()
                    if g == LATE[-1] and c == NS - 3:
                        moments_of(0)
                for b in range(GB):
                    shared_add(last, g, b)
                    if combine:
                        combine_one()
                    if g == LATE[-1]:
                        normalise(0, READY[0][b * len(READY[0]) // GB:(b + 1) * len(READY[0]) // GB])
            while combine:
                combine_one()
            for b in READY[1]:
                sums(b)
            moments_of(1)
            normalise(1, READY[1])


def build_program(nc, t):
    t = dict(t)
    scratch = (("x3", [GROUPS, P, GB, D], F32), ("pre", [GROUPS, E0, D], F32), ("fsum", [E0, D], F32),
               ("x5", [GROUPS, P, GB, D], F32), ("kpark", [2, P, 3, D], BF16), ("qpark", [2, P, 3, D], BF16),
               ("ovpark", [2, P, 2, D], F32),
               ("slots", [P, SEQS * 4 + NE + 2], U32), ("results", [SEQS * 4 + NE + 1, P, D], F32))
    for name, shape, dt in scratch:
        t[name] = nc.dram_tensor("scratch_" + name, shape, dt, kind="Internal").ap()
    build_layer0(nc, t)
    build_row_fix(nc, t)
    build_layer1(nc, t)
    build_experts(nc, t)


def chunks_of(n):
    return [(a, min(P, n - a)) for a in range(0, n, P)]


def by_group(a):
    return np.ascontiguousarray(a.reshape(GROUPS, GB, P, D).transpose(0, 2, 1, 3))


def by_feature(a):
    return np.ascontiguousarray(a.reshape(GROUPS, GT, KC, P).transpose(0, 3, 2, 1))


def rows_of(a):
    return np.ascontiguousarray(a.reshape(-1, P, a.shape[-1]).transpose(1, 0, 2))


def constants():
    t = {}
    f = np.float32
    inv = (1.0 / f(10000.0) ** (np.arange(0, P, 2, dtype=f) / f(P))).astype(f)
    angle = np.outer(inv, np.arange(P, dtype=f)).astype(f)
    t["cos0"] = np.concatenate([np.cos(angle), np.cos(angle)]).astype(f)
    t["sin0"] = np.concatenate([np.sin(angle), -np.sin(angle)]).astype(f)
    k, q = np.arange(P)[:, None], np.arange(P)[None, :]
    t["causal"] = (q >= k).astype(f)
    t["barred"] = np.where(q >= k, 0.0, BIG).astype(f)
    t["ident"] = np.eye(P, dtype=f)
    sel = np.zeros((P, HX, P), f)
    sel[64 + np.arange(HX), np.arange(HX)] = 1
    t["sel"] = sel
    t["iota"] = np.broadcast_to(np.arange(E0, dtype=f), (P, E0)).copy()
    t["iota1"] = np.broadcast_to(np.arange(NE, dtype=f), (P, NE)).copy()
    t["steps_of"] = np.broadcast_to(P * np.arange(1, SEQS, dtype=f), (P, SEQS - 1)).copy()
    t["block_no"] = np.arange(-1, SEQS * 4 + NE, dtype=f)[None, :].copy()
    seq = np.arange(SEQS)[None, :]
    t["token_no"] = (seq // GB * GT + np.arange(P)[:, None] * GB + seq % GB).astype(np.uint32)
    freq = np.concatenate([f(1 / 1024.0) ** np.linspace(0, 1, HD // 4, dtype=f), np.zeros(HD // 4, f)]).astype(f)
    theta = (np.arange(P, dtype=f)[:, None] * freq[None, :]).astype(f)
    t["cos1"], t["sin1"] = np.cos(theta).astype(f), np.sin(theta).astype(f)
    first = 2.0 ** (-2.0 ** (-(np.log2(HX) - 3)))
    slopes = np.array([first * first ** i for i in range(HX)])
    dist = (q - k)[:, None, :]
    t["decay1"] = np.where(dist >= 0, np.exp(-slopes[None, :, None] * np.maximum(dist, 0)), 0.0).astype(f)
    return t


def tables(i):
    t = constants()
    a = {k: np.asarray(v) for k, v in i.items()}
    t["x"], t["xT"] = by_group(a["x"]), by_feature(a["x"])
    t["c"], t["cT"] = by_group(a["ctx_2048"]), by_feature(a["ctx_2048"])
    t["wk0"], t["wv0"] = (rows_of(a["L0_attn_" + n].T) for n in ("Wk", "Wv"))
    t["wq0"] = np.stack([rows_of(w) for w in np.split(a["L0_attn_Wq"].T, KV0, axis=1)])
    t["wo0"] = np.stack([rows_of(w) for w in np.split(a["L0_attn_Wo"].T, KV0, axis=0)])
    t["wi0"], t["wf0"] = rows_of(a["L0_xattn_Wi"]), rows_of(a["L0_xattn_Wf"])
    bias = np.zeros((P, 2), np.float32)
    bias[0:HX, 0], bias[32:32 + HX, 0] = a["L0_xattn_bi"], a["L0_xattn_bf"]
    t["bias0"] = bias
    t["lnw0"] = np.broadcast_to(a["L0_xattn_ln_scale"], (P, D)).copy()
    t["w10"], t["w30"], t["w20"] = (rows_of(a["L0_ffn_" + n].T) for n in ("w1", "w3", "w2"))
    t["wr0"] = rows_of(a["L0_ffn_wr"].T)
    for n in ("q", "k", "v", "o"):
        t[f"w{n}1"] = rows_of(a[f"L1_attn_W{n}"])
    t["rms1"] = np.ascontiguousarray(a["L1_attn_rms_w"].reshape(KC, P).T)
    t["gamma1"] = np.broadcast_to(a["L1_xattn_gamma"], (P, 1)).copy()
    t["wg1"] = rows_of(a["L1_ffn_Wg"].T)
    both = np.stack([a["L1_ffn_W1"], a["L1_ffn_W3"]], axis=1)
    t["w131"] = np.ascontiguousarray(
        both.transpose(0, 3, 1, 2).reshape(NE, KC, P, 2, FI).transpose(0, 2, 3, 1, 4))
    t["ws1"], t["ws3"] = (rows_of(a["L1_ffn_" + n].T) for n in ("Ws1", "Ws3"))

    def padded(w):
        return rows_of(np.concatenate([w.T, np.zeros((-w.shape[1] % P, D), w.dtype)]))

    t["w21"] = np.stack([padded(w) for w in a["L1_ffn_W2"]])
    t["ws2"] = padded(a["L1_ffn_Ws2"])
    return t


def kernel(**inputs):
    import concourse.bacc as bacc
    from concourse.bass_utils import run_bass_kernel_spmd

    nc = bacc.Bacc("TRN2", target_bir_lowering=False, num_devices=1)
    arrays, t = {}, {}
    for name, a in tables(inputs).items():
        arrays[f"in_{name}"] = a
        t[name] = nc.dram_tensor(f"in_{name}", a.shape, mybir.dt.from_np(a.dtype), kind="ExternalInput").ap()
    t["out"] = nc.dram_tensor("out_x", [SEQS, P, D], F32, kind="ExternalOutput").ap()
    build_program(nc, t)
    result = run_bass_kernel_spmd(nc, [arrays], core_ids=[0])
    return result.results[0]["out_x"]
```
